# Optimizing a Trainium2 kernel written in Bass

```python
import numpy as np
import jax
import jax.numpy as jnp

def _softmax(x, axis=-1):
    return jax.nn.softmax(x, axis=axis)

def _gelu(x):
    return jax.nn.gelu(x, approximate=True)

def _silu(x):
    return jax.nn.silu(x)

def _sigmoid(x):
    return jax.nn.sigmoid(x)

def _layernorm(x, axis=-1, eps=1e-05):
    m = jnp.mean(x, axis=axis, keepdims=True)
    v = jnp.var(x, axis=axis, keepdims=True)
    return (x - m) / jnp.sqrt(v + eps)

def _scatter_add(tgt, idx, src, axis=0):
    return tgt.at[idx].add(src)

def _segment_sum(src, seg, n):
    return jax.ops.segment_sum(src, seg, n)
kernel_name = 'mk_gnn_ffn_d4_gnn_r8_945cbd'

def setup_inputs(seed: int=0):
    np.random.seed(seed)
    _w = jnp.asarray

    def _rec_inputs():
        import jax
        import jax.numpy as jnp
        _gk = jax.random.key(seed)
        x = -0.001003 + 1 * jax.random.normal(jax.random.fold_in(_gk, 1), (256, 768), jnp.float32)
        src = jax.random.randint(jax.random.fold_in(_gk, 2), (4096,), 0, 256, jnp.int32)
        dst = jax.random.randint(jax.random.fold_in(_gk, 3), (4096,), 0, 256, jnp.int32)
        _o = jnp.argsort(dst, stable=True)
        src = src[_o]
        dst = dst[_o]
        edge_type_3 = jax.random.randint(jax.random.fold_in(_gk, 12), (4096,), 0, 3, jnp.int32)
        return (x, src, dst, edge_type_3)
    x, src, dst, edge_type_3 = _rec_inputs()

    def _L0_gnn_setup():
        import jax, jax.numpy as jnp
        import numpy as np
        NUM_RELATIONS = 3

        def _rgcn(x, W_rel, W_root, bias, src, dst, etype):
            n = x.shape[0]
            xr = jnp.einsum('ni,rio->rno', x, W_rel)
            msg = xr[etype, src]
            out = x @ W_root + bias
            for r in range(NUM_RELATIONS):
                m = etype == r
                s = jax.ops.segment_sum(jnp.where(m[:, None], msg, 0.0), dst, num_segments=n)
                c = jax.ops.segment_sum(m.astype(x.dtype), dst, num_segments=n)
                out = out + s / jnp.maximum(c, 1.0)[:, None]
            return out

        def _gate(h, q, Wg, bg, Wq, bq):
            B, L, F = q.shape
            N = h.shape[0] // B
            h3 = h.reshape(B, N, F)
            hg = jnp.einsum('bnf,gf->bng', h3, Wg[:, :F])
            qg = jnp.einsum('blf,gf->blg', q, Wg[:, F:]) + bg
            attn = jax.nn.sigmoid(hg[:, :, None, :] + qg[:, None, :, :])
            qi = jnp.einsum('bnlf,blf->bnf', attn, q)
            alpha = jax.nn.sigmoid(jnp.einsum('bnf,gf->bng', h3, Wq[:, :F]) + jnp.einsum('bnf,gf->bng', qi, Wq[:, F:]) + bq)
            hn = alpha * jnp.tanh(qi) + (1.0 - alpha) * h3
            return hn.reshape(B * N, F)
        key = jax.random.key(seed)
        ks = jax.random.split(key, 16)
        F = 768
        BN, E, B, L = (256, 8192, 8, 64)
        s = 0.02
        return {'x': jax.random.normal(ks[0], (BN, F), jnp.float32), 'edge_index': jax.random.randint(ks[1], (2, E), 0, BN), 'edge_type': jax.random.randint(ks[2], (E,), 0, NUM_RELATIONS), 'query_embs': jax.random.normal(ks[3], (B, L, F), jnp.float32), 'W_rel1': jax.random.normal(ks[4], (NUM_RELATIONS, F, F), jnp.float32) * s, 'W_root1': jax.random.normal(ks[5], (F, F), jnp.float32) * s, 'b1': jnp.zeros((F,), jnp.float32), 'W_rel2': jax.random.normal(ks[6], (NUM_RELATIONS, F, F), jnp.float32) * s, 'W_root2': jax.random.normal(ks[7], (F, F), jnp.float32) * s, 'b2': jnp.zeros((F,), jnp.float32), 'Wg': jax.random.normal(ks[8], (F, 2 * F), jnp.float32) * s, 'bg': jnp.zeros((F,), jnp.float32), 'Wq': jax.random.normal(ks[9], (F, 2 * F), jnp.float32) * s, 'bq': jnp.zeros((F,), jnp.float32)}
    _L0_gnn_all = _L0_gnn_setup()
    _L0_gnn_in = {k: v for k, v in _L0_gnn_all.items() if k in ('query_embs', 'W_rel1', 'W_root1', 'b1', 'W_rel2', 'W_root2', 'b2', 'Wg', 'bg', 'Wq', 'bq')}
    del _L0_gnn_all

    def _L0_ffn_setup():
        import jax, jax.numpy as jnp
        import numpy as np
        ALPHA = 1.702
        LIMIT = 7.0
        TOP_K = 2
        B, S, H, E, I = (2, 1024, 768, 8, 768)
        key = jax.random.key(seed)
        ks = jax.random.split(key, 7)
        scale = 0.02
        return {'hidden_states': jax.random.normal(ks[0], (B, S, H), dtype=jnp.float32), 'Wr': jax.random.normal(ks[1], (H, E), dtype=jnp.float32) * scale, 'br': jax.random.normal(ks[2], (E,), dtype=jnp.float32) * scale, 'Wgu': jax.random.normal(ks[3], (E, H, 2 * I), dtype=jnp.float32) * scale, 'bgu': jax.random.normal(ks[4], (E, 2 * I), dtype=jnp.float32) * scale, 'Wd': jax.random.normal(ks[5], (E, I, H), dtype=jnp.float32) * scale, 'bd': jax.random.normal(ks[6], (E, H), dtype=jnp.float32) * scale}
    _L0_ffn_all = _L0_ffn_setup()
    _L0_ffn_in = {k: v for k, v in _L0_ffn_all.items() if k in ('Wr', 'br', 'Wgu', 'bgu', 'Wd', 'bd')}
    del _L0_ffn_all

    def _L1_gnn_setup():
        import jax, jax.numpy as jnp
        import numpy as np
        N_NODES = 1250
        NEG_SLOPE = 0.2
        EPS = 1e-16

        def gat_layer(x, W, att_src, att_dst, bias, src, dst, heads, out_ch, concat):
            n = x.shape[0]
            h = (x @ W.T).reshape(n, heads, out_ch)
            a_src = jnp.einsum('nhc,hc->nh', h, att_src)
            a_dst = jnp.einsum('nhc,hc->nh', h, att_dst)
            e = a_src[src] + a_dst[dst]
            e = jax.nn.leaky_relu(e, NEG_SLOPE)
            m = jax.ops.segment_max(e, dst, num_segments=n)
            ex = jnp.exp(e - m[dst])
            denom = jax.ops.segment_sum(ex, dst, num_segments=n)
            alpha = ex / (denom[dst] + EPS)
            msg = alpha[:, :, None] * h[src]
            out = jax.ops.segment_sum(msg, dst, num_segments=n)
            if concat:
                out = out.reshape(n, heads * out_ch)
            else:
                out = out.mean(axis=1)
            return out + bias
        key = jax.random.key(seed)
        ks = jax.random.split(key, 12)
        x = jax.random.normal(ks[0], (N_NODES, 768), dtype=jnp.float32)
        edge_index = jax.random.randint(ks[1], (2, 20000), 0, N_NODES, dtype=jnp.int64)
        s1 = 1.0 / np.sqrt(768.0)
        W1 = jax.random.normal(ks[2], (8 * 128, 768), dtype=jnp.float32) * s1
        att_src1 = jax.random.normal(ks[3], (8, 128), dtype=jnp.float32) * (1.0 / np.sqrt(128.0))
        att_dst1 = jax.random.normal(ks[4], (8, 128), dtype=jnp.float32) * (1.0 / np.sqrt(128.0))
        b1 = jnp.zeros((8 * 128,), dtype=jnp.float32)
        s2 = 1.0 / np.sqrt(1024.0)
        W2 = jax.random.normal(ks[5], (1 * 768, 1024), dtype=jnp.float32) * s2
        att_src2 = jax.random.normal(ks[6], (1, 768), dtype=jnp.float32) * (1.0 / np.sqrt(768.0))
        att_dst2 = jax.random.normal(ks[7], (1, 768), dtype=jnp.float32) * (1.0 / np.sqrt(768.0))
        b2 = jnp.zeros((768,), dtype=jnp.float32)
        return {'x': x, 'edge_index': edge_index, 'W1': W1, 'att_src1': att_src1, 'att_dst1': att_dst1, 'b1': b1, 'W2': W2, 'att_src2': att_src2, 'att_dst2': att_dst2, 'b2': b2}
    _L1_gnn_all = _L1_gnn_setup()
    _L1_gnn_in = {k: v for k, v in _L1_gnn_all.items() if k in ('W1', 'att_src1', 'att_dst1', 'b1', 'W2', 'att_src2', 'att_dst2', 'b2')}
    del _L1_gnn_all

    def _L1_ffn_setup():
        import jax, jax.numpy as jnp
        import numpy as np
        B, S, H = (4, 1024, 768)
        NH, HD = (12, 64)
        E, K, F = (8, 2, 384)
        SF = 768
        EPS = 1e-06

        def rmsnorm(x, w):
            xf = x.astype(jnp.float32)
            var = jnp.mean(xf * xf, axis=-1, keepdims=True)
            return w * (xf * jax.lax.rsqrt(var + EPS)).astype(x.dtype)
        key = jax.random.key(seed)
        ks = jax.random.split(key, 16)
        sc = 0.02
        return {'hidden_states': jax.random.normal(ks[0], (B, S, H), jnp.float32), 'norm1_w': jnp.ones((H,), jnp.float32), 'Wq': jax.random.normal(ks[1], (H, H), jnp.float32) * sc, 'Wk': jax.random.normal(ks[2], (H, H), jnp.float32) * sc, 'Wv': jax.random.normal(ks[3], (H, H), jnp.float32) * sc, 'Wo': jax.random.normal(ks[4], (H, H), jnp.float32) * sc, 'norm2_w': jnp.ones((H,), jnp.float32), 'gate_w': jax.random.normal(ks[5], (E, H), jnp.float32) * sc, 'Weg': jax.random.normal(ks[6], (E, F, H), jnp.float32) * sc, 'Weu': jax.random.normal(ks[7], (E, F, H), jnp.float32) * sc, 'Wed': jax.random.normal(ks[8], (E, H, F), jnp.float32) * sc, 'Wsg': jax.random.normal(ks[9], (SF, H), jnp.float32) * sc, 'Wsu': jax.random.normal(ks[10], (SF, H), jnp.float32) * sc, 'Wsd': jax.random.normal(ks[11], (H, SF), jnp.float32) * sc}
    _L1_ffn_all = _L1_ffn_setup()
    _L1_ffn_in = {k: v for k, v in _L1_ffn_all.items() if k in ('norm1_w', 'Wq', 'Wk', 'Wv', 'Wo', 'norm2_w', 'gate_w', 'Weg', 'Weu', 'Wed', 'Wsg', 'Wsu', 'Wsd')}
    del _L1_ffn_all

    def _L2_gnn_setup():
        import jax, jax.numpy as jnp
        import numpy as np
        NEG_SLOPE = 0.2
        EPS = 1e-16
        N_NODES = 4096
        N_EDGES = 20000
        DIM = 768
        HEADS1 = 4
        OUT1 = DIM // HEADS1
        HEADS2 = 1
        OUT2 = DIM
        N_REL = 3

        def rgat_conv(x, W, q, k, b, src, dst, etype, heads, out_ch, n_nodes):
            xr = jnp.einsum('nd,rdf->rnf', x, W)
            oi = xr[etype, dst]
            oj = xr[etype, src]
            qi = oi @ q
            kj = oj @ k
            alpha = jax.nn.leaky_relu(qi + kj, NEG_SLOPE)
            m = jax.ops.segment_max(alpha, dst, num_segments=n_nodes)
            e = jnp.exp(alpha - m[dst])
            z = jax.ops.segment_sum(e, dst, num_segments=n_nodes)
            a = e / (z[dst] + EPS)
            msg = (a[:, :, None] * oj.reshape(-1, heads, out_ch)).reshape(-1, heads * out_ch)
            out = jax.ops.segment_sum(msg, dst, num_segments=n_nodes)
            return out + b
        key = jax.random.key(seed)
        ks = jax.random.split(key, 12)
        s = 0.02
        return {'x': jax.random.normal(ks[0], (N_NODES, DIM), dtype=jnp.float32), 'edge_index': jax.random.randint(ks[1], (2, N_EDGES), 0, N_NODES, dtype=jnp.int64), 'edge_type': jax.random.randint(ks[2], (N_EDGES,), 0, N_REL, dtype=jnp.int64), 'W1': jax.random.normal(ks[3], (N_REL, DIM, HEADS1 * OUT1), dtype=jnp.float32) * s, 'q1': jax.random.normal(ks[4], (HEADS1 * OUT1, HEADS1), dtype=jnp.float32) * s, 'k1': jax.random.normal(ks[5], (HEADS1 * OUT1, HEADS1), dtype=jnp.float32) * s, 'b1': jnp.zeros((HEADS1 * OUT1,), dtype=jnp.float32), 'W2': jax.random.normal(ks[6], (N_REL, DIM, HEADS2 * OUT2), dtype=jnp.float32) * s, 'q2': jax.random.normal(ks[7], (HEADS2 * OUT2, HEADS2), dtype=jnp.float32) * s, 'k2': jax.random.normal(ks[8], (HEADS2 * OUT2, HEADS2), dtype=jnp.float32) * s, 'b2': jnp.zeros((HEADS2 * OUT2,), dtype=jnp.float32)}
    _L2_gnn_all = _L2_gnn_setup()
    _L2_gnn_in = {k: v for k, v in _L2_gnn_all.items() if k in ('W1', 'q1', 'k1', 'b1', 'W2', 'q2', 'k2', 'b2')}
    del _L2_gnn_all

    def _L2_ffn_setup():
        import jax, jax.numpy as jnp
        import numpy as np
        H, I, E, S, K = (768, 384, 16, 2, 2)
        SCALE = 1.0
        key = jax.random.key(seed)
        ks = jax.random.split(key, 8)
        sd = 0.02
        return {'hidden_states': jax.random.normal(ks[0], (2, 1024, H), jnp.float32), 'gate_w': jax.random.normal(ks[1], (E, H), jnp.float32) * sd, 'shared_wg': jax.random.normal(ks[2], (S, H, I), jnp.float32) * sd, 'shared_wu': jax.random.normal(ks[3], (S, H, I), jnp.float32) * sd, 'shared_wd': jax.random.normal(ks[4], (S, I, H), jnp.float32) * sd, 'wg': jax.random.normal(ks[5], (E, H, I), jnp.float32) * sd, 'wu': jax.random.normal(ks[6], (E, H, I), jnp.float32) * sd, 'wd': jax.random.normal(ks[7], (E, I, H), jnp.float32) * sd}
    _L2_ffn_all = _L2_ffn_setup()
    _L2_ffn_in = {k: v for k, v in _L2_ffn_all.items() if k in ('gate_w', 'shared_wg', 'shared_wu', 'shared_wd', 'wg', 'wu', 'wd')}
    del _L2_ffn_all

    def _L3_gnn_setup():
        import jax, jax.numpy as jnp
        import numpy as np
        N_NODES = 1250
        key = jax.random.key(seed)
        k1, k2, k3 = jax.random.split(key, 3)
        x = jax.random.normal(k1, (N_NODES, 768), dtype=jnp.float32)
        edge_index = jax.random.randint(k2, (2, 12500), 0, N_NODES, dtype=jnp.int32)
        W = jax.random.normal(k3, (768, 768), dtype=jnp.float32) * (1.0 / np.sqrt(768))
        b = jnp.zeros((768,), dtype=jnp.float32)
        return {'x': x, 'edge_index': edge_index, 'W': W, 'b': b}
    _L3_gnn_all = _L3_gnn_setup()
    _L3_gnn_in = {k: v for k, v in _L3_gnn_all.items() if k in ('W', 'b')}
    del _L3_gnn_all

    def _L3_ffn_setup():
        import jax, jax.numpy as jnp
        import numpy as np
        B, M, D = (32, 196, 768)
        N, P, H = (64, 1, 384)
        EPS = 1e-12

        def _l2norm(v, axis):
            n = jnp.sqrt(jnp.sum(v * v, axis=axis, keepdims=True))
            return v / jnp.maximum(n, EPS)
        key = jax.random.key(seed)
        ks = jax.random.split(key, 7)
        x = jax.random.normal(ks[0], (B, M, D), dtype=jnp.float32)
        phi = jax.random.normal(ks[1], (D, N, P), dtype=jnp.float32) * (1.0 / D ** 0.5)
        scale = jnp.ones((1,), dtype=jnp.float32)
        w1 = jax.random.normal(ks[2], (N, D, H), dtype=jnp.float32) * (1.0 / D ** 0.5)
        b1 = jnp.zeros((N, H), dtype=jnp.float32)
        w2 = jax.random.normal(ks[3], (N, H, D), dtype=jnp.float32) * (1.0 / H ** 0.5)
        b2 = jnp.zeros((N, D), dtype=jnp.float32)
        return {'x': x, 'phi': phi, 'scale': scale, 'w1': w1, 'b1': b1, 'w2': w2, 'b2': b2}
    _L3_ffn_all = _L3_ffn_setup()
    _L3_ffn_in = {k: v for k, v in _L3_ffn_all.items() if k in ('phi', 'scale', 'w1', 'b1', 'w2', 'b2')}
    del _L3_ffn_all
    return {'x': x, 'src': src, 'dst': dst, 'edge_type_3': edge_type_3, 'L0_gnn_query_embs': _L0_gnn_in['query_embs'], 'L0_gnn_W_rel1': _L0_gnn_in['W_rel1'], 'L0_gnn_W_root1': _L0_gnn_in['W_root1'], 'L0_gnn_b1': _L0_gnn_in['b1'], 'L0_gnn_W_rel2': _L0_gnn_in['W_rel2'], 'L0_gnn_W_root2': _L0_gnn_in['W_root2'], 'L0_gnn_b2': _L0_gnn_in['b2'], 'L0_gnn_Wg': _L0_gnn_in['Wg'], 'L0_gnn_bg': _L0_gnn_in['bg'], 'L0_gnn_Wq': _L0_gnn_in['Wq'], 'L0_gnn_bq': _L0_gnn_in['bq'], 'L0_ffn_Wr': _L0_ffn_in['Wr'], 'L0_ffn_br': _L0_ffn_in['br'], 'L0_ffn_Wgu': _L0_ffn_in['Wgu'], 'L0_ffn_bgu': _L0_ffn_in['bgu'], 'L0_ffn_Wd': _L0_ffn_in['Wd'], 'L0_ffn_bd': _L0_ffn_in['bd'], 'L1_gnn_W1': _L1_gnn_in['W1'], 'L1_gnn_att_src1': _L1_gnn_in['att_src1'], 'L1_gnn_att_dst1': _L1_gnn_in['att_dst1'], 'L1_gnn_b1': _L1_gnn_in['b1'], 'L1_gnn_W2': _L1_gnn_in['W2'], 'L1_gnn_att_src2': _L1_gnn_in['att_src2'], 'L1_gnn_att_dst2': _L1_gnn_in['att_dst2'], 'L1_gnn_b2': _L1_gnn_in['b2'], 'L1_ffn_norm1_w': _L1_ffn_in['norm1_w'], 'L1_ffn_Wq': _L1_ffn_in['Wq'], 'L1_ffn_Wk': _L1_ffn_in['Wk'], 'L1_ffn_Wv': _L1_ffn_in['Wv'], 'L1_ffn_Wo': _L1_ffn_in['Wo'], 'L1_ffn_norm2_w': _L1_ffn_in['norm2_w'], 'L1_ffn_gate_w': _L1_ffn_in['gate_w'], 'L1_ffn_Weg': _L1_ffn_in['Weg'], 'L1_ffn_Weu': _L1_ffn_in['Weu'], 'L1_ffn_Wed': _L1_ffn_in['Wed'], 'L1_ffn_Wsg': _L1_ffn_in['Wsg'], 'L1_ffn_Wsu': _L1_ffn_in['Wsu'], 'L1_ffn_Wsd': _L1_ffn_in['Wsd'], 'L2_gnn_W1': _L2_gnn_in['W1'], 'L2_gnn_q1': _L2_gnn_in['q1'], 'L2_gnn_k1': _L2_gnn_in['k1'], 'L2_gnn_b1': _L2_gnn_in['b1'], 'L2_gnn_W2': _L2_gnn_in['W2'], 'L2_gnn_q2': _L2_gnn_in['q2'], 'L2_gnn_k2': _L2_gnn_in['k2'], 'L2_gnn_b2': _L2_gnn_in['b2'], 'L2_ffn_gate_w': _L2_ffn_in['gate_w'], 'L2_ffn_shared_wg': _L2_ffn_in['shared_wg'], 'L2_ffn_shared_wu': _L2_ffn_in['shared_wu'], 'L2_ffn_shared_wd': _L2_ffn_in['shared_wd'], 'L2_ffn_wg': _L2_ffn_in['wg'], 'L2_ffn_wu': _L2_ffn_in['wu'], 'L2_ffn_wd': _L2_ffn_in['wd'], 'L3_gnn_W': _L3_gnn_in['W'], 'L3_gnn_b': _L3_gnn_in['b'], 'L3_ffn_phi': _L3_ffn_in['phi'], 'L3_ffn_scale': _L3_ffn_in['scale'], 'L3_ffn_w1': _L3_ffn_in['w1'], 'L3_ffn_b1': _L3_ffn_in['b1'], 'L3_ffn_w2': _L3_ffn_in['w2'], 'L3_ffn_b2': _L3_ffn_in['b2']}

def reference(x, src, dst, edge_type_3, L0_gnn_query_embs, L0_gnn_W_rel1, L0_gnn_W_root1, L0_gnn_b1, L0_gnn_W_rel2, L0_gnn_W_root2, L0_gnn_b2, L0_gnn_Wg, L0_gnn_bg, L0_gnn_Wq, L0_gnn_bq, L0_ffn_Wr, L0_ffn_br, L0_ffn_Wgu, L0_ffn_bgu, L0_ffn_Wd, L0_ffn_bd, L1_gnn_W1, L1_gnn_att_src1, L1_gnn_att_dst1, L1_gnn_b1, L1_gnn_W2, L1_gnn_att_src2, L1_gnn_att_dst2, L1_gnn_b2, L1_ffn_norm1_w, L1_ffn_Wq, L1_ffn_Wk, L1_ffn_Wv, L1_ffn_Wo, L1_ffn_norm2_w, L1_ffn_gate_w, L1_ffn_Weg, L1_ffn_Weu, L1_ffn_Wed, L1_ffn_Wsg, L1_ffn_Wsu, L1_ffn_Wsd, L2_gnn_W1, L2_gnn_q1, L2_gnn_k1, L2_gnn_b1, L2_gnn_W2, L2_gnn_q2, L2_gnn_k2, L2_gnn_b2, L2_ffn_gate_w, L2_ffn_shared_wg, L2_ffn_shared_wu, L2_ffn_shared_wd, L2_ffn_wg, L2_ffn_wu, L2_ffn_wd, L3_gnn_W, L3_gnn_b, L3_ffn_phi, L3_ffn_scale, L3_ffn_w1, L3_ffn_b1, L3_ffn_w2, L3_ffn_b2):
    import jax
    import jax.numpy as jnp

    def _L0_gnn_ref(x, edge_index, edge_type, query_embs, W_rel1, W_root1, b1, W_rel2, W_root2, b2, Wg, bg, Wq, bq):
        import jax, jax.numpy as jnp
        import numpy as np
        NUM_RELATIONS = 3

        def _rgcn(x, W_rel, W_root, bias, src, dst, etype):
            n = x.shape[0]
            xr = jnp.einsum('ni,rio->rno', x, W_rel)
            msg = xr[etype, src]
            out = x @ W_root + bias
            for r in range(NUM_RELATIONS):
                m = etype == r
                s = jax.ops.segment_sum(jnp.where(m[:, None], msg, 0.0), dst, num_segments=n)
                c = jax.ops.segment_sum(m.astype(x.dtype), dst, num_segments=n)
                out = out + s / jnp.maximum(c, 1.0)[:, None]
            return out

        def _gate(h, q, Wg, bg, Wq, bq):
            B, L, F = q.shape
            N = h.shape[0] // B
            h3 = h.reshape(B, N, F)
            hg = jnp.einsum('bnf,gf->bng', h3, Wg[:, :F])
            qg = jnp.einsum('blf,gf->blg', q, Wg[:, F:]) + bg
            attn = jax.nn.sigmoid(hg[:, :, None, :] + qg[:, None, :, :])
            qi = jnp.einsum('bnlf,blf->bnf', attn, q)
            alpha = jax.nn.sigmoid(jnp.einsum('bnf,gf->bng', h3, Wq[:, :F]) + jnp.einsum('bnf,gf->bng', qi, Wq[:, F:]) + bq)
            hn = alpha * jnp.tanh(qi) + (1.0 - alpha) * h3
            return hn.reshape(B * N, F)
        src, dst = (edge_index[0], edge_index[1])
        h = jax.nn.relu(_rgcn(x, W_rel1, W_root1, b1, src, dst, edge_type))
        h = _gate(h, query_embs, Wg, bg, Wq, bq)
        h = jax.nn.relu(_rgcn(h, W_rel2, W_root2, b2, src, dst, edge_type))
        h = _gate(h, query_embs, Wg, bg, Wq, bq)
        return h

    def _L0_ffn_ref(hidden_states, Wr, br, Wgu, bgu, Wd, bd):
        import jax, jax.numpy as jnp
        import numpy as np
        ALPHA = 1.702
        LIMIT = 7.0
        TOP_K = 2
        B, S, H, E, I = (2, 1024, 768, 8, 768)
        logits = jnp.einsum('bsh,he->bse', hidden_states, Wr) + br
        topk_vals, topk_idx = jax.lax.top_k(logits, TOP_K)
        router_scores = jax.nn.softmax(topk_vals, axis=-1)
        gu = jnp.einsum('bsh,ehf->bsef', hidden_states, Wgu) + bgu
        gu = jnp.minimum(gu, LIMIT)
        gate = gu[..., :I]
        up = jnp.maximum(gu[..., I:], -LIMIT)
        glu = gate * jax.nn.sigmoid(gate * ALPHA)
        activated = (up + 1.0) * glu
        down = jnp.einsum('bsei,eih->bseh', activated, Wd) + bd
        sel = jnp.take_along_axis(down, topk_idx[..., None], axis=2)
        output = jnp.sum(sel * router_scores[..., None], axis=2)
        return output

    def _L1_gnn_ref(x, edge_index, W1, att_src1, att_dst1, b1, W2, att_src2, att_dst2, b2):
        import jax, jax.numpy as jnp
        import numpy as np
        N_NODES = 1250
        NEG_SLOPE = 0.2
        EPS = 1e-16

        def gat_layer(x, W, att_src, att_dst, bias, src, dst, heads, out_ch, concat):
            n = x.shape[0]
            h = (x @ W.T).reshape(n, heads, out_ch)
            a_src = jnp.einsum('nhc,hc->nh', h, att_src)
            a_dst = jnp.einsum('nhc,hc->nh', h, att_dst)
            e = a_src[src] + a_dst[dst]
            e = jax.nn.leaky_relu(e, NEG_SLOPE)
            m = jax.ops.segment_max(e, dst, num_segments=n)
            ex = jnp.exp(e - m[dst])
            denom = jax.ops.segment_sum(ex, dst, num_segments=n)
            alpha = ex / (denom[dst] + EPS)
            msg = alpha[:, :, None] * h[src]
            out = jax.ops.segment_sum(msg, dst, num_segments=n)
            if concat:
                out = out.reshape(n, heads * out_ch)
            else:
                out = out.mean(axis=1)
            return out + bias
        src, dst = (edge_index[0], edge_index[1])
        h = gat_layer(x, W1, att_src1, att_dst1, b1, src, dst, heads=8, out_ch=128, concat=True)
        h = jax.nn.relu(h)
        out = gat_layer(h, W2, att_src2, att_dst2, b2, src, dst, heads=1, out_ch=768, concat=True)
        return out

    def _L1_ffn_ref(hidden_states, norm1_w, Wq, Wk, Wv, Wo, norm2_w, gate_w, Weg, Weu, Wed, Wsg, Wsu, Wsd):
        import jax, jax.numpy as jnp
        import numpy as np
        B, S, H = (4, 1024, 768)
        NH, HD = (12, 64)
        E, K, F = (8, 2, 384)
        SF = 768
        EPS = 1e-06

        def rmsnorm(x, w):
            xf = x.astype(jnp.float32)
            var = jnp.mean(xf * xf, axis=-1, keepdims=True)
            return w * (xf * jax.lax.rsqrt(var + EPS)).astype(x.dtype)
        b, s, h = hidden_states.shape
        res = hidden_states
        x = rmsnorm(hidden_states, norm1_w)

        def heads(t):
            return t.reshape(b, s, NH, HD).transpose(0, 2, 1, 3)
        q, k, v = (heads(x @ Wq.T), heads(x @ Wk.T), heads(x @ Wv.T))
        scores = jnp.einsum('bhqd,bhkd->bhqk', q, k) / np.float32(np.sqrt(HD))
        attn = jax.nn.softmax(scores, axis=-1)
        ctx = jnp.einsum('bhqk,bhkd->bhqd', attn, v)
        ctx = ctx.transpose(0, 2, 1, 3).reshape(b, s, h)
        x = res + ctx @ Wo.T
        res2 = x
        xn = rmsnorm(x, norm2_w)
        t = xn.reshape(-1, h)
        gate_scores = jax.nn.softmax(t @ gate_w.T, axis=-1)
        topk_w, topk_idx = jax.lax.top_k(gate_scores, K)
        topk_w = topk_w / (topk_w.sum(-1, keepdims=True) + 1e-20)
        combine = (jax.nn.one_hot(topk_idx, E, dtype=t.dtype) * topk_w[..., None]).sum(1)
        g = jnp.einsum('td,efd->tef', t, Weg)
        u = jnp.einsum('td,efd->tef', t, Weu)
        act = jax.nn.silu(g) * u
        y_routed = jnp.einsum('tef,edf,te->td', act, Wed, combine)
        y_shared = jax.nn.silu(t @ Wsg.T) * (t @ Wsu.T) @ Wsd.T
        y = (y_routed + y_shared).reshape(b, s, h)
        return res2 + y

    def _L2_gnn_ref(x, edge_index, edge_type, W1, q1, k1, b1, W2, q2, k2, b2):
        import jax, jax.numpy as jnp
        import numpy as np
        NEG_SLOPE = 0.2
        EPS = 1e-16
        N_NODES = 4096
        N_EDGES = 20000
        DIM = 768
        HEADS1 = 4
        OUT1 = DIM // HEADS1
        HEADS2 = 1
        OUT2 = DIM
        N_REL = 3

        def rgat_conv(x, W, q, k, b, src, dst, etype, heads, out_ch, n_nodes):
            xr = jnp.einsum('nd,rdf->rnf', x, W)
            oi = xr[etype, dst]
            oj = xr[etype, src]
            qi = oi @ q
            kj = oj @ k
            alpha = jax.nn.leaky_relu(qi + kj, NEG_SLOPE)
            m = jax.ops.segment_max(alpha, dst, num_segments=n_nodes)
            e = jnp.exp(alpha - m[dst])
            z = jax.ops.segment_sum(e, dst, num_segments=n_nodes)
            a = e / (z[dst] + EPS)
            msg = (a[:, :, None] * oj.reshape(-1, heads, out_ch)).reshape(-1, heads * out_ch)
            out = jax.ops.segment_sum(msg, dst, num_segments=n_nodes)
            return out + b
        src, dst = (edge_index[0], edge_index[1])
        n = x.shape[0]
        h = rgat_conv(x, W1, q1, k1, b1, src, dst, edge_type, HEADS1, OUT1, n)
        h = jax.nn.elu(h)
        out = rgat_conv(h, W2, q2, k2, b2, src, dst, edge_type, HEADS2, OUT2, n)
        return out

    def _L2_ffn_ref(hidden_states, gate_w, shared_wg, shared_wu, shared_wd, wg, wu, wd):
        import jax, jax.numpy as jnp
        import numpy as np
        H, I, E, S, K = (768, 384, 16, 2, 2)
        SCALE = 1.0
        B, T, _ = hidden_states.shape
        x = hidden_states.reshape(-1, H)
        N = x.shape[0]
        g = jnp.einsum('nh,shi->sni', x, shared_wg)
        u = jnp.einsum('nh,shi->sni', x, shared_wu)
        shared_out = jnp.einsum('sni,sih->snh', jax.nn.silu(g) * u, shared_wd).mean(axis=0)
        router_logits = x @ gate_w.T
        routing_weights = jax.nn.softmax(router_logits, axis=-1)
        topk_w, topk_idx = jax.lax.top_k(routing_weights, K)
        topk_w = topk_w / (topk_w.sum(axis=-1, keepdims=True) + 1e-08)
        topk_w = topk_w * SCALE
        combine = jnp.zeros((N, E), x.dtype).at[jnp.arange(N)[:, None], topk_idx].add(topk_w)
        ge = jnp.einsum('nh,ehi->eni', x, wg)
        ue = jnp.einsum('nh,ehi->eni', x, wu)
        ye = jnp.einsum('eni,eih->enh', jax.nn.silu(ge) * ue, wd)
        routed_out = jnp.einsum('ne,enh->nh', combine, ye)
        return (shared_out + routed_out).reshape(B, T, H)

    def _L3_gnn_ref(x, edge_index, W, b):
        import jax, jax.numpy as jnp
        import numpy as np
        N_NODES = 1250
        n = x.shape[0]
        loops = jnp.arange(n, dtype=edge_index.dtype)
        row = jnp.concatenate([edge_index[0], loops])
        col = jnp.concatenate([edge_index[1], loops])
        ones = jnp.ones(row.shape[0], dtype=x.dtype)
        deg = jax.ops.segment_sum(ones, col, num_segments=n)
        dinv = jnp.where(deg > 0, jax.lax.rsqrt(deg), 0.0)
        norm = dinv[row] * dinv[col]
        h = x @ W
        msg = h[row] * norm[:, None]
        out = jax.ops.segment_sum(msg, col, num_segments=n) + b
        return out

    def _L3_ffn_ref(x, phi, scale, w1, b1, w2, b2):
        import jax, jax.numpy as jnp
        import numpy as np
        B, M, D = (32, 196, 768)
        N, P, H = (64, 1, 384)
        EPS = 1e-12

        def _l2norm(v, axis):
            n = jnp.sqrt(jnp.sum(v * v, axis=axis, keepdims=True))
            return v / jnp.maximum(n, EPS)
        xn = _l2norm(x, axis=2)
        phin = scale * _l2norm(phi, axis=0)
        logits = jnp.einsum('bmd,dnp->bmnp', xn, phin)
        d = jax.nn.softmax(logits, axis=1)
        b_, m_, n_, p_ = logits.shape
        c = jax.nn.softmax(logits.reshape(b_, m_, n_ * p_), axis=-1).reshape(b_, m_, n_, p_)
        xs = jnp.einsum('bmd,bmnp->bnpd', xn, d)
        h = jax.nn.gelu(jnp.einsum('bnpd,ndh->bnph', xs, w1) + b1[None, :, None, :], approximate=False)
        ys = jnp.einsum('bnph,nhd->bnpd', h, w2) + b2[None, :, None, :]
        y = jnp.einsum('bnpd,bmnp->bmd', ys, c)
        return y
    edge_index = jnp.stack([src, dst])
    x = x + _L0_gnn_ref(_layernorm(x, axis=-1), edge_index, edge_type_3, L0_gnn_query_embs, L0_gnn_W_rel1, L0_gnn_W_root1, L0_gnn_b1, L0_gnn_W_rel2, L0_gnn_W_root2, L0_gnn_b2, L0_gnn_Wg, L0_gnn_bg, L0_gnn_Wq, L0_gnn_bq)
    x = x + _L0_ffn_ref(_layernorm(x, axis=-1)[None], L0_ffn_Wr, L0_ffn_br, L0_ffn_Wgu, L0_ffn_bgu, L0_ffn_Wd, L0_ffn_bd)[0]
    x = x + _L1_gnn_ref(_layernorm(x, axis=-1), edge_index, L1_gnn_W1, L1_gnn_att_src1, L1_gnn_att_dst1, L1_gnn_b1, L1_gnn_W2, L1_gnn_att_src2, L1_gnn_att_dst2, L1_gnn_b2)
    x = x + _L1_ffn_ref(_layernorm(x, axis=-1)[None], L1_ffn_norm1_w, L1_ffn_Wq, L1_ffn_Wk, L1_ffn_Wv, L1_ffn_Wo, L1_ffn_norm2_w, L1_ffn_gate_w, L1_ffn_Weg, L1_ffn_Weu, L1_ffn_Wed, L1_ffn_Wsg, L1_ffn_Wsu, L1_ffn_Wsd)[0]
    x = x + _L2_gnn_ref(_layernorm(x, axis=-1), edge_index, edge_type_3, L2_gnn_W1, L2_gnn_q1, L2_gnn_k1, L2_gnn_b1, L2_gnn_W2, L2_gnn_q2, L2_gnn_k2, L2_gnn_b2)
    x = x + _L2_ffn_ref(_layernorm(x, axis=-1)[None], L2_ffn_gate_w, L2_ffn_shared_wg, L2_ffn_shared_wu, L2_ffn_shared_wd, L2_ffn_wg, L2_ffn_wu, L2_ffn_wd)[0]
    x = x + _L3_gnn_ref(_layernorm(x, axis=-1), edge_index, L3_gnn_W, L3_gnn_b)
    x = x + _L3_ffn_ref(_layernorm(x, axis=-1)[None], L3_ffn_phi, L3_ffn_scale, L3_ffn_w1, L3_ffn_b1, L3_ffn_w2, L3_ffn_b2)[0]
    return x

_drawn_inputs = setup_inputs


def setup_inputs(seed=0):
    import zlib

    import numpy as np

    out = dict(_drawn_inputs(seed))
    spreads = {'L0_gnn_b1': (0.0, 0.407),
     'L0_gnn_b2': (0.0, 0.1),
     'L0_gnn_bg': (0.0, 0.358),
     'L0_gnn_bq': (0.0, 0.377),
     'L1_gnn_b1': (0.0, 0.1),
     'L1_gnn_b2': (0.0, 0.1),
     'L1_ffn_norm1_w': (1.0, 0.6),
     'L1_ffn_norm2_w': (1.0, 0.6),
     'L2_gnn_b1': (0.0, 0.529),
     'L2_gnn_b2': (0.0, 0.1),
     'L3_gnn_b': (0.0, 0.1),
     'L3_ffn_b1': (0.0, 0.8),
     'L3_ffn_b2': (0.0, 0.8)}
    factors = {'L0_ffn_br': 4.852,
     'L0_ffn_bgu': 8.0,
     'L0_ffn_bd': 4.267,
     'L1_gnn_att_dst1': 4.864,
     'L1_gnn_att_src2': 6.729,
     'L1_gnn_att_dst2': 27.854,
     'L1_ffn_Wq': 7.442,
     'L1_ffn_Wk': 6.602,
     'L1_ffn_gate_w': 2.708,
     'L2_gnn_W1': 3.564,
     'L2_gnn_q1': 8.0,
     'L2_gnn_k1': 8.0,
     'L2_gnn_q2': 8.0,
     'L2_gnn_k2': 8.0,
     'L2_ffn_gate_w': 2.866,
     'L2_ffn_shared_wg': 2.758,
     'L2_ffn_shared_wu': 2.696,
     'L2_ffn_shared_wd': 2.696,
     'L2_ffn_wg': 2.672,
     'L3_ffn_phi': 64.0,
     'L3_ffn_w1': 8.0,
     'L3_ffn_w2': 8.0}
    for name, (base, spread) in spreads.items():
        noise = np.random.default_rng([zlib.crc32(name.encode()), seed]).standard_normal(out[name].shape)
        drawn = base * np.exp(spread * noise) if base else spread * noise
        out[name] = jnp.asarray(drawn.astype(out[name].dtype))
    for name, factor in factors.items():
        out[name] = (out[name] * factor).astype(out[name].dtype)
    return out
```

```python
from contextlib import ExitStack, contextmanager

import concourse.bass as bass
from concourse import mybir

F32 = mybir.dt.float32
BF16 = mybir.dt.bfloat16
I32 = mybir.dt.int32
U32 = mybir.dt.uint32
ALU = mybir.AluOpType
ACT = mybir.ActivationFunctionType
AX_X = mybir.AxisListType.X

P = 128
N = 256
T = N // P
D = 768
K = D // P
E = 4096
EDGE_TILES = E // P
REL = 3
B, L = 8, 64
GROUP = N // B
PIECE = 2304
RING = 12
HALF = 384
LOW = -1e30
HEADS, HEAD = 12, 64
SLOTS, SLOT_HIDDEN = 64, 384
CHUNKS = K * B
CHUNK_RING = 3

GATE_PIECES = 2 + 4
RGCN_PIECES = 8
L0_GNN_PIECES = 2 + 2 * (RGCN_PIECES + GATE_PIECES)
UNITS = (16, 10, 18)
EXPERTS = (8, 8, 16)
STREAM = (L0_GNN_PIECES + 3 * sum(UNITS) + 3 + 3 + 8 + 2 * REL * 2 + 2 + 2 * SLOTS)

SMALL = {}
_at = 0
for _name, _width in (("bg", K), ("bq", K), ("unit_bias", UNITS[0] * 6), ("norm1", K), ("norm2", K),
                      ("router0", K * 8), ("router1", K * 8), ("router2", K * 16), ("br", 8), ("scale", 1),
                      ("att0", 8 * 16), ("att1", K * 2), ("att2", K * 8), ("att3", K * 2)):
    SMALL[_name] = (_at, _width)
    _at += _width
SMALL_WIDTH = _at
BIAS_ROWS = (D, D, 1024, D, D, D, D)
BIAS_AT = [sum(BIAS_ROWS[:i]) for i in range(len(BIAS_ROWS))]

EDGE_LAYERS = (
    dict(rel=1, heads=8, width=128, pieces=((0, 2), (2, 4), (4, 6)), att="att0"),
    dict(rel=1, heads=1, width=768, pieces=((0, 3), (3, 6), (6, 8)), att="att1"),
    dict(rel=REL, heads=4, width=192, pieces=((0, 3), (3, 6)), att="att2"),
    dict(rel=REL, heads=1, width=768, pieces=((0, 3), (3, 6)), att="att3"),
)


class Counts:

    def __init__(self):
        self.count, self.grows, self.inner, self.i = {}, {}, {}, None

    def upto(self, sem, more=1):
        if self.i is None:
            self.count[sem] = self.count.get(sem, 0) + more
            return self.count[sem]
        self.inner[sem] = self.inner.get(sem, 0) + more
        return self.i * self.grows[sem] + (self.count.get(sem, 0) + self.inner[sem])

    @contextmanager
    def loop(self, engine, trips, grows):
        with engine.Fori(0, trips) as i:
            self.i, self.grows, self.inner = i, grows, {}
            yield i
        assert self.inner == grows, (self.inner, grows)
        self.i = None
        for sem, per in grows.items():
            self.count[sem] = self.count.get(sem, 0) + trips * per


def build(nc, x_in, edges, query, small_in, bias_in, bd_in, phi_in, slot_b1_in, slot_b2_in, stream, out):
    with ExitStack() as ctx:
        def sb(name, shape, dt=F32, where=ctx):
            return where.enter_context(nc.sbuf_tensor(name, shape, dt))

        def sem(name):
            return ctx.enter_context(nc.semaphore(name))

        ring = [sb(f"ring{i}", [P, PIECE]) for i in range(RING)]
        x = sb("x", [P, T, D])
        rows = sb("rows", [P, T, D])
        cols = sb("cols", [P, K, N])
        counts = sb("counts", [P, T, REL, N])
        loop_counts = sb("loop_counts", [P, T, N])
        bias = sb("bias", [P, 1024])
        ident = sb("ident", [P, P])
        ones = sb("ones", [P, P])
        tiny = sb("tiny", [P, 2], BF16)
        iota = sb("iota", [P, SLOTS])
        small = sb("small", [P, SMALL_WIDTH])
        stats = sb("stats", [P, T, 2, 6])
        moments = sb("moments", [P, T, 2])
        root = sb("root", [P, SLOTS])
        inverse = sb("inverse", [P, T])
        dinv = sb("dinv", [P, T])

        with ExitStack() as l0:
            query_cols = sb("query_cols", [P, K, B * L], F32, l0)
            query_gate = sb("query_gate", [P, K, B * L], F32, l0)
            hidden_gate = sb("hidden_gate", [P, K, N], F32, l0)
            mean_counts = sb("mean_counts", [P, T, REL * N], F32, l0)
            hidden = sb("hidden", [P, K, N], F32, l0)
            with ExitStack() as part:
                edge_ints = sb("edge_ints", [P, 3, EDGE_TILES], I32, part)
                edge_src = sb("edge_src", [P, EDGE_TILES], F32, part)
                edge_dst = sb("edge_dst", [P, EDGE_TILES], F32, part)
                edge_key = sb("edge_key", [P, EDGE_TILES], F32, part)
                key_iota = sb("key_iota", [P, REL * N], F32, part)
                src_hot = [sb(f"src_hot{i}", [P, N], BF16, part) for i in range(2)]
                key_hot = [sb(f"key_hot{i}", [P, REL * N], BF16, part) for i in range(2)]
                raw_counts = sb("raw_counts", [P, T, REL * N], F32, part)
                in_degree = sb("in_degree", [P, REL * N], F32, part)
            with ExitStack() as part:
                aggregate = [sb(f"aggregate{i}", [P, K, N], F32, part) for i in range(2)]
            with ExitStack() as part:
                chunk = [sb(f"chunk{i}", [P, GROUP, L], F32, part) for i in range(CHUNK_RING)]
            with ExitStack() as part:
                alpha = sb("alpha", [P, K, N], F32, part)

        with ExitStack() as part:
            logits = sb("logits", [P, T, 16], F32, part)
            row_max = sb("row_max", [P, T], F32, part)
            row_sum = sb("row_sum", [P, T], F32, part)
            top = sb("top", [P, T, 8], F32, part)
            top_at = sb("top_at", [P, T, 8], U32, part)
            top_place = sb("top_place", [P, T, 8], F32, part)
            top_weight = sb("top_weight", [P, T, 2], F32, part)
            gap = sb("gap", [P, T], F32, part)
            combine = sb("combine", [P, T, 16], F32, part)
            second = sb("second", [P, T, 16], F32, part)
            combine_cols = sb("combine_cols", [16, N], F32, part)
            unit_weight = sb("unit_weight", [P, T, 18], F32, part)
            bd_rows = sb("bd_rows", [8, D], F32, part)
            gate_part = sb("gate_part", [P, 3, N], F32, part)
            up_part = sb("up_part", [P, 3, N], F32, part)
            squash = sb("squash", [P, 3, N], F32, part)
            act_cols = sb("act_cols", [P, 3, N], F32, part)

        with ExitStack() as part:
            message = sb("message", [P, REL * T * D], F32, part)
            wide_rows = sb("wide_rows", [P, T, 1024], F32, part)
            wide_cols = sb("wide_cols", [P, 8, N], F32, part)
            edge_scores = [sb(f"edge_scores{i}", [P, REL * N], F32, part) for i in range(2)]
            edge_exp = [sb(f"edge_exp{i}", [P, REL * N], F32, part) for i in range(2)]
            edge_turned = [sb(f"edge_turned{i}", [P, REL * T, P], F32, part) for i in range(2)]
            absent = sb("absent", [P, T, REL * N], F32, part)
            all_counts = sb("all_counts", [P, T, N], F32, part)
            queries_keys = sb("queries_keys", [P, T, REL, 16], F32, part)
            keys = sb("keys", [P, T, 16], F32, part)
            key_rows = sb("key_rows", [12, N], F32, part)
            edge_max = sb("edge_max", [P, 2], F32, part)
            edge_negmax = sb("edge_negmax", [P, 2], F32, part)
            edge_sum = sb("edge_sum", [P, 4], F32, part)
            edge_inverse = sb("edge_inverse", [P, 4], F32, part)

        with ExitStack() as part:
            head_q = sb("head_q", [P, K, N], F32, part)
            head_k = sb("head_k", [P, K, N], F32, part)
            values = sb("values", [P, T, D], F32, part)
            context = sb("context", [P, K, N], F32, part)
            normed = sb("normed", [P, T, D], F32, part)
            probs = [sb(f"probs{i}", [P, T, N], F32, part) for i in range(2)]
            probs_turned = [sb(f"probs_turned{i}", [P, T, N], F32, part) for i in range(2)]
            head_max = sb("head_max", [P, 2, T], F32, part)
            head_negmax = sb("head_negmax", [P, 2, T], F32, part)
            head_sum = sb("head_sum", [P, 2, T], F32, part)
            head_inverse = sb("head_inverse", [P, 2, T], F32, part)

        with ExitStack() as part:
            phi = sb("phi", [P, K, SLOTS], F32, part)
            phi_squares = sb("phi_squares", [P, K, SLOTS], F32, part)
            phi_scale = sb("phi_scale", [P, SLOTS], F32, part)
            dispatch = sb("dispatch", [SLOTS, N], F32, part)
            dispatch_rows = sb("dispatch_rows", [P, T, SLOTS], F32, part)
            mixing = sb("mixing", [P, T, SLOTS], F32, part)
            mixing_cols = sb("mixing_cols", [SLOTS, N], F32, part)
            soft = sb("soft", [P, 8], F32, part)
            slot_in = sb("slot_in", [P, K, SLOTS], F32, part)
            slot_mask = [sb(f"slot_mask{i}", [P, K, SLOTS], F32, part) for i in range(2)]
            slot_b1 = sb("slot_b1", [SLOTS, SLOT_HIDDEN], F32, part)
            slot_b2 = sb("slot_b2", [SLOTS, D], F32, part)
            slot_hidden = sb("slot_hidden", [SLOTS, SLOT_HIDDEN], F32, part)
            slot_hidden_cols = sb("slot_hidden_cols", [P, 3, SLOTS], F32, part)
            slot_out = sb("slot_out", [SLOTS, D], F32, part)
            squares = sb("squares", [P, D], F32, part)

        psum = ctx.enter_context(nc.psum_tensor("psum", [P, 8, 512], F32))
        flat = psum[:].rearrange("p b c -> p (b c)")

        small_landed, x_landed, edges_landed, query_landed = (
            sem(n) for n in ("small_landed", "x_landed", "edges_landed", "query_landed"))
        piece_landed = [sem(f"piece_landed{i}") for i in range(RING)]
        piece_used = sem("piece_used")
        bias_landed, bias_used = sem("bias_landed"), sem("bias_used")
        bd_landed, slots_landed = sem("bd_landed"), sem("slots_landed")
        arena_free = sem("arena_free")
        pool_wrote, vector_wrote, scalar_wrote = sem("pool_wrote"), sem("vector_wrote"), sem("scalar_wrote")
        constants_ready, ones_ready = sem("constants_ready"), sem("ones_ready")
        root_asked, root_ready = sem("root_asked"), sem("root_ready")
        exp_asked, exp_ready = sem("exp_asked"), sem("exp_ready")
        rows_ready, turned, cols_ready, rows_done = (
            sem(n) for n in ("rows_ready", "turned", "cols_ready", "rows_done"))
        tile_done = sem("tile_done")
        hot_ready, hot_used, counted = sem("hot_ready"), sem("hot_used"), sem("counted")
        raw_ready, degree_done, counts_turned, counts_ready = (
            sem(n) for n in ("raw_ready", "degree_done", "counts_turned", "counts_ready"))
        aggregated, aggregate_ready = sem("aggregated"), sem("aggregate_ready")
        gate_hidden_ready, chunk_summed, chunk_squashed, chunk_weighted, chunk_folded, chunk_reduced = (
            sem(n) for n in ("gate_hidden_ready", "chunk_summed", "chunk_squashed", "chunk_weighted",
                             "chunk_folded", "chunk_reduced"))
        tanh_ready, alpha_ready, hidden_ready, turned_back, rows_back = (
            sem(n) for n in ("tanh_ready", "alpha_ready", "hidden_ready", "turned_back", "rows_back"))
        logits_taken = sem("logits_taken")
        logits_done, combine_ready, combine_turned, combine_cols_ready = (
            sem(n) for n in ("logits_done", "combine_ready", "combine_turned", "combine_cols_ready"))
        gate_done, gate_clipped, squashed, up_done, act_ready, down_done, down_taken = (
            sem(n) for n in ("gate_done", "gate_clipped", "squashed", "up_done", "act_ready", "down_done",
                             "down_taken"))
        query_keys_done, keys_ready, keys_turned, key_rows_ready = (
            sem(n) for n in ("query_keys_done", "keys_ready", "keys_turned", "key_rows_ready"))
        picked, lifted, edge_max_ready, edge_exp_ready, edge_weighted, edges_turned, edges_copied, mixed, stored = (
            sem(n) for n in ("picked", "lifted", "edge_max_ready", "edge_exp_ready", "edge_weighted",
                             "edges_turned", "edges_copied", "mixed", "stored"))
        heads_ready, scored, head_max_ready, probs_exp, probs_ready, probs_done, probs_copied, context_done, \
            context_ready = (sem(n) for n in ("heads_ready", "scored", "head_max_ready", "probs_exp", "probs_ready",
                                              "probs_done", "probs_copied", "context_done", "context_ready"))
        phi_squared, phi_summed, phi_ready, slot_logits_done, soft_ready, soft_turned, soft_copied = (
            sem(n) for n in ("phi_squared", "phi_summed", "phi_ready", "slot_logits_done", "soft_ready",
                             "soft_turned", "soft_copied"))
        slot_in_done, mask_ready, mask_used, slot_hidden_done, slot_pre, slot_act, slot_hidden_turned, \
            slot_hidden_ready, slot_out_done, slot_out_ready = (
                sem(n) for n in ("slot_in_done", "mask_ready", "mask_used", "slot_hidden_done", "slot_pre", "slot_act",
                                 "slot_hidden_turned", "slot_hidden_ready", "slot_out_done", "slot_out_ready"))
        x_final, out_stored = sem("x_final"), sem("out_stored")

        def row_parts(width):
            return [(0, 0, min(width, 512))] + ([(1, 512, width - 512)] if width > 512 else [])

        def row_bank(t, j, n):
            if j == 0:
                return psum[:, 3 + t, 0:n]
            return psum[:, 5, t * N:t * N + n] if n == N else psum[:, 5 + t, 0:n]

        def opens(t, j, n):
            return t == 0 or j == 0 or n != N

        def col_tile(f):
            return flat[:, f * N:(f + 1) * N]

        UNIT_BANKS = ((0, 1), (2, 6))

        def unit_bank(part, last):
            return psum[:, UNIT_BANKS[part][last], 0:N if last else 2 * N]

        def unit_tile(part, f):
            return psum[:, UNIT_BANKS[part][f // 2], f % 2 * N:(f % 2 + 1) * N]

        def node_tile(t):
            return slice(t * P, (t + 1) * P)

        def small_at(name, i=0, n=1):
            return small[:, SMALL[name][0] + i:SMALL[name][0] + i + n]

        flat_x = x[:].rearrange("p t d -> p (t d)")
        flat_rows = rows[:].rearrange("p t d -> p (t d)")
        flat_cols = cols[:].rearrange("p k n -> p (k n)")
        flat_hidden = hidden[:].rearrange("p k n -> p (k n)")
        flat_gate = hidden_gate[:].rearrange("p k n -> p (k n)")
        flat_counts = counts[:].rearrange("p t r n -> p (t r n)")

        def message_rows(layer):
            width = layer["heads"] * layer["width"]
            n = layer["rel"] * T * width
            return message[:, 0:n].rearrange("p (r t d) -> p r t d", r=layer["rel"], t=T)

        block = ctx.enter_context(nc.Block())

        @block.sync
        def _(sp):
            seen = Counts()
            sp.dma_start(x[:], x_in.rearrange("(t p) d -> p t d", p=P)).then_inc(x_landed, 16)
            for i in range(RING):
                sp.dma_start(ring[i][:], stream[i]).then_inc(piece_landed[i], 16)
            turns, rest = divmod(STREAM - RING, RING)
            with seen.loop(sp, turns, {piece_used: RING}) as i:
                for s in range(RING):
                    sp.wait_ge(piece_used, seen.upto(piece_used))
                    piece = stream[bass.ds(i * RING + (RING + s), 1)].rearrange("a p c -> (a p) c")
                    sp.dma_start(ring[s][:], piece).then_inc(piece_landed[s], 16)
            for s in range(rest):
                sp.wait_ge(piece_used, seen.upto(piece_used))
                sp.dma_start(ring[s][:], stream[STREAM - rest + s]).then_inc(piece_landed[s], 16)
            sp.wait_ge(x_final, 1)
            sp.dma_start(out.rearrange("(t p) d -> p t d", p=P), x[:]).then_inc(out_stored, 16)
            sp.wait_ge(out_stored, 16)

        @block.gpsimd
        def _(pool):
            seen = Counts()
            pool.memset(ident[:], 0.0).then_inc(pool_wrote, 1)
            pool.wait_ge(pool_wrote, seen.upto(pool_wrote))
            pool.affine_select(out=ident[:], in_=ident[:], compare_op=ALU.not_equal, fill=1.0, base=0,
                               pattern=[[-1, P]], channel_multiplier=1).then_inc(constants_ready, 1)
            pool.iota(iota[:], [[1, SLOTS]], base=0, channel_multiplier=0,
                      allow_small_or_imprecise_dtypes=True).then_inc(constants_ready, 1)
            pool.iota(key_iota[:], [[1, REL * N]], base=0, channel_multiplier=0,
                      allow_small_or_imprecise_dtypes=True).then_inc(constants_ready, 1)

            def load_bias(n):
                if n:
                    pool.wait_ge(bias_used, seen.upto(bias_used))
                at, width = BIAS_AT[n], BIAS_ROWS[n]
                pool.dma_start(bias[:, 0:width], bias_in[:, at:at + width].broadcast_to([P, width]))\
                    .then_inc(bias_landed, 16)

            def sum_chunk(c, slot):
                by_node = flat_gate[:, bass.ds(c * GROUP, GROUP)].unsqueeze(2).broadcast_to([P, GROUP, L])
                by_query = query_gate[:].rearrange("p k q -> p (k q)")[:, bass.ds(c * L, L)]\
                    .unsqueeze(1).broadcast_to([P, GROUP, L])
                pool.tensor_tensor(chunk[slot][:], by_node, by_query, ALU.add).then_inc(chunk_summed, 1)

            load_bias(0)
            for layer in range(2):
                pool.wait_ge(gate_hidden_ready, seen.upto(gate_hidden_ready, 6 + 3 if layer == 0 else 3))
                for c in range(CHUNK_RING):
                    sum_chunk(c, c)
                with seen.loop(pool, CHUNKS // CHUNK_RING - 1, {chunk_folded: CHUNK_RING}) as i:
                    for s in range(CHUNK_RING):
                        pool.wait_ge(chunk_folded, seen.upto(chunk_folded))
                        sum_chunk(i * CHUNK_RING + (CHUNK_RING + s), s)
                seen.upto(chunk_folded, CHUNK_RING)
                load_bias(layer + 1)
            pool.wait_ge(arena_free, seen.upto(arena_free))
            pool.dma_start(bd_rows[:], bd_in).then_inc(bd_landed, 16)
            for n in range(3, len(BIAS_ROWS)):
                load_bias(n)
            pool.wait_ge(arena_free, seen.upto(arena_free))
            pool.dma_start(phi[:], phi_in).then_inc(slots_landed, 16)
            pool.dma_start(slot_b1[:], slot_b1_in).then_inc(slots_landed, 16)
            pool.dma_start(slot_b2[:], slot_b2_in).then_inc(slots_landed, 16)

        @block.tensor
        def _(pe):
            seen = Counts()
            place = [0]

            def signal(what, n=1):
                pe.matmul(psum[0:2, 7, 508:510], tiny[:], tiny[:], start=True, stop=True).then_inc(what, n)

            def piece(turn=None, ahead=0):
                n = place[0] + ahead
                slot = n % RING
                rounds = n // RING + 1
                if turn is None:
                    pe.wait_ge(piece_landed[slot], 16 * rounds)
                else:
                    pe.wait_ge(piece_landed[slot], turn * 16 + 16 * rounds)
                return ring[slot]

            def use(n=1):
                place[0] += n

            def product_rows(source, pieces, width, first=True, last=True):
                end = pieces[-1][1] - 1
                for k0, k1 in pieces:
                    weights = piece()
                    for k in range(k0, k1):
                        for t in range(T):
                            for j, c, n in row_parts(width):
                                at = (k - k0) * width + c
                                mm = pe.matmul(row_bank(t, j, n), source[:, k, node_tile(t)],
                                               weights[:, at:at + n], start=first and k == 0 and opens(t, j, n),
                                               stop=last and k == end, skip_group_check=True)
                    mm.then_inc(piece_used, 1)
                    use()
                if last:
                    signal(rows_done, 1)

            def product_cols(source, n, tile, done):
                for half in range(2):
                    weights = piece()
                    for f in range(3):
                        for k in range(K):
                            mm = pe.matmul(tile(3 * half + f), weights[:, k * HALF + f * P:k * HALF + (f + 1) * P],
                                           source[:, k, 0:n], start=k == 0, stop=k == K - 1)
                        if f == 2:
                            mm.then_inc(piece_used, 1)
                        if n == 512 or (3 * half + f) % 2 == 1:
                            signal(done)
                    use()

            def turn_rows(source, tiles=K):
                pe.wait_ge(rows_ready, seen.upto(rows_ready))
                for k in range(tiles):
                    for t in range(T):
                        mm = pe.transpose(flat[:, k * N + t * P:k * N + (t + 1) * P],
                                          source[:, t, k * P:(k + 1) * P], ident[:])
                    if k % 2 == 1:
                        mm.then_inc(turned, 1)
                pe.wait_ge(cols_ready, seen.upto(cols_ready, tiles // 2))

            def turn_cols_back(source):
                for t in range(T):
                    for k in range(K):
                        at = t * D + k * P
                        mm = pe.transpose(flat[:, at:at + P], source[:, k, node_tile(t)], ident[:])
                        if (at + P) % 512 == 0:
                            mm.then_inc(turned_back, 1)

            pe.wait_ge(constants_ready, seen.upto(constants_ready, 3))
            pe.wait_ge(ones_ready, seen.upto(ones_ready))
            pe.wait_ge(small_landed, seen.upto(small_landed, 16))

            def count_edges():
                def tile(q, first, last):
                    pe.wait_ge(hot_ready, seen.upto(hot_ready))
                    for t in range(T):
                        for j, c, n in row_parts(REL * N):
                            mm = pe.matmul(row_bank(t, j, n), src_hot[q][:, node_tile(t)], key_hot[q][:, c:c + n],
                                           start=first and opens(t, j, n), stop=last, skip_group_check=True)
                    mm.then_inc(hot_used, 1)

                tile(0, True, False)
                tile(1, False, False)
                with seen.loop(pe, EDGE_TILES // 2 - 2, {hot_ready: 2}):
                    tile(0, False, False)
                    tile(1, False, False)
                tile(0, False, False)
                tile(1, False, True)
                signal(counted, 1)
                pe.wait_ge(raw_ready, seen.upto(raw_ready))
                for j, c, n in row_parts(REL * N):
                    for t in range(T):
                        mm = pe.matmul(row_bank(0, j, n), ones[:], raw_counts[:, t, c:c + n],
                                       start=t == 0, stop=t == T - 1)
                mm.then_inc(degree_done, 1)
                for t in range(T):
                    for r in range(REL):
                        for s in range(T):
                            at = t * REL * N + r * N + s * P
                            mm = pe.transpose(flat[:, at:at + P], raw_counts[:, s, r * N + t * P:r * N + (t + 1) * P],
                                              ident[:])
                mm.then_inc(counts_turned, 1)

            def l0_gnn():
                count_edges()
                pe.wait_ge(counts_ready, seen.upto(counts_ready))
                pe.wait_ge(query_landed, seen.upto(query_landed, 16))
                product_cols(query_cols, B * L, lambda f: psum[:, f, 0:512], tile_done)
                pe.wait_ge(gate_hidden_ready, seen.upto(gate_hidden_ready, 6))
                for layer in range(2):
                    if layer == 0:
                        turn_rows(rows)
                        source = cols
                    else:
                        pe.wait_ge(rows_back, seen.upto(rows_back, 3))
                        source = hidden

                    def aggregate_nodes(r):
                        for f in range(K):
                            for s in range(T):
                                mm = pe.matmul(col_tile(f), rows[:, s, f * P:(f + 1) * P],
                                               mean_counts[:, s, r * N:(r + 1) * N], start=s == 0, stop=s == T - 1)
                            if f % 2 == 1:
                                mm.then_inc(aggregated, 1)

                    halves = ((0, 3), (3, 6))
                    aggregate_nodes(0)
                    product_rows(source, halves, D, last=False)
                    for r in range(REL):
                        pe.wait_ge(aggregate_ready, seen.upto(aggregate_ready, 3))
                        if r + 1 < REL:
                            aggregate_nodes(r + 1)
                        product_rows(aggregate[r % 2], halves, D, first=False, last=r == REL - 1)
                    turn_rows(rows)
                    product_cols(cols, N, col_tile, tile_done)
                    seen.upto(gate_hidden_ready, 3)

                    def fold(q):
                        pe.wait_ge(chunk_weighted, seen.upto(chunk_weighted))
                        for s in range(L // 16):
                            mm = pe.matmul(psum[:, 5 + q, :].rearrange("p (n l) -> p n l", n=GROUP), ident[:],
                                           chunk[q][:, :, 16 * s:16 * s + 16], start=s == 0, stop=s == L // 16 - 1)
                        mm.then_inc(chunk_folded, 1)

                    for c in range(CHUNK_RING):
                        fold(c)
                    with seen.loop(pe, CHUNKS // CHUNK_RING - 1,
                                   {chunk_weighted: CHUNK_RING, chunk_reduced: CHUNK_RING}):
                        for q in range(CHUNK_RING):
                            pe.wait_ge(chunk_reduced, seen.upto(chunk_reduced))
                            fold(q)
                    pe.wait_ge(chunk_reduced, seen.upto(chunk_reduced, CHUNK_RING))
                    for half in range(2):
                        hidden_part, query_part = piece(), piece(ahead=1)
                        for f in range(3):
                            for part, (weights, source) in enumerate(((hidden_part, cols), (query_part, hidden_gate))):
                                for k in range(K):
                                    mm = pe.matmul(col_tile(3 * half + f),
                                                   weights[:, k * HALF + f * P:k * HALF + (f + 1) * P],
                                                   source[:, k, :], start=part == 0 and k == 0,
                                                   stop=part == 1 and k == K - 1)
                            if (3 * half + f) % 2 == 1:
                                mm.then_inc(tile_done, 1)
                        signal(piece_used, 2)
                        use(2)
                    pe.wait_ge(hidden_ready, seen.upto(hidden_ready))
                    turn_cols_back(hidden)

            def experts(layer):
                units = UNITS[layer]
                count = EXPERTS[layer]
                turn_rows(rows)
                at, _ = SMALL[f"router{layer}"]
                for t in range(T):
                    for k in range(K):
                        mm = pe.matmul(psum[:, 6, t * 16:t * 16 + count], cols[:, k, node_tile(t)],
                                       small[:, at + k * count:at + (k + 1) * count], start=k == 0, stop=k == K - 1)
                mm.then_inc(logits_done, 1)
                pe.wait_ge(logits_taken, seen.upto(logits_taken))
                if layer == 0:
                    pe.wait_ge(combine_ready, seen.upto(combine_ready))
                    for t in range(T):
                        mm = pe.transpose(psum[0:count, 6, 64 + t * P:64 + (t + 1) * P], combine[:, t, 0:count],
                                          ident[:])
                    mm.then_inc(combine_turned, 1)
                    pe.wait_ge(combine_cols_ready, seen.upto(combine_cols_ready))
                    pe.wait_ge(bd_landed, seen.upto(bd_landed, 16))
                    for t in range(T):
                        for j, c, n in row_parts(D):
                            mm = pe.matmul(row_bank(t, j, n), combine_cols[0:count, node_tile(t)],
                                           bd_rows[0:count, c:c + n], start=opens(t, j, n), stop=True,
                                           skip_group_check=True)
                    mm.then_inc(down_done, 1)

                def unit(turn, ahead):
                    for n, done in enumerate((gate_done, up_done)):
                        weights = piece(turn, ahead + n)
                        for f in range(3):
                            for k in range(K):
                                mm = pe.matmul(unit_tile(n, f), weights[:, k * HALF + f * P:k * HALF + (f + 1) * P],
                                               cols[:, k, :], start=k == 0, stop=k == K - 1)
                            if f > 0:
                                mm.then_inc(done, 1)
                        signal(piece_used, 1)
                    weights = piece(turn, ahead + 2)
                    if layer == 0 or turn is not None or ahead > 0 or place[0] != start:
                        pe.wait_ge(down_taken, seen.upto(down_taken))
                    for f in range(3):
                        if f != 1:
                            pe.wait_ge(act_ready, seen.upto(act_ready))
                        for t in range(T):
                            for j, c, n in row_parts(D):
                                mm = pe.matmul(row_bank(t, j, n), act_cols[:, f, node_tile(t)],
                                               weights[:, f * D + c:f * D + c + n],
                                               start=f == 0 and opens(t, j, n), stop=f == 2, skip_group_check=True)
                    mm.then_inc(down_done, 1)
                    signal(piece_used, 1)

                start = place[0]
                unit(None, 0)
                use(3)
                turns, rest = divmod(units - 1, RING // 3)
                with seen.loop(pe, turns, {down_taken: RING // 3, act_ready: 2 * RING // 3}) as i:
                    for u in range(RING // 3):
                        unit(i, 3 * u)
                use(turns * RING)
                for _ in range(rest):
                    unit(None, 0)
                    use(3)
                pe.wait_ge(down_taken, seen.upto(down_taken))

            def edge_layer(n):
                layer = EDGE_LAYERS[n]
                rel, heads, width = layer["rel"], layer["heads"], layer["width"]
                out_width = heads * width
                tiles = out_width // P
                source = wide_cols if n == 1 else cols
                messages = message_rows(layer)
                turn_rows(wide_rows if n == 1 else rows, 8 if n == 1 else K)
                at, _ = SMALL[layer["att"]]
                for r in range(rel):
                    product_rows(source, layer["pieces"], out_width)
                    turn_rows(messages[:, r], tiles)
                    for t in range(T):
                        for k in range(tiles):
                            mm = pe.matmul(psum[:, 7, (t * rel + r) * 16:(t * rel + r) * 16 + 2 * heads],
                                           wide_cols[:, k, node_tile(t)],
                                           small[:, at + k * 2 * heads:at + (k + 1) * 2 * heads],
                                           start=k == 0, stop=k == tiles - 1)
                mm.then_inc(query_keys_done, 1)
                pe.wait_ge(keys_ready, seen.upto(keys_ready))
                count = rel * heads
                for t in range(T):
                    mm = pe.transpose(psum[0:count, 7, t * P:(t + 1) * P], keys[:, t, 0:count], ident[:])
                mm.then_inc(keys_turned, 1)
                pe.wait_ge(key_rows_ready, seen.upto(key_rows_ready))
                items = [(t, h) for h in range(heads) for t in range(T)]

                def pick_keys(i):
                    if i >= 2:
                        pe.wait_ge(lifted, seen.upto(lifted))
                    t, h = items[i]
                    for r in range(rel):
                        at = i % 2 * 1024 + r * N
                        row = r * heads + h
                        mm = pe.matmul(flat[:, at:at + N], ident[0:count, row:row + 1].broadcast_to([count, P]),
                                       key_rows[0:count, :],
                                       start=True, stop=True)
                    mm.then_inc(picked, 1)

                def turn_edges(i):
                    pe.wait_ge(edge_weighted, seen.upto(edge_weighted))
                    for m in range(rel * T):
                        at = 4 * 512 + m * P
                        mm = pe.transpose(flat[:, at:at + P], edge_exp[i % 2][:, m * P:(m + 1) * P], ident[:])
                    mm.then_inc(edges_turned, 1)

                def mix(i):
                    t, h = items[i]
                    pe.wait_ge(edges_copied, seen.upto(edges_copied))
                    if width > 512:
                        if i >= 1:
                            pe.wait_ge(stored, seen.upto(stored))
                    elif i >= 2:
                        pe.wait_ge(stored, seen.upto(stored))
                    for j, c, size in row_parts(width):
                        bank = 6 + j if width > 512 else 6 + i % 2
                        for m in range(rel * T):
                            r, s = divmod(m, T)
                            mm = pe.matmul(psum[:, bank, 0:size], edge_turned[i % 2][:, m, :],
                                           messages[:, r, s, h * width + c:h * width + c + size],
                                           start=m == 0, stop=m == rel * T - 1)
                    mm.then_inc(mixed, 1)

                last = len(items)
                for s in range(last + 3):
                    if s < last:
                        pick_keys(s)
                    if 0 <= s - 3 < last:
                        mix(s - 3)
                    if 0 <= s - 2 < last:
                        turn_edges(s - 2)
                pe.wait_ge(lifted, seen.upto(lifted, 2))
                pe.wait_ge(stored, seen.upto(stored, 1 if width > 512 else 2))

            def self_attention():
                turn_rows(normed)
                product_cols(cols, N, col_tile, tile_done)
                pe.wait_ge(heads_ready, seen.upto(heads_ready, 3))
                product_cols(cols, N, col_tile, tile_done)
                product_rows(cols, ((0, 3), (3, 6)), D)
                pe.wait_ge(heads_ready, seen.upto(heads_ready, 3))
                pe.wait_ge(rows_ready, seen.upto(rows_ready))

                def scores(h):
                    if h >= 2:
                        pe.wait_ge(probs_exp, seen.upto(probs_exp))
                    at = h % 2 * HEAD
                    for t in range(T):
                        mm = pe.matmul(psum[:, h % 2, t * N:(t + 1) * N], head_q[at:at + HEAD, h // 2, node_tile(t)],
                                       head_k[at:at + HEAD, h // 2, :], start=True, stop=True)
                    mm.then_inc(scored, 1)

                def turn_probs(h):
                    pe.wait_ge(probs_ready, seen.upto(probs_ready))
                    for s in range(T):
                        for t in range(T):
                            mm = pe.transpose(psum[:, 2 + h % 2, s * N + t * P:s * N + (t + 1) * P],
                                              probs[h % 2][:, t, s * P:(s + 1) * P], ident[:])
                    mm.then_inc(probs_done, 1)

                def mix_values(h):
                    pe.wait_ge(probs_copied, seen.upto(probs_copied))
                    if h >= 2:
                        pe.wait_ge(context_ready, seen.upto(context_ready))
                    at = h % 2 * HEAD
                    for s in range(T):
                        mm = pe.matmul(psum[at:at + HEAD, 4 + h % 2, 0:N], values[:, s, h * HEAD:(h + 1) * HEAD],
                                       probs_turned[h % 2][:, s, :], start=s == 0, stop=s == T - 1)
                    mm.then_inc(context_done, 1)

                for s in range(HEADS + 2):
                    if s < HEADS:
                        scores(s)
                    if 0 <= s - 1 < HEADS:
                        turn_probs(s - 1)
                    if 0 <= s - 2 < HEADS:
                        mix_values(s - 2)
                pe.wait_ge(probs_exp, seen.upto(probs_exp, 2))
                pe.wait_ge(context_ready, seen.upto(context_ready, 2))
                product_rows(context, ((0, 3), (3, 6)), D)

            def l1_gnn():
                edge_layer(0)
                edge_layer(1)

            def l1_ffn():
                self_attention()
                experts(1)

            def l2_gnn():
                edge_layer(2)
                edge_layer(3)

            def l3_gnn():
                turn_rows(rows)
                product_rows(cols, ((0, 3), (3, 6)), D)
                pe.wait_ge(rows_ready, seen.upto(rows_ready))
                for t in range(T):
                    for j, c, n in row_parts(D):
                        for s in range(T):
                            mm = pe.matmul(row_bank(t, j, n), loop_counts[:, s, node_tile(t)], rows[:, s, c:c + n],
                                           start=s == 0 and opens(t, j, n), stop=s == T - 1, skip_group_check=True)
                mm.then_inc(rows_done, 1)

            def l3_ffn():
                pe.wait_ge(phi_squared, seen.upto(phi_squared))
                for k in range(K):
                    mm = pe.matmul(psum[:, 7, 0:SLOTS], ones[:], phi_squares[:, k, :], start=k == 0, stop=k == K - 1)
                mm.then_inc(phi_summed, 1)
                turn_rows(rows)
                pe.wait_ge(phi_ready, seen.upto(phi_ready))
                for t in range(T):
                    for k in range(K):
                        pe.matmul(psum[:, 3, t * SLOTS:(t + 1) * SLOTS], cols[:, k, node_tile(t)], phi[:, k, :],
                                  start=k == 0, stop=k == K - 1)
                for k in range(K):
                    mm = pe.matmul(psum[0:SLOTS, 4, 0:N], phi[:, k, :], cols[:, k, :], start=k == 0, stop=k == K - 1)
                mm.then_inc(slot_logits_done, 1)
                pe.wait_ge(soft_ready, seen.upto(soft_ready))
                for t in range(T):
                    pe.transpose(psum[0:SLOTS, 5, t * P:(t + 1) * P], mixing[:, t, :], ident[:])
                    mm = pe.transpose(psum[:, 6, t * SLOTS:(t + 1) * SLOTS], dispatch[:, node_tile(t)],
                                      ident[0:SLOTS, 0:SLOTS])
                mm.then_inc(soft_turned, 1)
                pe.wait_ge(soft_copied, seen.upto(soft_copied))
                for f in range(K):
                    for s in range(T):
                        mm = pe.matmul(psum[:, 7, f * SLOTS:(f + 1) * SLOTS], rows[:, s, f * P:(f + 1) * P],
                                       dispatch_rows[:, s, :], start=s == 0, stop=s == T - 1)
                mm.then_inc(slot_in_done, 1)

                def slot_products(tiles, width):
                    def one(turn, ahead, q, first=False, last=False):
                        pe.wait_ge(mask_ready, seen.upto(mask_ready))
                        weights = piece(turn, ahead)
                        for k in range(tiles):
                            for j, c, n in row_parts(width):
                                mm = pe.matmul(psum[0:SLOTS, 3 + j, 0:n], slot_mask[q][:, k, :],
                                               weights[:, k * width + c:k * width + c + n],
                                               start=first and k == 0, stop=last and k == tiles - 1)
                        mm.then_inc(piece_used, 1)
                        signal(mask_used, 1)

                    one(None, 0, 0, first=True)
                    use()
                    one(None, 0, 1)
                    use()
                    turns = (SLOTS - 4) // RING
                    with seen.loop(pe, turns, {mask_ready: RING}) as i:
                        for a in range(RING):
                            one(i, a, a % 2)
                    use(turns * RING)
                    one(None, 0, 0)
                    use()
                    one(None, 0, 1, last=True)
                    use()

                assert (SLOTS - 4) % RING == 0
                slot_products(K, SLOT_HIDDEN)
                signal(slot_hidden_done, 1)
                pe.wait_ge(slot_act, seen.upto(slot_act))
                for k in range(3):
                    mm = pe.transpose(psum[:, 5, k * SLOTS:(k + 1) * SLOTS], slot_hidden[:, k * P:(k + 1) * P],
                                      ident[0:SLOTS, 0:SLOTS])
                mm.then_inc(slot_hidden_turned, 1)
                slot_products(3, D)
                signal(slot_out_done, 1)
                pe.wait_ge(slot_out_ready, seen.upto(slot_out_ready))
                for t in range(T):
                    for j, c, n in row_parts(D):
                        mm = pe.matmul(row_bank(t, j, n), mixing_cols[:, node_tile(t)], slot_out[:, c:c + n],
                                       start=opens(t, j, n), stop=True, skip_group_check=True)
                mm.then_inc(rows_done, 1)

            for stage in (l0_gnn, lambda: experts(0), l1_gnn, l1_ffn, l2_gnn, lambda: experts(2), l3_gnn,
                          l3_ffn):
                stage()

        @block.scalar
        def _(act):
            seen = Counts()
            act.dma_start(edge_ints[:], edges).then_inc(edges_landed, 16)
            act.dma_start(small[:], small_in).then_inc(small_landed, 16)
            act.dma_start(query_cols[:], query).then_inc(query_landed, 16)
            act.wait_ge(small_landed, seen.upto(small_landed, 16))

            def take_root(n, p=P):
                act.wait_ge(root_asked, seen.upto(root_asked))
                act.activation(root[0:p, 0:n], root[0:p, 0:n], ACT.Sqrt).then_inc(root_ready, 1)

            def copy_turned(target, tiles=K, relu=False, scale=None):
                for b in range(tiles // 2):
                    act.wait_ge(turned, seen.upto(turned))
                    for f in ((2 * b,) if scale is None else (2 * b, 2 * b + 1)):
                        n = 2 if scale is None else 1
                        to = target[:, f:f + n, :].rearrange("p k n -> p (k n)")
                        of = flat[:, f * N:(f + n) * N]
                        if scale is None:
                            ins = act.activation(to, of, ACT.Relu if relu else ACT.Copy)
                        else:
                            ins = act.activation(to, of, ACT.Identity, scale=small_at(scale, f))
                    ins.then_inc(cols_ready, 1)

            def l0_gnn():
                for f in range(K):
                    act.wait_ge(tile_done, seen.upto(tile_done))
                    act.activation(query_gate[:, f, :], psum[:, f, :], ACT.Identity, bias=small_at("bg", f))\
                        .then_inc(gate_hidden_ready, 1)
                take_root(T)
                for layer in range(2):
                    if layer == 0:
                        copy_turned(cols)
                    for r in range(REL):
                        for b in range(3):
                            act.wait_ge(aggregated, seen.upto(aggregated))
                            act.activation(aggregate[r % 2][:, 2 * b:2 * b + 2, :].rearrange("p k n -> p (k n)"),
                                           psum[:, b, :], ACT.Copy).then_inc(aggregate_ready, 1)
                    copy_turned(cols, relu=True)
                    for b in range(3):
                        act.wait_ge(tile_done, seen.upto(tile_done))
                        act.activation(flat_gate[:, 512 * b:512 * b + 512], psum[:, b, :], ACT.Copy)\
                            .then_inc(gate_hidden_ready, 1)
                    with seen.loop(act, CHUNKS // CHUNK_RING, {chunk_summed: CHUNK_RING}):
                        for q in range(CHUNK_RING):
                            act.wait_ge(chunk_summed, seen.upto(chunk_summed))
                            act.activation(chunk[q][:], chunk[q][:], ACT.Sigmoid).then_inc(chunk_squashed, 1)
                    act.wait_ge(chunk_reduced, seen.upto(chunk_reduced, CHUNKS))
                    act.activation(flat_hidden, flat_gate, ACT.Tanh).then_inc(tanh_ready, 1)
                    for f in range(K):
                        if f % 2 == 0:
                            act.wait_ge(tile_done, seen.upto(tile_done))
                        act.activation(alpha[:, f, :], col_tile(f), ACT.Sigmoid, bias=small_at("bq", f))\
                            .then_inc(alpha_ready, 1)
                    if layer == 0:
                        for b in range(3):
                            act.wait_ge(turned_back, seen.upto(turned_back))
                            act.activation(flat_rows[:, 512 * b:512 * b + 512], psum[:, b, :], ACT.Copy)\
                                .then_inc(rows_back, 1)

            def experts(layer):
                take_root(T)
                copy_turned(cols, scale="norm2" if layer == 1 else None)
                act.wait_ge(exp_asked, seen.upto(exp_asked))
                if layer == 0:
                    act.activation(gap[:], gap[:], ACT.Exp).then_inc(exp_ready, 1)
                else:
                    act.activation(logits[:, :, 0:EXPERTS[layer]], logits[:, :, 0:EXPERTS[layer]], ACT.Exp)\
                        .then_inc(exp_ready, 1)
                with seen.loop(act, UNITS[layer] // 2, {gate_clipped if layer == 0 else gate_done: 4}):
                    for _ in range(2):
                        for last, tiles in ((0, slice(0, 2)), (1, slice(2, 3))):
                            to = squash[:, tiles, :].rearrange("p f n -> p (f n)")
                            if layer == 0:
                                act.wait_ge(gate_clipped, seen.upto(gate_clipped))
                                of = gate_part[:, tiles, :].rearrange("p f n -> p (f n)")
                                act.activation(to, of, ACT.Sigmoid, scale=1.702).then_inc(squashed, 1)
                            else:
                                act.wait_ge(gate_done, seen.upto(gate_done))
                                act.activation(to, unit_bank(0, last), ACT.Silu).then_inc(squashed, 1)
                if layer == 0:
                    seen.upto(gate_done, 2 * UNITS[0])

            def edge_layer(n):
                layer = EDGE_LAYERS[n]
                rel, heads, width = layer["rel"], layer["heads"], layer["width"]
                tiles = heads * width // P
                if n % 2 == 0:
                    take_root(T)
                if n == 1:
                    copy_turned(wide_cols, 8, relu=True)
                else:
                    copy_turned(cols)
                for _ in range(rel):
                    copy_turned(wide_cols, tiles)
                count = rel * heads
                act.wait_ge(keys_turned, seen.upto(keys_turned))
                act.activation(key_rows[0:count, :], psum[0:count, 7, 0:N], ACT.Copy).then_inc(key_rows_ready, 1)
                items = [(t, h) for h in range(heads) for t in range(T)]
                act.wait_ge(keys_ready, seen.upto(keys_ready))

                def lift(i):
                    t, h = items[i]
                    act.wait_ge(picked, seen.upto(picked))
                    if i >= 2:
                        act.wait_ge(edge_exp_ready, seen.upto(edge_exp_ready))
                    for r in range(rel):
                        at = i % 2 * 1024 + r * N
                        ins = act.activation(edge_scores[i % 2][:, r * N:(r + 1) * N], flat[:, at:at + N],
                                             ACT.Identity, bias=queries_keys[:, t, r, h:h + 1])
                    ins.then_inc(lifted, 1)

                def exp_edges(i):
                    act.wait_ge(edge_max_ready, seen.upto(edge_max_ready))
                    act.activation(edge_exp[i % 2][:, 0:rel * N], edge_scores[i % 2][:, 0:rel * N], ACT.Exp,
                                   bias=edge_negmax[:, i % 2:i % 2 + 1]).then_inc(edge_exp_ready, 1)

                def copy_edges(i):
                    act.wait_ge(edges_turned, seen.upto(edges_turned))
                    at = 4 * 512
                    act.activation(edge_turned[i % 2][:, 0:rel * T, :].rearrange("p m n -> p (m n)"),
                                   flat[:, at:at + rel * T * P], ACT.Copy).then_inc(edges_copied, 1)

                last = len(items)
                for s in range(last + 2):
                    if s < last:
                        lift(s)
                    if 0 <= s - 1 < last:
                        exp_edges(s - 1)
                    if 0 <= s - 2 < last:
                        copy_edges(s - 2)
                act.wait_ge(edge_exp_ready, seen.upto(edge_exp_ready, 2))
                if n == 2:
                    act.wait_ge(exp_asked, seen.upto(exp_asked))
                    act.activation(wide_rows[:, :, 0:D], wide_rows[:, :, 0:D], ACT.Exp).then_inc(exp_ready, 1)

            def self_attention():
                take_root(T)
                take_root(T)
                copy_turned(cols, scale="norm1")
                for target in (head_q, head_k):
                    for b in range(3):
                        act.wait_ge(tile_done, seen.upto(tile_done))
                        act.activation(target[:, 2 * b:2 * b + 2, :].rearrange("p k n -> p (k n)"), psum[:, b, :],
                                       ACT.Copy).then_inc(heads_ready, 1)

                def exps(h):
                    act.wait_ge(head_max_ready, seen.upto(head_max_ready))
                    for t in range(T):
                        ins = act.activation(probs[h % 2][:, t, :], psum[:, h % 2, t * N:(t + 1) * N], ACT.Exp,
                                             bias=head_negmax[:, h % 2, t:t + 1], scale=HEAD ** -0.5,
                                             accum_out=head_sum[:, h % 2, t:t + 1])
                    ins.then_inc(probs_exp, 1)

                def copy_probs(h):
                    act.wait_ge(probs_done, seen.upto(probs_done))
                    act.activation(probs_turned[h % 2][:].rearrange("p t n -> p (t n)"), psum[:, 2 + h % 2, :],
                                   ACT.Copy).then_inc(probs_copied, 1)

                for s in range(HEADS + 1):
                    if s < HEADS:
                        exps(s)
                    if 0 <= s - 1 < HEADS:
                        copy_probs(s - 1)

            def l1_gnn():
                edge_layer(0)
                edge_layer(1)

            def l1_ffn():
                self_attention()
                experts(1)

            def l2_gnn():
                edge_layer(2)
                edge_layer(3)

            def l3_gnn():
                take_root(T)
                take_root(T)
                copy_turned(cols)

            def l3_ffn():
                take_root(T)
                take_root(T)
                take_root(SLOTS)
                copy_turned(cols)
                for target in (mixing[:], dispatch[:]):
                    act.wait_ge(exp_asked, seen.upto(exp_asked))
                    act.activation(target, target, ACT.Exp).then_inc(exp_ready, 1)
                act.wait_ge(slot_pre, seen.upto(slot_pre))
                act.activation(slot_hidden[:], slot_hidden[:], ACT.Gelu).then_inc(slot_act, 1)

            for stage in (l0_gnn, lambda: experts(0), l1_gnn, l1_ffn, l2_gnn, lambda: experts(2), l3_gnn,
                          l3_ffn):
                stage()

        @block.vector
        def _(dve):
            seen = Counts()

            def ask_root(n, p=P):
                dve.sem_inc(root_asked, 1)
                dve.wait_ge(root_ready, seen.upto(root_ready))

            def layernorm(target):
                for t in range(T):
                    for h in range(2):
                        dve.bn_stats(stats[:, t, h, :], x[:, t, h * HALF:(h + 1) * HALF]).then_inc(vector_wrote, 1)
                        dve.wait_ge(vector_wrote, seen.upto(vector_wrote))
                for t in range(T):
                    dve.bn_aggr(moments[:, t, :], stats[:, t, :, :].rearrange("p a b -> p (a b)"))\
                        .then_inc(vector_wrote, 1)
                    dve.wait_ge(vector_wrote, seen.upto(vector_wrote))
                dve.tensor_scalar(root[:, 0:T], moments[:, :, 1], 1e-5, None, ALU.add).then_inc(root_asked, 1)
                dve.wait_ge(root_ready, seen.upto(root_ready))
                dve.reciprocal(inverse[:], root[:, 0:T]).then_inc(vector_wrote, 1)
                dve.wait_ge(vector_wrote, seen.upto(vector_wrote))
                for t in range(T):
                    ins = dve.tensor_scalar(target[:, t, 0:D], x[:, t, :], moments[:, t, 0:1], inverse[:, t:t + 1],
                                            ALU.subtract, ALU.mult)
                return ins

            def count_edges():
                dve.wait_ge(edges_landed, seen.upto(edges_landed, 16))
                for n, target in ((0, edge_src), (1, edge_dst), (2, edge_key)):
                    dve.tensor_copy(target[:], edge_ints[:, n, :]).then_inc(vector_wrote, 1)
                    dve.wait_ge(vector_wrote, seen.upto(vector_wrote))
                dve.scalar_tensor_tensor(edge_key[:], edge_key[:], float(N), edge_dst[:], ALU.mult, ALU.add)\
                    .then_inc(vector_wrote, 1)
                dve.wait_ge(vector_wrote, seen.upto(vector_wrote))

                def hots(c, q):
                    dve.tensor_scalar(src_hot[q][:], key_iota[:, 0:N], edge_src[:, bass.ds(c, 1)], None, ALU.is_equal)
                    dve.tensor_scalar(key_hot[q][:], key_iota[:], edge_key[:, bass.ds(c, 1)], None, ALU.is_equal)\
                        .then_inc(hot_ready, 1)

                hots(0, 0)
                hots(1, 1)
                with seen.loop(dve, EDGE_TILES // 2 - 1, {hot_used: 2}) as i:
                    for q in range(2):
                        dve.wait_ge(hot_used, seen.upto(hot_used))
                        hots(i * 2 + (2 + q), q)
                seen.upto(hot_used, 2)
                dve.wait_ge(counted, seen.upto(counted))
                for t in range(T):
                    for j, c, n in row_parts(REL * N):
                        ins = dve.tensor_copy(raw_counts[:, t, c:c + n], row_bank(t, j, n))
                ins.then_inc(vector_wrote, 1)
                dve.wait_ge(vector_wrote, seen.upto(vector_wrote))
                dve.sem_inc(raw_ready, 1)
                for t in range(T):
                    dve.tensor_tensor(loop_counts[:, t, :], raw_counts[:, t, 0:N], raw_counts[:, t, N:2 * N],
                                      ALU.add).then_inc(vector_wrote, 1)
                    dve.wait_ge(vector_wrote, seen.upto(vector_wrote))
                    dve.tensor_tensor(loop_counts[:, t, :], loop_counts[:, t, :], raw_counts[:, t, 2 * N:3 * N],
                                      ALU.add).then_inc(vector_wrote, 1)
                    dve.wait_ge(vector_wrote, seen.upto(vector_wrote))
                    dve.tensor_tensor(loop_counts[:, t, node_tile(t)], loop_counts[:, t, node_tile(t)], ident[:],
                                      ALU.add).then_inc(vector_wrote, 1)
                    dve.wait_ge(vector_wrote, seen.upto(vector_wrote))
                dve.wait_ge(degree_done, seen.upto(degree_done))
                for j, c, n in row_parts(REL * N):
                    dve.tensor_scalar(in_degree[:, c:c + n], row_bank(0, j, n), 1.0, None, ALU.max)\
                        .then_inc(vector_wrote, 1)
                    dve.wait_ge(vector_wrote, seen.upto(vector_wrote))
                dve.reciprocal(in_degree[:], in_degree[:]).then_inc(vector_wrote, 1)
                dve.wait_ge(vector_wrote, seen.upto(vector_wrote))
                for t in range(T):
                    dve.tensor_tensor(mean_counts[:, t, :], raw_counts[:, t, :], in_degree[:], ALU.mult)\
                        .then_inc(vector_wrote, 1)
                    dve.wait_ge(vector_wrote, seen.upto(vector_wrote))
                dve.wait_ge(counts_turned, seen.upto(counts_turned))
                for b in range(3):
                    ins = dve.tensor_copy(flat_counts[:, 512 * b:512 * b + 512], psum[:, b, :])
                ins.then_inc(vector_wrote, 1)
                dve.wait_ge(vector_wrote, seen.upto(vector_wrote))
                dve.sem_inc(counts_ready, 1)

            def l0_gnn():
                dve.memset(tiny[:], 0.0).then_inc(vector_wrote, 1)
                dve.wait_ge(vector_wrote, seen.upto(vector_wrote))
                dve.memset(ones[:], 1.0).then_inc(ones_ready, 1)
                dve.wait_ge(constants_ready, seen.upto(constants_ready, 3))
                dve.wait_ge(small_landed, seen.upto(small_landed, 16))
                count_edges()
                dve.wait_ge(x_landed, seen.upto(x_landed, 16))
                layernorm(rows).then_inc(rows_ready, 1)
                dve.wait_ge(query_landed, seen.upto(query_landed, 16))
                for layer in range(2):
                    dve.wait_ge(rows_done, seen.upto(rows_done))
                    dve.wait_ge(bias_landed, seen.upto(bias_landed, 16))
                    for t in range(T):
                        for j, c, n in row_parts(D):
                            ins = dve.tensor_tensor(rows[:, t, c:c + n], row_bank(t, j, n), bias[:, c:c + n], ALU.add)
                    ins.then_inc(vector_wrote, 1)
                    dve.wait_ge(vector_wrote, seen.upto(vector_wrote))
                    dve.sem_inc(bias_used, 1)
                    dve.sem_inc(rows_ready, 1)

                    def weigh(c, q):
                        dve.wait_ge(chunk_squashed, seen.upto(chunk_squashed))
                        by_query = query_cols[:].rearrange("p k q -> p (k q)")[:, bass.ds(c * L, L)]\
                            .unsqueeze(1).broadcast_to([P, GROUP, L])
                        dve.tensor_tensor(chunk[q][:], chunk[q][:], by_query, ALU.mult).then_inc(chunk_weighted, 1)

                    def reduce(c, q):
                        dve.wait_ge(chunk_folded, seen.upto(chunk_folded))
                        dve.tensor_reduce(flat_gate[:, bass.ds(c * GROUP, GROUP)],
                                          psum[:, 5 + q, :].rearrange("p (n l) -> p n l", n=GROUP), AX_X, ALU.add)\
                            .then_inc(chunk_reduced, 1)

                    weigh(0, 0)
                    with seen.loop(dve, CHUNKS // CHUNK_RING - 1, {chunk_squashed: CHUNK_RING, chunk_folded: CHUNK_RING}) as i:
                        for q in range(CHUNK_RING):
                            weigh(i * CHUNK_RING + (q + 1), (q + 1) % CHUNK_RING)
                            reduce(i * CHUNK_RING + q, q)
                    for c in range(CHUNKS - 2, CHUNKS):
                        weigh(c, c % CHUNK_RING)
                        reduce(c - 1, (c - 1) % CHUNK_RING)
                    reduce(CHUNKS - 1, (CHUNKS - 1) % CHUNK_RING)
                    dve.wait_ge(tanh_ready, seen.upto(tanh_ready))
                    dve.tensor_tensor(flat_hidden, flat_hidden, flat_cols, ALU.subtract).then_inc(vector_wrote, 1)
                    dve.wait_ge(vector_wrote, seen.upto(vector_wrote))
                    dve.wait_ge(alpha_ready, seen.upto(alpha_ready, 6))
                    dve.tensor_tensor(flat_hidden, flat_hidden, alpha[:].rearrange("p k n -> p (k n)"), ALU.mult)\
                        .then_inc(vector_wrote, 1)
                    dve.wait_ge(vector_wrote, seen.upto(vector_wrote))
                    dve.tensor_tensor(flat_hidden, flat_hidden, flat_cols, ALU.add).then_inc(vector_wrote, 1)
                    dve.wait_ge(vector_wrote, seen.upto(vector_wrote))
                    dve.sem_inc(hidden_ready, 1)
                dve.wait_ge(turned_back, seen.upto(turned_back, 6))
                for b in range(3):
                    ins = dve.tensor_tensor(flat_x[:, 512 * b:512 * b + 512], flat_x[:, 512 * b:512 * b + 512],
                                            psum[:, b, :], ALU.add)
                ins.then_inc(vector_wrote, 1)
                dve.wait_ge(vector_wrote, seen.upto(vector_wrote))
                dve.sem_inc(arena_free, 1)

            def route(layer):
                count = EXPERTS[layer]
                scores = logits[:, :, 0:count]
                dve.wait_ge(logits_done, seen.upto(logits_done))
                of = psum[:, 6, 0:32].rearrange("p (t e) -> p t e", t=T)[:, :, 0:count]
                if layer == 0:
                    dve.tensor_tensor(scores, of, small_at("br", 0, 8).unsqueeze(1).broadcast_to([P, T, 8]),
                                      ALU.add).then_inc(vector_wrote, 1)
                    dve.wait_ge(vector_wrote, seen.upto(vector_wrote))
                    dve.sem_inc(logits_taken, 1)
                else:
                    dve.tensor_copy(scores, of).then_inc(vector_wrote, 1)
                    dve.wait_ge(vector_wrote, seen.upto(vector_wrote))
                    dve.sem_inc(logits_taken, 1)
                    dve.tensor_reduce(row_max[:], scores, AX_X, ALU.max).then_inc(vector_wrote, 1)
                    dve.wait_ge(vector_wrote, seen.upto(vector_wrote))
                    for t in range(T):
                        ins = dve.tensor_scalar(logits[:, t, 0:count], logits[:, t, 0:count], row_max[:, t:t + 1],
                                                None, ALU.subtract)
                    ins.then_inc(exp_asked, 1)
                    dve.wait_ge(exp_ready, seen.upto(exp_ready))
                    dve.tensor_reduce(row_sum[:], scores, AX_X, ALU.add).then_inc(vector_wrote, 1)
                    dve.wait_ge(vector_wrote, seen.upto(vector_wrote))
                    dve.reciprocal(row_sum[:], row_sum[:]).then_inc(vector_wrote, 1)
                    dve.wait_ge(vector_wrote, seen.upto(vector_wrote))
                    for t in range(T):
                        dve.tensor_scalar(logits[:, t, 0:count], logits[:, t, 0:count], row_sum[:, t:t + 1],
                                          None, ALU.mult).then_inc(vector_wrote, 1)
                        dve.wait_ge(vector_wrote, seen.upto(vector_wrote))
                for t in range(T):
                    dve.max(top[:, t, :], logits[:, t, 0:count]).then_inc(vector_wrote, 1)
                    dve.wait_ge(vector_wrote, seen.upto(vector_wrote))
                    dve.max_index(top_at[:, t, :], top[:, t, :], logits[:, t, 0:count]).then_inc(vector_wrote, 1)
                    dve.wait_ge(vector_wrote, seen.upto(vector_wrote))
                dve.tensor_copy(top_place[:], top_at[:]).then_inc(vector_wrote, 1)
                dve.wait_ge(vector_wrote, seen.upto(vector_wrote))
                if layer == 0:
                    dve.tensor_tensor(gap[:], top[:, :, 1], top[:, :, 0], ALU.subtract).then_inc(exp_asked, 1)
                    dve.wait_ge(exp_ready, seen.upto(exp_ready))
                    dve.tensor_scalar(row_sum[:], gap[:], 1.0, None, ALU.add).then_inc(vector_wrote, 1)
                    dve.wait_ge(vector_wrote, seen.upto(vector_wrote))
                    dve.reciprocal(top_weight[:, :, 0], row_sum[:]).then_inc(vector_wrote, 1)
                    dve.wait_ge(vector_wrote, seen.upto(vector_wrote))
                    dve.tensor_tensor(top_weight[:, :, 1], gap[:], top_weight[:, :, 0], ALU.mult)\
                        .then_inc(vector_wrote, 1)
                    dve.wait_ge(vector_wrote, seen.upto(vector_wrote))
                else:
                    dve.tensor_tensor(row_sum[:], top[:, :, 0], top[:, :, 1], ALU.add).then_inc(vector_wrote, 1)
                    dve.wait_ge(vector_wrote, seen.upto(vector_wrote))
                    dve.tensor_scalar(row_sum[:], row_sum[:], 1e-20 if layer == 1 else 1e-8, None, ALU.add)\
                        .then_inc(vector_wrote, 1)
                    dve.wait_ge(vector_wrote, seen.upto(vector_wrote))
                    dve.reciprocal(row_sum[:], row_sum[:]).then_inc(vector_wrote, 1)
                    dve.wait_ge(vector_wrote, seen.upto(vector_wrote))
                    for n in range(2):
                        dve.tensor_tensor(top_weight[:, :, n], top[:, :, n], row_sum[:], ALU.mult)\
                            .then_inc(vector_wrote, 1)
                        dve.wait_ge(vector_wrote, seen.upto(vector_wrote))
                for t in range(T):
                    for n, target in ((0, combine), (1, second)):
                        dve.tensor_scalar(target[:, t, 0:count], iota[:, 0:count], top_place[:, t, n:n + 1],
                                          top_weight[:, t, n:n + 1], ALU.is_equal, ALU.mult).then_inc(vector_wrote, 1)
                        dve.wait_ge(vector_wrote, seen.upto(vector_wrote))
                dve.tensor_tensor(combine[:, :, 0:count], combine[:, :, 0:count], second[:, :, 0:count], ALU.add)\
                    .then_inc(vector_wrote, 1)
                dve.wait_ge(vector_wrote, seen.upto(vector_wrote))
                if layer == 0:
                    pairs = unit_weight[:, :, 0:16].rearrange("p t (e h) -> p t e h", h=2)
                    for h in range(2):
                        dve.tensor_copy(pairs[:, :, :, h], combine[:, :, 0:8]).then_inc(vector_wrote, 1)
                        dve.wait_ge(vector_wrote, seen.upto(vector_wrote))
                    dve.sem_inc(combine_ready, 1)
                else:
                    dve.tensor_copy(unit_weight[:, :, 0:count], combine[:, :, 0:count]).then_inc(vector_wrote, 1)
                    dve.wait_ge(vector_wrote, seen.upto(vector_wrote))
                    dve.memset(unit_weight[:, :, count:count + 2], 1.0 if layer == 1 else 0.5)\
                        .then_inc(vector_wrote, 1)
                    dve.wait_ge(vector_wrote, seen.upto(vector_wrote))

            def experts(layer):
                if layer != 1:
                    layernorm(rows).then_inc(vector_wrote, 1)
                    dve.wait_ge(vector_wrote, seen.upto(vector_wrote))
                    dve.sem_inc(rows_ready, 1)
                route(layer)
                if layer == 0:
                    dve.wait_ge(combine_turned, seen.upto(combine_turned))
                    dve.tensor_copy(combine_cols[0:8, :], psum[0:8, 6, 64:64 + N]).then_inc(vector_wrote, 1)
                    dve.wait_ge(vector_wrote, seen.upto(vector_wrote))
                    dve.sem_inc(combine_cols_ready, 1)
                    dve.wait_ge(down_done, seen.upto(down_done))
                    for t in range(T):
                        for j, c, n in row_parts(D):
                            ins = dve.tensor_tensor(x[:, t, c:c + n], x[:, t, c:c + n], row_bank(t, j, n), ALU.add)
                    ins.then_inc(vector_wrote, 1)
                    dve.wait_ge(vector_wrote, seen.upto(vector_wrote))
                    dve.sem_inc(down_taken, 1)

                def unit(u):
                    if layer == 0:
                        for f in range(3):
                            if f != 1:
                                dve.wait_ge(gate_done, seen.upto(gate_done))
                            ins = dve.tensor_scalar(gate_part[:, f, :], unit_tile(0, f),
                                                    small[:, bass.ds(u * 6 + (SMALL["unit_bias"][0] + f), 1)], 7.0,
                                                    ALU.add, ALU.min)
                            if f > 0:
                                ins.then_inc(gate_clipped, 1)
                        for tiles in ((0, 1), (2,)):
                            of = slice(tiles[0], tiles[-1] + 1)
                            dve.wait_ge(up_done, seen.upto(up_done))
                            for f in tiles:
                                ins = dve.tensor_scalar(up_part[:, f, :], unit_tile(1, f),
                                                        small[:, bass.ds(u * 6 + (SMALL["unit_bias"][0] + 3 + f), 1)],
                                                        7.0, ALU.add, ALU.min)
                            ins.then_inc(vector_wrote, 1)
                            dve.wait_ge(vector_wrote, seen.upto(vector_wrote))
                            dve.tensor_scalar(up_part[:, of, :], up_part[:, of, :], -7.0, 1.0, ALU.max, ALU.add)
                            dve.wait_ge(squashed, seen.upto(squashed))
                            dve.tensor_tensor(gate_part[:, of, :], gate_part[:, of, :], squash[:, of, :],
                                              ALU.mult).then_inc(vector_wrote, 1)
                            dve.wait_ge(vector_wrote, seen.upto(vector_wrote))
                            dve.tensor_tensor(act_cols[:, of, :], gate_part[:, of, :], up_part[:, of, :], ALU.mult)\
                                .then_inc(act_ready, 1)
                    else:
                        for last, tiles in ((0, slice(0, 2)), (1, slice(2, 3))):
                            dve.wait_ge(squashed, seen.upto(squashed))
                            dve.wait_ge(up_done, seen.upto(up_done))
                            dve.tensor_tensor(act_cols[:, tiles, :].rearrange("p f n -> p (f n)"),
                                              squash[:, tiles, :].rearrange("p f n -> p (f n)"), unit_bank(1, last),
                                              ALU.mult).then_inc(act_ready, 1)
                    dve.wait_ge(down_done, seen.upto(down_done))
                    for t in range(T):
                        for j, c, n in row_parts(D):
                            ins = dve.scalar_tensor_tensor(x[:, t, c:c + n], row_bank(t, j, n),
                                                           unit_weight[:, t, bass.ds(u, 1)], x[:, t, c:c + n],
                                                           ALU.mult, ALU.add)
                    ins.then_inc(vector_wrote, 1)
                    dve.wait_ge(vector_wrote, seen.upto(vector_wrote))
                    dve.sem_inc(down_taken, 1)

                if layer == 0:
                    grows = {gate_done: 4, up_done: 4, squashed: 4, down_done: 2, vector_wrote: 2 * (2 * 2 + 1)}
                else:
                    grows = {squashed: 4, up_done: 4, down_done: 2, vector_wrote: 2}
                with seen.loop(dve, UNITS[layer] // 2, grows) as i:
                    for q in range(2):
                        unit(i * 2 + q)
                if layer == 2:
                    dve.sem_inc(arena_free, 1)

            def edge_layer(n):
                layer = EDGE_LAYERS[n]
                rel, heads, width = layer["rel"], layer["heads"], layer["width"]
                out_width = heads * width
                messages = message_rows(layer)
                if n == 0:
                    for t in range(T):
                        dve.tensor_tensor(all_counts[:, t, :], counts[:, t, 0, :], counts[:, t, 1, :], ALU.add)\
                            .then_inc(vector_wrote, 1)
                        dve.wait_ge(vector_wrote, seen.upto(vector_wrote))
                        dve.tensor_tensor(all_counts[:, t, :], all_counts[:, t, :], counts[:, t, 2, :], ALU.add)\
                            .then_inc(vector_wrote, 1)
                        dve.wait_ge(vector_wrote, seen.upto(vector_wrote))
                        dve.tensor_scalar(absent[:, t, 0:N], all_counts[:, t, :], 0.0, LOW, ALU.is_equal,
                                          ALU.mult).then_inc(vector_wrote, 1)
                        dve.wait_ge(vector_wrote, seen.upto(vector_wrote))
                        dve.tensor_reduce(dinv[:, t:t + 1], all_counts[:, t, :], AX_X, ALU.add)\
                            .then_inc(vector_wrote, 1)
                        dve.wait_ge(vector_wrote, seen.upto(vector_wrote))
                    dve.tensor_scalar(dinv[:], dinv[:], 1.0, None, ALU.add).then_inc(vector_wrote, 1)
                    dve.wait_ge(vector_wrote, seen.upto(vector_wrote))
                if n == 2:
                    for t in range(T):
                        dve.tensor_scalar(absent[:, t, :], counts[:, t].rearrange("p r n -> p (r n)"), 0.0, LOW,
                                          ALU.is_equal, ALU.mult).then_inc(vector_wrote, 1)
                        dve.wait_ge(vector_wrote, seen.upto(vector_wrote))
                if n % 2 == 0:
                    layernorm(rows).then_inc(vector_wrote, 1)
                    dve.wait_ge(vector_wrote, seen.upto(vector_wrote))
                    dve.sem_inc(rows_ready, 1)
                for r in range(rel):
                    dve.wait_ge(rows_done, seen.upto(rows_done))
                    for t in range(T):
                        for j, c, size in row_parts(out_width):
                            ins = dve.tensor_copy(messages[:, r, t, c:c + size], row_bank(t, j, size))
                    ins.then_inc(vector_wrote, 1)
                    dve.wait_ge(vector_wrote, seen.upto(vector_wrote))
                    dve.sem_inc(rows_ready, 1)
                dve.wait_ge(query_keys_done, seen.upto(query_keys_done))
                dve.tensor_copy(queries_keys[:, :, 0:rel, 0:2 * heads],
                                psum[:, 7, 0:T * rel * 16].rearrange("p (t r c) -> p t r c", t=T, r=rel)
                                [:, :, :, 0:2 * heads]).then_inc(vector_wrote, 1)
                dve.wait_ge(vector_wrote, seen.upto(vector_wrote))
                for t in range(T):
                    dve.tensor_copy(keys[:, t, 0:rel * heads].rearrange("p (r h) -> p r h", r=rel),
                                    queries_keys[:, t, 0:rel, heads:2 * heads]).then_inc(vector_wrote, 1)
                    dve.wait_ge(vector_wrote, seen.upto(vector_wrote))
                dve.sem_inc(keys_ready, 1)
                dve.wait_ge(bias_landed, seen.upto(bias_landed, 16))
                target = wide_rows if n == 0 else rows
                items = [(t, h) for h in range(heads) for t in range(T)]

                def highest(i):
                    t, h = items[i]
                    scores = edge_scores[i % 2][:, 0:rel * N]
                    dve.wait_ge(lifted, seen.upto(lifted))
                    dve.scalar_tensor_tensor(scores, scores, 0.2, scores, ALU.mult, ALU.max).then_inc(vector_wrote, 1)
                    dve.wait_ge(vector_wrote, seen.upto(vector_wrote))
                    dve.tensor_tensor_reduce(scores, scores, absent[:, t, 0:rel * N], 1.0, -3e38, ALU.add,
                                             ALU.max, edge_max[:, i % 2:i % 2 + 1]).then_inc(vector_wrote, 1)
                    dve.wait_ge(vector_wrote, seen.upto(vector_wrote))
                    dve.tensor_scalar(edge_negmax[:, i % 2:i % 2 + 1], edge_max[:, i % 2:i % 2 + 1], -1.0, None,
                                      ALU.mult).then_inc(edge_max_ready, 1)

                def weigh(i):
                    t, h = items[i]
                    by = all_counts[:, t, :] if rel == 1 else counts[:, t].rearrange("p r n -> p (r n)")
                    q = i % 4
                    dve.wait_ge(edge_exp_ready, seen.upto(edge_exp_ready))
                    dve.tensor_tensor_reduce(edge_exp[i % 2][:, 0:rel * N], edge_exp[i % 2][:, 0:rel * N], by,
                                             1.0, 0.0, ALU.mult, ALU.add, edge_sum[:, q:q + 1])\
                        .then_inc(vector_wrote, 1)
                    dve.wait_ge(vector_wrote, seen.upto(vector_wrote))
                    dve.sem_inc(edge_weighted, 1)
                    dve.tensor_scalar(edge_sum[:, q:q + 1], edge_sum[:, q:q + 1], 1e-16, None, ALU.add)\
                        .then_inc(vector_wrote, 1)
                    dve.wait_ge(vector_wrote, seen.upto(vector_wrote))
                    dve.reciprocal(edge_inverse[:, q:q + 1], edge_sum[:, q:q + 1]).then_inc(vector_wrote, 1)
                    dve.wait_ge(vector_wrote, seen.upto(vector_wrote))

                def store(i):
                    t, h = items[i]
                    q = i % 4
                    dve.wait_ge(mixed, seen.upto(mixed))
                    for j, c, size in row_parts(width):
                        bank = 6 + j if width > 512 else 6 + i % 2
                        at = h * width + c
                        ins = dve.scalar_tensor_tensor(target[:, t, at:at + size], psum[:, bank, 0:size],
                                                       edge_inverse[:, q:q + 1], bias[:, at:at + size], ALU.mult,
                                                       ALU.add)
                    ins.then_inc(vector_wrote, 1)
                    dve.wait_ge(vector_wrote, seen.upto(vector_wrote))
                    dve.sem_inc(stored, 1)

                last = len(items)
                for s in range(last + 3):
                    if s < last:
                        highest(s)
                    if 0 <= s - 1 < last:
                        weigh(s - 1)
                    if 0 <= s - 3 < last:
                        store(s - 3)
                dve.sem_inc(bias_used, 1)
                if n == 0:
                    dve.sem_inc(rows_ready, 1)
                elif n == 2:
                    dve.tensor_scalar(wide_rows[:, :, 0:D], rows[:], 0.0, None, ALU.min).then_inc(exp_asked, 1)
                    dve.tensor_scalar(rows[:], rows[:], 0.0, None, ALU.max).then_inc(vector_wrote, 1)
                    dve.wait_ge(vector_wrote, seen.upto(vector_wrote))
                    dve.wait_ge(exp_ready, seen.upto(exp_ready))
                    dve.scalar_tensor_tensor(rows[:], wide_rows[:, :, 0:D], -1.0, rows[:], ALU.add, ALU.add)\
                        .then_inc(vector_wrote, 1)
                    dve.wait_ge(vector_wrote, seen.upto(vector_wrote))
                    dve.sem_inc(rows_ready, 1)
                else:
                    dve.tensor_tensor(x[:], x[:], rows[:], ALU.add).then_inc(vector_wrote, 1)
                    dve.wait_ge(vector_wrote, seen.upto(vector_wrote))

            def rms_rows(target, source):
                for t in range(T):
                    dve.tensor_tensor_reduce(normed[:, t, :], source[:, t, :], source[:, t, :], 1.0, 0.0,
                                             ALU.mult, ALU.add, root[:, t:t + 1]).then_inc(vector_wrote, 1)
                    dve.wait_ge(vector_wrote, seen.upto(vector_wrote))
                dve.tensor_scalar(root[:, 0:T], root[:, 0:T], 1.0 / D, 1e-6, ALU.mult, ALU.add)\
                    .then_inc(root_asked, 1)
                dve.wait_ge(root_ready, seen.upto(root_ready))
                dve.reciprocal(inverse[:], root[:, 0:T]).then_inc(vector_wrote, 1)
                dve.wait_ge(vector_wrote, seen.upto(vector_wrote))
                for t in range(T):
                    dve.tensor_scalar(target[:, t, :], source[:, t, :], inverse[:, t:t + 1], None, ALU.mult)\
                        .then_inc(vector_wrote, 1)
                    dve.wait_ge(vector_wrote, seen.upto(vector_wrote))
                dve.sem_inc(rows_ready, 1)

            def self_attention():
                layernorm(rows).then_inc(vector_wrote, 1)
                dve.wait_ge(vector_wrote, seen.upto(vector_wrote))
                rms_rows(normed, rows)
                dve.wait_ge(rows_done, seen.upto(rows_done))
                for t in range(T):
                    for j, c, n in row_parts(D):
                        ins = dve.tensor_copy(values[:, t, c:c + n], row_bank(t, j, n))
                ins.then_inc(vector_wrote, 1)
                dve.wait_ge(vector_wrote, seen.upto(vector_wrote))
                dve.sem_inc(rows_ready, 1)

                def highest(h):
                    q = h % 2
                    dve.wait_ge(scored, seen.upto(scored))
                    dve.tensor_reduce(head_max[:, q, :], psum[:, q, :].rearrange("p (t n) -> p t n", t=T), AX_X,
                                      ALU.max).then_inc(vector_wrote, 1)
                    dve.wait_ge(vector_wrote, seen.upto(vector_wrote))
                    dve.tensor_scalar(head_negmax[:, q, :], head_max[:, q, :], -HEAD ** -0.5, None, ALU.mult)\
                        .then_inc(head_max_ready, 1)

                def normalise(h):
                    q = h % 2
                    dve.wait_ge(probs_exp, seen.upto(probs_exp))
                    dve.reciprocal(head_inverse[:, q, :], head_sum[:, q, :]).then_inc(vector_wrote, 1)
                    dve.wait_ge(vector_wrote, seen.upto(vector_wrote))
                    for t in range(T):
                        ins = dve.tensor_scalar(probs[q][:, t, :], probs[q][:, t, :], head_inverse[:, q, t:t + 1],
                                                None, ALU.mult)
                    ins.then_inc(probs_ready, 1)

                def store(h):
                    at = h % 2 * HEAD
                    dve.wait_ge(context_done, seen.upto(context_done))
                    dve.tensor_copy(context[at:at + HEAD, h // 2, :], psum[at:at + HEAD, 4 + h % 2, 0:N])\
                        .then_inc(vector_wrote, 1)
                    dve.wait_ge(vector_wrote, seen.upto(vector_wrote))
                    dve.sem_inc(context_ready, 1)

                for s in range(HEADS + 2):
                    if s < HEADS:
                        highest(s)
                    if 0 <= s - 1 < HEADS:
                        normalise(s - 1)
                    if 0 <= s - 2 < HEADS:
                        store(s - 2)
                dve.wait_ge(rows_done, seen.upto(rows_done))
                for t in range(T):
                    for j, c, n in row_parts(D):
                        ins = dve.tensor_tensor(rows[:, t, c:c + n], rows[:, t, c:c + n], row_bank(t, j, n), ALU.add)
                ins.then_inc(vector_wrote, 1)
                dve.wait_ge(vector_wrote, seen.upto(vector_wrote))
                dve.tensor_tensor(x[:], x[:], rows[:], ALU.add).then_inc(vector_wrote, 1)
                dve.wait_ge(vector_wrote, seen.upto(vector_wrote))
                rms_rows(rows, rows)

            def l1_gnn():
                edge_layer(0)
                edge_layer(1)

            def l1_ffn():
                self_attention()
                experts(1)

            def l2_gnn():
                edge_layer(2)
                edge_layer(3)

            def l3_gnn():
                dve.tensor_copy(root[:, 0:T], dinv[:]).then_inc(vector_wrote, 1)
                dve.wait_ge(vector_wrote, seen.upto(vector_wrote))
                dve.sem_inc(root_asked, 1)
                dve.wait_ge(root_ready, seen.upto(root_ready))
                dve.reciprocal(dinv[:], root[:, 0:T]).then_inc(vector_wrote, 1)
                dve.wait_ge(vector_wrote, seen.upto(vector_wrote))
                layernorm(rows).then_inc(vector_wrote, 1)
                dve.wait_ge(vector_wrote, seen.upto(vector_wrote))
                dve.sem_inc(rows_ready, 1)
                dve.wait_ge(rows_done, seen.upto(rows_done))
                for t in range(T):
                    for j, c, n in row_parts(D):
                        ins = dve.tensor_scalar(rows[:, t, c:c + n], row_bank(t, j, n), dinv[:, t:t + 1], None,
                                                ALU.mult)
                ins.then_inc(vector_wrote, 1)
                dve.wait_ge(vector_wrote, seen.upto(vector_wrote))
                dve.sem_inc(rows_ready, 1)
                dve.wait_ge(rows_done, seen.upto(rows_done))
                dve.wait_ge(bias_landed, seen.upto(bias_landed, 16))
                for t in range(T):
                    for j, c, n in row_parts(D):
                        ins = dve.scalar_tensor_tensor(rows[:, t, c:c + n], row_bank(t, j, n), dinv[:, t:t + 1],
                                                       bias[:, c:c + n], ALU.mult, ALU.add)
                ins.then_inc(vector_wrote, 1)
                dve.wait_ge(vector_wrote, seen.upto(vector_wrote))
                dve.sem_inc(bias_used, 1)
                dve.tensor_tensor(x[:], x[:], rows[:], ALU.add).then_inc(vector_wrote, 1)
                dve.wait_ge(vector_wrote, seen.upto(vector_wrote))

            def l3_ffn():
                layernorm(rows).then_inc(vector_wrote, 1)
                dve.wait_ge(vector_wrote, seen.upto(vector_wrote))
                for t in range(T):
                    dve.tensor_tensor_reduce(squares[:], rows[:, t, :], rows[:, t, :], 1.0, 0.0, ALU.mult,
                                             ALU.add, root[:, t:t + 1]).then_inc(vector_wrote, 1)
                    dve.wait_ge(vector_wrote, seen.upto(vector_wrote))
                dve.sem_inc(root_asked, 1)
                dve.wait_ge(root_ready, seen.upto(root_ready))
                dve.tensor_scalar(root[:, 0:T], root[:, 0:T], 1e-12, None, ALU.max).then_inc(vector_wrote, 1)
                dve.wait_ge(vector_wrote, seen.upto(vector_wrote))
                dve.reciprocal(inverse[:], root[:, 0:T]).then_inc(vector_wrote, 1)
                dve.wait_ge(vector_wrote, seen.upto(vector_wrote))
                for t in range(T):
                    dve.tensor_scalar(rows[:, t, :], rows[:, t, :], inverse[:, t:t + 1], None, ALU.mult)\
                        .then_inc(vector_wrote, 1)
                    dve.wait_ge(vector_wrote, seen.upto(vector_wrote))
                dve.sem_inc(rows_ready, 1)
                dve.wait_ge(slots_landed, seen.upto(slots_landed, 48))
                dve.tensor_tensor(phi_squares[:], phi[:], phi[:], ALU.mult).then_inc(vector_wrote, 1)
                dve.wait_ge(vector_wrote, seen.upto(vector_wrote))
                dve.sem_inc(phi_squared, 1)
                dve.wait_ge(phi_summed, seen.upto(phi_summed))
                dve.tensor_copy(root[:], psum[:, 7, 0:SLOTS]).then_inc(root_asked, 1)
                dve.wait_ge(root_ready, seen.upto(root_ready))
                dve.tensor_scalar(phi_scale[:], root[:], 1e-12, None, ALU.max).then_inc(vector_wrote, 1)
                dve.wait_ge(vector_wrote, seen.upto(vector_wrote))
                dve.reciprocal(phi_scale[:], phi_scale[:]).then_inc(vector_wrote, 1)
                dve.wait_ge(vector_wrote, seen.upto(vector_wrote))
                dve.tensor_scalar(phi_scale[:], phi_scale[:], small_at("scale"), None, ALU.mult)\
                    .then_inc(vector_wrote, 1)
                dve.wait_ge(vector_wrote, seen.upto(vector_wrote))
                dve.tensor_tensor(phi[:], phi[:], phi_scale[:].unsqueeze(1).broadcast_to([P, K, SLOTS]),
                                  ALU.mult).then_inc(vector_wrote, 1)
                dve.wait_ge(vector_wrote, seen.upto(vector_wrote))
                dve.sem_inc(phi_ready, 1)
                dve.wait_ge(slot_logits_done, seen.upto(slot_logits_done))
                dve.tensor_reduce(soft[:, 0:2], psum[:, 3, 0:T * SLOTS].rearrange("p (t n) -> p t n", t=T), AX_X,
                                  ALU.max).then_inc(vector_wrote, 1)
                dve.wait_ge(vector_wrote, seen.upto(vector_wrote))
                for t in range(T):
                    ins = dve.tensor_scalar(mixing[:, t, :], psum[:, 3, t * SLOTS:(t + 1) * SLOTS], soft[:, t:t + 1],
                                            None, ALU.subtract)
                ins.then_inc(vector_wrote, 1)
                dve.wait_ge(vector_wrote, seen.upto(vector_wrote))
                dve.sem_inc(exp_asked, 1)
                dve.tensor_reduce(soft[0:SLOTS, 2:3], psum[0:SLOTS, 4, 0:N], AX_X, ALU.max).then_inc(vector_wrote, 1)
                dve.wait_ge(vector_wrote, seen.upto(vector_wrote))
                dve.tensor_scalar(dispatch[:], psum[0:SLOTS, 4, 0:N], soft[0:SLOTS, 2:3], None, ALU.subtract)\
                    .then_inc(exp_asked, 1)
                dve.wait_ge(exp_ready, seen.upto(exp_ready))
                dve.tensor_reduce(soft[:, 4:6], mixing[:], AX_X, ALU.add).then_inc(vector_wrote, 1)
                dve.wait_ge(vector_wrote, seen.upto(vector_wrote))
                dve.reciprocal(soft[:, 4:6], soft[:, 4:6]).then_inc(vector_wrote, 1)
                dve.wait_ge(vector_wrote, seen.upto(vector_wrote))
                for t in range(T):
                    dve.tensor_scalar(mixing[:, t, :], mixing[:, t, :], soft[:, 4 + t:5 + t], None, ALU.mult)\
                        .then_inc(vector_wrote, 1)
                    dve.wait_ge(vector_wrote, seen.upto(vector_wrote))
                dve.wait_ge(exp_ready, seen.upto(exp_ready))
                dve.tensor_reduce(soft[0:SLOTS, 6:7], dispatch[:], AX_X, ALU.add).then_inc(vector_wrote, 1)
                dve.wait_ge(vector_wrote, seen.upto(vector_wrote))
                dve.reciprocal(soft[0:SLOTS, 6:7], soft[0:SLOTS, 6:7]).then_inc(vector_wrote, 1)
                dve.wait_ge(vector_wrote, seen.upto(vector_wrote))
                dve.tensor_scalar(dispatch[:], dispatch[:], soft[0:SLOTS, 6:7], None, ALU.mult)\
                    .then_inc(soft_ready, 1)
                dve.wait_ge(soft_turned, seen.upto(soft_turned))
                dve.tensor_copy(mixing_cols[:], psum[0:SLOTS, 5, 0:N])
                dve.tensor_copy(dispatch_rows[:].rearrange("p t n -> p (t n)"), psum[:, 6, 0:T * SLOTS])\
                    .then_inc(soft_copied, 1)
                dve.wait_ge(slot_in_done, seen.upto(slot_in_done))
                dve.tensor_copy(slot_in[:].rearrange("p k n -> p (k n)"), psum[:, 7, 0:K * SLOTS])\
                    .then_inc(vector_wrote, 1)
                dve.wait_ge(vector_wrote, seen.upto(vector_wrote))

                def mask_slots(source, tiles):
                    def one(n, q):
                        dve.scalar_tensor_tensor(slot_mask[q][:, 0:tiles, :],
                                                 iota[:].unsqueeze(1).broadcast_to([P, tiles, SLOTS]),
                                                 iota[:, bass.ds(n, 1)], source[:], ALU.is_equal, ALU.mult)\
                            .then_inc(mask_ready, 1)

                    one(0, 0)
                    one(1, 1)
                    with seen.loop(dve, SLOTS // 2 - 1, {mask_used: 2}) as i:
                        for q in range(2):
                            dve.wait_ge(mask_used, seen.upto(mask_used))
                            one(i * 2 + (2 + q), q)
                    dve.wait_ge(mask_used, seen.upto(mask_used, 2))

                mask_slots(slot_in, K)
                dve.wait_ge(slot_hidden_done, seen.upto(slot_hidden_done))
                dve.tensor_tensor(slot_hidden[:], psum[0:SLOTS, 3, 0:SLOT_HIDDEN], slot_b1[:], ALU.add)\
                    .then_inc(slot_pre, 1)
                dve.wait_ge(slot_hidden_turned, seen.upto(slot_hidden_turned))
                dve.tensor_copy(slot_hidden_cols[:].rearrange("p k n -> p (k n)"), psum[:, 5, 0:3 * SLOTS])\
                    .then_inc(vector_wrote, 1)
                dve.wait_ge(vector_wrote, seen.upto(vector_wrote))
                mask_slots(slot_hidden_cols, 3)
                dve.wait_ge(slot_out_done, seen.upto(slot_out_done))
                for j, c, n in row_parts(D):
                    ins = dve.tensor_tensor(slot_out[:, c:c + n], psum[0:SLOTS, 3 + j, 0:n], slot_b2[:, c:c + n],
                                            ALU.add)
                ins.then_inc(vector_wrote, 1)
                dve.wait_ge(vector_wrote, seen.upto(vector_wrote))
                dve.sem_inc(slot_out_ready, 1)
                dve.wait_ge(rows_done, seen.upto(rows_done))
                for t in range(T):
                    for j, c, n in row_parts(D):
                        ins = dve.tensor_tensor(x[:, t, c:c + n], x[:, t, c:c + n], row_bank(t, j, n), ALU.add)
                ins.then_inc(vector_wrote, 1)
                dve.wait_ge(vector_wrote, seen.upto(vector_wrote))

            for stage in (l0_gnn, lambda: experts(0), l1_gnn, l1_ffn, l2_gnn, lambda: experts(2), l3_gnn,
                          l3_ffn):
                stage()
            dve.sem_inc(x_final, 1)



def _by_columns(w):
    w = w.reshape(K, P, D)
    return [w[:, :, h * HALF:(h + 1) * HALF].transpose(1, 0, 2).reshape(P, -1) for h in range(2)]


def _by_rows(w, pieces=((0, 3), (3, 6))):
    w = w.reshape(-1, P, w.shape[1])
    return [w[a:b].transpose(1, 0, 2).reshape(P, -1) for a, b in pieces]


def _unit(gate, up, down):
    return [gate.reshape(K, P, HALF).transpose(1, 0, 2).reshape(P, -1),
            up.reshape(K, P, HALF).transpose(1, 0, 2).reshape(P, -1)] + _by_rows(down, ((0, 3),))


def _stream(a):
    pieces = _by_columns(a["L0_gnn_Wg"][:, D:].T)
    for n in (1, 2):
        pieces += _by_rows(a[f"L0_gnn_W_root{n}"])
        for r in range(REL):
            pieces += _by_rows(a[f"L0_gnn_W_rel{n}"][r])
        pieces += _by_columns(a["L0_gnn_Wg"][:, :D].T)
        hidden, query = _by_columns(a["L0_gnn_Wq"][:, :D].T), _by_columns(a["L0_gnn_Wq"][:, D:].T)
        pieces += [hidden[0], query[0], hidden[1], query[1]]
    for e in range(8):
        for h in range(2):
            cut = slice(h * HALF, (h + 1) * HALF)
            pieces += _unit(a["L0_ffn_Wgu"][e][:, :D][:, cut], a["L0_ffn_Wgu"][e][:, D:][:, cut],
                            a["L0_ffn_Wd"][e][cut])
    pieces += _by_rows(a["L1_gnn_W1"].T, EDGE_LAYERS[0]["pieces"])
    pieces += _by_rows(a["L1_gnn_W2"].T, EDGE_LAYERS[1]["pieces"])
    pieces += _by_columns(a["L1_ffn_Wq"].T) + _by_columns(a["L1_ffn_Wk"].T)
    pieces += _by_rows(a["L1_ffn_Wv"].T) + _by_rows(a["L1_ffn_Wo"].T)
    for e in range(8):
        pieces += _unit(a["L1_ffn_Weg"][e].T, a["L1_ffn_Weu"][e].T, a["L1_ffn_Wed"][e].T)
    for h in range(2):
        cut = slice(h * HALF, (h + 1) * HALF)
        pieces += _unit(a["L1_ffn_Wsg"][cut].T, a["L1_ffn_Wsu"][cut].T, a["L1_ffn_Wsd"].T[cut])
    for n in (1, 2):
        for r in range(REL):
            pieces += _by_rows(a[f"L2_gnn_W{n}"][r])
    for e in range(16):
        pieces += _unit(a["L2_ffn_wg"][e], a["L2_ffn_wu"][e], a["L2_ffn_wd"][e])
    for e in range(2):
        pieces += _unit(a["L2_ffn_shared_wg"][e], a["L2_ffn_shared_wu"][e], a["L2_ffn_shared_wd"][e])
    pieces += _by_rows(a["L3_gnn_W"])
    for n in range(SLOTS):
        pieces += [a["L3_ffn_w1"][n].reshape(K, P, SLOT_HIDDEN).transpose(1, 0, 2).reshape(P, -1)]
    for n in range(SLOTS):
        pieces += _by_rows(a["L3_ffn_w2"][n], ((0, 3),))
    return pieces


def _small(a, np):
    def cols(v):
        return v.reshape(-1, P).T

    def tiled(m):
        return m.reshape(-1, P, m.shape[1]).transpose(1, 0, 2).reshape(P, -1)

    bgu = a["L0_ffn_bgu"].reshape(8, 2, 2, 3, P)
    att = np.zeros((8, P, 16), np.float32)
    for h in range(8):
        att[h, :, h] = a["L1_gnn_att_dst1"][h]
        att[h, :, 8 + h] = a["L1_gnn_att_src1"][h]
    parts = {
        "bg": cols(a["L0_gnn_bg"]), "bq": cols(a["L0_gnn_bq"]),
        "unit_bias": bgu.transpose(4, 0, 2, 1, 3).reshape(P, -1),
        "norm1": cols(a["L1_ffn_norm1_w"]), "norm2": cols(a["L1_ffn_norm2_w"]),
        "router0": tiled(a["L0_ffn_Wr"]), "router1": tiled(a["L1_ffn_gate_w"].T),
        "router2": tiled(a["L2_ffn_gate_w"].T),
        "br": np.broadcast_to(a["L0_ffn_br"], (P, 8)), "scale": np.broadcast_to(a["L3_ffn_scale"], (P, 1)),
        "att0": att.transpose(1, 0, 2).reshape(P, -1),
        "att1": tiled(np.stack([a["L1_gnn_att_dst2"][0], a["L1_gnn_att_src2"][0]], axis=1)),
        "att2": tiled(np.concatenate([a["L2_gnn_q1"], a["L2_gnn_k1"]], axis=1)),
        "att3": tiled(np.concatenate([a["L2_gnn_q2"], a["L2_gnn_k2"]], axis=1)),
    }
    assert all(parts[n].shape == (P, width) for n, (_, width) in SMALL.items())
    return np.concatenate([parts[n] for n in SMALL], axis=1)


def kernel(**inputs):
    import concourse.bacc as bacc
    import numpy as np
    from concourse.bass_utils import run_bass_kernel_spmd

    a = {name: np.asarray(value) for name, value in inputs.items()}
    pieces = _stream(a)
    assert len(pieces) == STREAM
    stream = np.zeros((STREAM, P, PIECE), np.float32)
    for n, piece in enumerate(pieces):
        stream[n, :, :piece.shape[1]] = piece
    edges = np.stack([a["src"], a["dst"], a["edge_type_3"]]).reshape(3, EDGE_TILES, P).transpose(2, 0, 1)
    query = a["L0_gnn_query_embs"].reshape(B * L, K, P).transpose(2, 1, 0)
    rows = [a[n] for n in ("L0_gnn_b1", "L0_gnn_b2", "L1_gnn_b1", "L1_gnn_b2", "L2_gnn_b1", "L2_gnn_b2", "L3_gnn_b")]
    arrays = {
        "x_in": a["x"], "edges": edges, "query": query, "small_in": _small(a, np),
        "bias_in": np.concatenate(rows)[None], "bd_in": a["L0_ffn_bd"],
        "phi_in": a["L3_ffn_phi"].reshape(K, P, SLOTS).transpose(1, 0, 2),
        "slot_b1_in": a["L3_ffn_b1"], "slot_b2_in": a["L3_ffn_b2"], "stream": stream,
    }
    arrays = {name: np.ascontiguousarray(value) for name, value in arrays.items()}
    nc = bacc.Bacc("TRN2", target_bir_lowering=False, num_devices=1)
    tensors = [nc.dram_tensor(name, v.shape, mybir.dt.from_np(v.dtype), kind="ExternalInput").ap()
               for name, v in arrays.items()]
    out = nc.dram_tensor("out", (N, D), F32, kind="ExternalOutput").ap()
    build(nc, *tensors, out)
    result = run_bass_kernel_spmd(nc, [arrays], core_ids=[0])
    return result.results[0]["out"]
```

```python
from contextlib import ExitStack, contextmanager

import concourse.bass as bass
from concourse import mybir

F32 = mybir.dt.float32
F32R = mybir.dt.float32r
BF16 = mybir.dt.bfloat16
I32 = mybir.dt.int32
U32 = mybir.dt.uint32
ALU = mybir.AluOpType
ACT = mybir.ActivationFunctionType
AX_X = mybir.AxisListType.X

P = 128
N = 256
T = N // P
D = 768
K = D // P
E = 4096
EDGE_TILES = E // P
REL = 3
B, L = 8, 64
GROUP = N // B
PIECE = 2304
RING = 9
HALF = 384
LOW = -1e30
HEADS, HEAD = 12, 64
SLOTS, SLOT_HIDDEN = 64, 384
CHUNKS = K * B
CHUNK_RING = 6
BIASED = 4
WHOLE = 4
GATE, UP, DOWN = range(3)

GATE_PIECES = 2 + 4
RGCN_PIECES = 8
L0_GNN_PIECES = 2 + 2 * (RGCN_PIECES + GATE_PIECES)
UNITS = (16, 10, 18)
EXPERTS = (8, 8, 16)
SLOT_PAIR = 2 * SLOTS
STREAM = (L0_GNN_PIECES + 3 * sum(UNITS) + 3 + 3 + 8 + 2 * REL * 2 + 2 + 2 * SLOTS)

SMALL = {}
_at = 0
for _name, _width in (("bg", K), ("bq", K), ("unit_bias", UNITS[0] * 6), ("norm1", K), ("norm2", K),
                      ("router0", K * 8), ("router1", K * 8), ("router2", K * 16), ("br", 8), ("scale", 1),
                      ("att0", 8 * 16), ("att1", K * 2), ("att2", K * 8), ("att3", K * 2)):
    SMALL[_name] = (_at, _width)
    _at += _width
SMALL_WIDTH = _at
BIAS_ROWS = (D, D, 1024, D, D, D, D)
BIAS_AT = [sum(BIAS_ROWS[:i]) for i in range(len(BIAS_ROWS))]

EDGE_LAYERS = (
    dict(rel=1, heads=8, width=128, pieces=((0, 2), (2, 4), (4, 6)), att="att0"),
    dict(rel=1, heads=1, width=768, pieces=((0, 3), (3, 6), (6, 8)), att="att1"),
    dict(rel=REL, heads=4, width=192, pieces=((0, 3), (3, 6)), att="att2"),
    dict(rel=REL, heads=1, width=768, pieces=((0, 3), (3, 6)), att="att3"),
)


class Counts:

    def __init__(self):
        self.count, self.grows, self.inner, self.i = {}, {}, {}, None

    def upto(self, sem, more=1):
        if self.i is None:
            self.count[sem] = self.count.get(sem, 0) + more
            return self.count[sem]
        self.inner[sem] = self.inner.get(sem, 0) + more
        return self.i * self.grows[sem] + (self.count.get(sem, 0) + self.inner[sem])

    @contextmanager
    def loop(self, engine, trips, grows):
        with engine.Fori(0, trips) as i:
            self.i, self.grows, self.inner = i, grows, {}
            yield i
        assert self.inner == grows, (self.inner, grows)
        self.i = None
        for sem, per in grows.items():
            self.count[sem] = self.count.get(sem, 0) + trips * per


UNITS_AT = (L0_GNN_PIECES, L0_GNN_PIECES + 3 * UNITS[0] + 3 + 3 + 8,
            L0_GNN_PIECES + 3 * UNITS[0] + 3 + 3 + 8 + 3 * UNITS[1] + 2 * REL * 2)
SLOTS_AT = STREAM - 2 * SLOTS


def build(nc, x_in, edges, query, small_in, bias_in, bd_in, phi_in, slot_b1_in, slot_b2_in, stream, out):
    with ExitStack() as ctx:
        def sb(name, shape, dt=F32, where=ctx):
            return where.enter_context(nc.sbuf_tensor(name, shape, dt))

        def sem(name):
            return ctx.enter_context(nc.semaphore(name))

        ring = [sb(f"ring{i}", [P, PIECE]) for i in range(RING)]
        x = sb("x", [P, T, D])
        rows = sb("rows", [P, T, D])
        cols = sb("cols", [P, K, N])
        counts = sb("counts", [P, T, REL, N])
        loop_counts = sb("loop_counts", [P, T, N])
        bias = sb("bias", [P, 1024])
        ident = sb("ident", [P, P])
        ones = sb("ones", [P, P])
        tiny = sb("tiny", [P, 2], BF16)
        iota = sb("iota", [P, SLOTS])
        small = sb("small", [P, SMALL_WIDTH])
        stats = sb("stats", [P, T, 2, 6])
        moments = sb("moments", [P, T, 2])
        root = sb("root", [P, SLOTS])
        inverse = sb("inverse", [P, T])
        dinv = sb("dinv", [P, T])

        with ExitStack() as l0:
            query_cols = sb("query_cols", [P, K, B * L], F32, l0)
            query_gate = sb("query_gate", [P, K, B * L], F32, l0)
            hidden_gate = sb("hidden_gate", [P, K, N], F32, l0)
            mean_counts = sb("mean_counts", [P, T, REL * N], F32, l0)
            hidden = sb("hidden", [P, K, N], F32, l0)
            with ExitStack() as part:
                edge_ints = sb("edge_ints", [P, 3, EDGE_TILES], I32, part)
                edge_src = sb("edge_src", [P, EDGE_TILES], F32, part)
                edge_dst = sb("edge_dst", [P, EDGE_TILES], F32, part)
                edge_key = sb("edge_key", [P, EDGE_TILES], F32, part)
                key_iota = sb("key_iota", [P, REL * N], F32, part)
                src_hot = [sb(f"src_hot{i}", [P, N], BF16, part) for i in range(2)]
                key_hot = [sb(f"key_hot{i}", [P, REL * N], BF16, part) for i in range(2)]
                raw_counts = sb("raw_counts", [P, T, REL * N], F32, part)
                in_degree = sb("in_degree", [P, REL * N], F32, part)
            with ExitStack() as part:
                aggregate = [sb(f"aggregate{i}", [P, K, N], F32, part) for i in range(2)]
            with ExitStack() as part:
                chunk = [sb(f"chunk{i}", [P, GROUP, L], F32, part) for i in range(CHUNK_RING)]
            with ExitStack() as part:
                alpha = sb("alpha", [P, K, N], F32, part)

        with ExitStack() as part:
            logits = sb("logits", [P, T, 16], F32, part)
            row_max = sb("row_max", [P, T], F32, part)
            row_sum = sb("row_sum", [P, T], F32, part)
            top = sb("top", [P, T, 8], F32, part)
            top_at = sb("top_at", [P, T, 8], U32, part)
            top_place = sb("top_place", [P, T, 8], F32, part)
            top_weight = sb("top_weight", [P, T, 2], F32, part)
            gap = sb("gap", [P, T], F32, part)
            combine = sb("combine", [P, T, 16], F32, part)
            second = sb("second", [P, T, 16], F32, part)
            combine_cols = sb("combine_cols", [16, N], F32, part)
            unit_weight = sb("unit_weight", [P, T, 18], F32, part)
            bd_rows = sb("bd_rows", [8, D], F32, part)
            high = [sb(f"high{i}", [P, PIECE], F32R, part) for i in range(3)]
            low = [sb(f"low{i}", [P, PIECE], F32R, part) for i in range(3)]
            cols_high = sb("cols_high", [P, K, N], F32R, part)
            cols_low = sb("cols_low", [P, K, N], F32R, part)
            act_high = sb("act_high", [P, 3, N], F32R, part)
            act_low = sb("act_low", [P, 3, N], F32R, part)
            gate_part = sb("gate_part", [P, 3, N], F32, part)
            up_part = sb("up_part", [P, 3, N], F32, part)
            squash = sb("squash", [P, 3, N], F32, part)
            act_cols = sb("act_cols", [P, 3, N], F32, part)

        with ExitStack() as part:
            message = sb("message", [P, REL * T * D], F32, part)
            wide_rows = sb("wide_rows", [P, T, 1024], F32, part)
            wide_cols = sb("wide_cols", [P, 8, N], F32, part)
            edge_scores = [sb(f"edge_scores{i}", [P, REL * N], F32, part) for i in range(2)]
            edge_exp = [sb(f"edge_exp{i}", [P, REL * N], F32, part) for i in range(2)]
            edge_turned = [sb(f"edge_turned{i}", [P, REL * T, P], F32, part) for i in range(2)]
            absent = sb("absent", [P, T, REL * N], F32, part)
            all_counts = sb("all_counts", [P, T, N], F32, part)
            queries_keys = sb("queries_keys", [P, T, REL, 16], F32, part)
            keys = sb("keys", [P, T, 16], F32, part)
            key_rows = sb("key_rows", [12, N], F32, part)
            edge_max = sb("edge_max", [P, 2], F32, part)
            edge_negmax = sb("edge_negmax", [P, 2], F32, part)
            edge_sum = sb("edge_sum", [P, 4], F32, part)
            edge_inverse = sb("edge_inverse", [P, 4], F32, part)

        with ExitStack() as part:
            head_q = sb("head_q", [P, K, N], F32, part)
            head_k = sb("head_k", [P, K, N], F32, part)
            values = sb("values", [P, T, D], F32, part)
            context = sb("context", [P, K, N], F32, part)
            normed = sb("normed", [P, T, D], F32, part)
            probs = [sb(f"probs{i}", [P, T, N], F32, part) for i in range(2)]
            probs_turned = [sb(f"probs_turned{i}", [P, T, N], F32, part) for i in range(2)]
            head_max = sb("head_max", [P, 2, T], F32, part)
            head_negmax = sb("head_negmax", [P, 2, T], F32, part)
            head_sum = sb("head_sum", [P, 2, T], F32, part)
            head_inverse = sb("head_inverse", [P, 2, T], F32, part)

        with ExitStack() as part:
            phi = sb("phi", [P, K, SLOTS], F32, part)
            phi_squares = sb("phi_squares", [P, K, SLOTS], F32, part)
            phi_scale = sb("phi_scale", [P, SLOTS], F32, part)
            dispatch = sb("dispatch", [SLOTS, N], F32, part)
            dispatch_rows = sb("dispatch_rows", [P, T, SLOTS], F32, part)
            mixing = sb("mixing", [P, T, SLOTS], F32, part)
            mixing_pair = sb("mixing_pair", [P, T, 2, SLOTS], F32, part)
            mixing_cols = sb("mixing_cols", [SLOT_PAIR, N], F32, part)
            soft = sb("soft", [P, 8], F32, part)
            slot_high = [sb(f"slot_high{i}", [P, PIECE], F32R, part) for i in range(3)]
            slot_low = [sb(f"slot_low{i}", [P, PIECE], F32R, part) for i in range(3)]
            slot_in = sb("slot_in", [P, K, SLOTS], F32, part)
            slot_pair = sb("slot_pair", [P, K, SLOT_PAIR], F32R, part)
            slot_mask = [sb(f"slot_mask{i}", [P, K, SLOT_PAIR], F32R, part) for i in range(3)]
            slot_fold = sb("slot_fold", [SLOT_PAIR, SLOTS], F32, part)
            slot_sum = sb("slot_sum", [SLOT_PAIR, SLOT_HIDDEN], F32, part)
            slot_b1 = sb("slot_b1", [P, 3, SLOTS], F32, part)
            slot_b2 = sb("slot_b2", [SLOT_PAIR, D], F32, part)
            slot_hidden = sb("slot_hidden", [P, 3, SLOTS], F32, part)
            slot_out = sb("slot_out", [SLOT_PAIR, D], F32, part)
            squares = sb("squares", [P, D], F32, part)

        psum = ctx.enter_context(nc.psum_tensor("psum", [P, 8, 512], F32))
        flat = psum[:].rearrange("p b c -> p (b c)")

        small_landed, x_landed, edges_landed, query_landed = (
            sem(n) for n in ("small_landed", "x_landed", "edges_landed", "query_landed"))
        piece_landed = [sem(f"piece_landed{i}") for i in range(RING)]
        ring_taken = sem("ring_taken")
        bias_landed, bias_used = sem("bias_landed"), sem("bias_used")
        bd_landed, slots_landed = sem("bd_landed"), sem("slots_landed")
        arena_free = sem("arena_free")
        pool_wrote, vector_wrote, scalar_wrote = sem("pool_wrote"), sem("vector_wrote"), sem("scalar_wrote")
        constants_ready, ones_ready = sem("constants_ready"), sem("ones_ready")
        root_asked, root_ready = sem("root_asked"), sem("root_ready")
        exp_asked, exp_ready = sem("exp_asked"), sem("exp_ready")
        rows_ready, turned, cols_ready, rows_done = (
            sem(n) for n in ("rows_ready", "turned", "cols_ready", "rows_done"))
        tile_done = sem("tile_done")
        hot_ready, hot_used, counted = sem("hot_ready"), sem("hot_used"), sem("counted")
        raw_ready, degree_done, counts_turned, counts_ready = (
            sem(n) for n in ("raw_ready", "degree_done", "counts_turned", "counts_ready"))
        aggregated, aggregate_ready = sem("aggregated"), sem("aggregate_ready")
        gate_hidden_ready, chunk_summed, chunk_squashed, chunk_weighted, chunk_folded, chunk_reduced = (
            sem(n) for n in ("gate_hidden_ready", "chunk_summed", "chunk_squashed", "chunk_weighted",
                             "chunk_folded", "chunk_reduced"))
        tanh_ready, alpha_ready, hidden_ready, turned_back, rows_back = (
            sem(n) for n in ("tanh_ready", "alpha_ready", "hidden_ready", "turned_back", "rows_back"))
        logits_taken = sem("logits_taken")
        high_ready, cols_high_ready, cols_split = sem("high_ready"), sem("cols_high_ready"), sem("cols_split")
        logits_done, combine_ready, combine_turned, combine_cols_ready = (
            sem(n) for n in ("logits_done", "combine_ready", "combine_turned", "combine_cols_ready"))
        gate_done, gate_clipped, squashed, up_done, act_ready, down_done, down_taken = (
            sem(n) for n in ("gate_done", "gate_clipped", "squashed", "up_done", "act_ready", "down_done",
                             "down_taken"))
        query_keys_done, keys_ready, keys_turned, key_rows_ready = (
            sem(n) for n in ("query_keys_done", "keys_ready", "keys_turned", "key_rows_ready"))
        picked, lifted, edge_max_ready, edge_exp_ready, edge_weighted, edges_turned, edges_copied, mixed, stored = (
            sem(n) for n in ("picked", "lifted", "edge_max_ready", "edge_exp_ready", "edge_weighted",
                             "edges_turned", "edges_copied", "mixed", "stored"))
        heads_ready, scored, head_max_ready, probs_exp, probs_ready, probs_done, probs_copied, context_done, \
            context_ready = (sem(n) for n in ("heads_ready", "scored", "head_max_ready", "probs_exp", "probs_ready",
                                              "probs_done", "probs_copied", "context_done", "context_ready"))
        phi_squared, phi_summed, phi_ready, slot_logits_done, soft_ready, soft_turned, soft_copied = (
            sem(n) for n in ("phi_squared", "phi_summed", "phi_ready", "slot_logits_done", "soft_ready",
                             "soft_turned", "soft_copied"))
        slot_in_done, mask_ready, slot_used, slot_sums_done, slot_sums_ready, slot_folded, slot_pre, slot_act, \
            slot_out_done, slot_out_ready = (
                sem(n) for n in ("slot_in_done", "mask_ready", "slot_used", "slot_sums_done", "slot_sums_ready", "slot_folded",
                                 "slot_pre", "slot_act", "slot_out_done", "slot_out_ready"))
        x_final, out_stored = sem("x_final"), sem("out_stored")

        def row_parts(width):
            return [(0, 0, min(width, 512))] + ([(1, 512, width - 512)] if width > 512 else [])

        def row_bank(t, j, n):
            if j == 0:
                return psum[:, 3 + t, 0:n]
            return psum[:, 5, t * N:t * N + n] if n == N else psum[:, 5 + t, 0:n]

        def opens(t, j, n):
            return t == 0 or j == 0 or n != N

        def col_tile(f):
            return flat[:, f * N:(f + 1) * N]

        UNIT_BANKS = ((0, 1), (2, 6))

        def unit_bank(part, last):
            return psum[:, UNIT_BANKS[part][last], 0:N if last else 2 * N]

        def unit_tile(part, f):
            return psum[:, UNIT_BANKS[part][f // 2], f % 2 * N:(f % 2 + 1) * N]

        def node_tile(t):
            return slice(t * P, (t + 1) * P)

        def small_at(name, i=0, n=1):
            return small[:, SMALL[name][0] + i:SMALL[name][0] + i + n]

        flat_x = x[:].rearrange("p t d -> p (t d)")
        flat_rows = rows[:].rearrange("p t d -> p (t d)")
        flat_cols = cols[:].rearrange("p k n -> p (k n)")
        flat_hidden = hidden[:].rearrange("p k n -> p (k n)")
        flat_gate = hidden_gate[:].rearrange("p k n -> p (k n)")
        flat_counts = counts[:].rearrange("p t r n -> p (t r n)")

        def message_rows(layer):
            width = layer["heads"] * layer["width"]
            n = layer["rel"] * T * width
            return message[:, 0:n].rearrange("p (r t d) -> p r t d", r=layer["rel"], t=T)

        block = ctx.enter_context(nc.Block())

        @block.sync
        def _(sp):
            seen = Counts()
            sp.dma_start(x[:], x_in.rearrange("(t p) d -> p t d", p=P)).then_inc(x_landed, 16)
            for i in range(RING):
                sp.dma_start(ring[i][:], stream[i]).then_inc(piece_landed[i], 16)
            turns, rest = divmod(STREAM - RING, RING)
            with seen.loop(sp, turns, {ring_taken: RING}) as i:
                for s in range(RING):
                    sp.wait_ge(ring_taken, seen.upto(ring_taken))
                    piece = stream[bass.ds(i * RING + (RING + s), 1)].rearrange("a p c -> (a p) c")
                    sp.dma_start(ring[s][:], piece).then_inc(piece_landed[s], 16)
            for s in range(rest):
                sp.wait_ge(ring_taken, seen.upto(ring_taken))
                sp.dma_start(ring[s][:], stream[STREAM - rest + s]).then_inc(piece_landed[s], 16)
            sp.wait_ge(x_final, 1)
            sp.dma_start(out.rearrange("(t p) d -> p t d", p=P), x[:]).then_inc(out_stored, 16)
            sp.wait_ge(out_stored, 16)

        @block.gpsimd
        def _(pool):
            seen = Counts()
            pool.memset(ident[:], 0.0).then_inc(pool_wrote, 1)
            pool.wait_ge(pool_wrote, seen.upto(pool_wrote))
            pool.affine_select(out=ident[:], in_=ident[:], compare_op=ALU.not_equal, fill=1.0, base=0,
                               pattern=[[-1, P]], channel_multiplier=1).then_inc(constants_ready, 1)
            pool.iota(iota[:], [[1, SLOTS]], base=0, channel_multiplier=0,
                      allow_small_or_imprecise_dtypes=True).then_inc(constants_ready, 1)
            pool.iota(key_iota[:], [[1, REL * N]], base=0, channel_multiplier=0,
                      allow_small_or_imprecise_dtypes=True).then_inc(constants_ready, 1)

            def load_bias(n):
                if n:
                    pool.wait_ge(bias_used, seen.upto(bias_used))
                at, width = BIAS_AT[n], BIAS_ROWS[n]
                pool.dma_start(bias[:, 0:width], bias_in[:, at:at + width].broadcast_to([P, width]))\
                    .then_inc(bias_landed, 16)

            def sum_chunk(c, slot):
                nodes = GROUP - BIASED
                by_node = flat_gate[:, bass.ds(c * GROUP + BIASED, nodes)].unsqueeze(2).broadcast_to([P, nodes, L])
                by_query = query_gate[:].rearrange("p k q -> p (k q)")[:, bass.ds(c * L, L)]\
                    .unsqueeze(1).broadcast_to([P, nodes, L])
                pool.tensor_tensor(chunk[slot][:, BIASED:, :], by_node, by_query, ALU.add).then_inc(chunk_summed, 1)

            load_bias(0)
            for layer in range(2):
                pool.wait_ge(gate_hidden_ready, seen.upto(gate_hidden_ready, 6 + 3 if layer == 0 else 3))
                for c in range(CHUNK_RING):
                    sum_chunk(c, c)
                with seen.loop(pool, CHUNKS // CHUNK_RING - 1, {chunk_reduced: CHUNK_RING}) as i:
                    for s in range(CHUNK_RING):
                        pool.wait_ge(chunk_reduced, seen.upto(chunk_reduced))
                        sum_chunk(i * CHUNK_RING + (CHUNK_RING + s), s)
                seen.upto(chunk_reduced, CHUNK_RING)
                load_bias(layer + 1)
            pool.wait_ge(arena_free, seen.upto(arena_free))
            pool.dma_start(bd_rows[:], bd_in).then_inc(bd_landed, 16)
            for n in range(3, len(BIAS_ROWS)):
                load_bias(n)
            pool.wait_ge(arena_free, seen.upto(arena_free))
            pool.dma_start(phi[:], phi_in).then_inc(slots_landed, 16)
            pool.dma_start(slot_b1[:], slot_b1_in).then_inc(slots_landed, 16)
            pool.dma_start(slot_b2[:], slot_b2_in).then_inc(slots_landed, 16)

        @block.tensor
        def _(pe):
            seen = Counts()
            place = [0]

            def signal(what, n=1):
                pe.matmul(psum[0:2, 7, 508:510], tiny[:], tiny[:], start=True, stop=True).then_inc(what, n)

            def piece(turn=None, ahead=0):
                n = place[0] + ahead
                slot = n % RING
                rounds = n // RING + 1
                if turn is None:
                    pe.wait_ge(piece_landed[slot], 16 * rounds)
                else:
                    pe.wait_ge(piece_landed[slot], turn * 16 + 16 * rounds)
                return ring[slot]

            def use(n=1):
                place[0] += n

            def product_rows(source, pieces, width, first=True, last=True):
                end = pieces[-1][1] - 1
                for k0, k1 in pieces:
                    weights = piece()
                    for k in range(k0, k1):
                        for t in range(T):
                            for j, c, n in row_parts(width):
                                at = (k - k0) * width + c
                                mm = pe.matmul(row_bank(t, j, n), source[:, k, node_tile(t)],
                                               weights[:, at:at + n], start=first and k == 0 and opens(t, j, n),
                                               stop=last and k == end, skip_group_check=True)
                    mm.then_inc(ring_taken, 1)
                    use()
                if last:
                    signal(rows_done, 1)

            def product_cols(source, n, tile, done):
                for half in range(2):
                    weights = piece()
                    for f in range(3):
                        for k in range(K):
                            mm = pe.matmul(tile(3 * half + f), weights[:, k * HALF + f * P:k * HALF + (f + 1) * P],
                                           source[:, k, 0:n], start=k == 0, stop=k == K - 1)
                        if f == 2:
                            mm.then_inc(ring_taken, 1)
                        if n == 512 or (3 * half + f) % 2 == 1:
                            signal(done)
                    use()

            def turn_rows(source, tiles=K, awaited=False):
                if not awaited:
                    pe.wait_ge(rows_ready, seen.upto(rows_ready))
                for k in range(tiles):
                    for t in range(T):
                        mm = pe.transpose(flat[:, k * N + t * P:k * N + (t + 1) * P],
                                          source[:, t, k * P:(k + 1) * P], ident[:])
                    if k % 2 == 1:
                        mm.then_inc(turned, 1)
                pe.wait_ge(cols_ready, seen.upto(cols_ready, tiles // 2))

            def turn_cols_back(source):
                for t in range(T):
                    for k in range(K):
                        at = t * D + k * P
                        mm = pe.transpose(flat[:, at:at + P], source[:, k, node_tile(t)], ident[:])
                        if (at + P) % 512 == 0:
                            mm.then_inc(turned_back, 1)

            pe.wait_ge(constants_ready, seen.upto(constants_ready, 3))
            pe.wait_ge(ones_ready, seen.upto(ones_ready))
            pe.wait_ge(small_landed, seen.upto(small_landed, 16))

            def count_edges():
                def tile(q, first, last):
                    pe.wait_ge(hot_ready, seen.upto(hot_ready))
                    for t in range(T):
                        for j, c, n in row_parts(REL * N):
                            mm = pe.matmul(row_bank(t, j, n), src_hot[q][:, node_tile(t)], key_hot[q][:, c:c + n],
                                           start=first and opens(t, j, n), stop=last, skip_group_check=True)
                    mm.then_inc(hot_used, 1)

                tile(0, True, False)
                tile(1, False, False)
                with seen.loop(pe, EDGE_TILES // 2 - 2, {hot_ready: 2}):
                    tile(0, False, False)
                    tile(1, False, False)
                tile(0, False, False)
                tile(1, False, True)
                signal(counted, 1)
                pe.wait_ge(raw_ready, seen.upto(raw_ready))
                for j, c, n in row_parts(REL * N):
                    for t in range(T):
                        mm = pe.matmul(row_bank(0, j, n), ones[:], raw_counts[:, t, c:c + n],
                                       start=t == 0, stop=t == T - 1)
                mm.then_inc(degree_done, 1)
                for t in range(T):
                    for r in range(REL):
                        for s in range(T):
                            at = t * REL * N + r * N + s * P
                            mm = pe.transpose(flat[:, at:at + P], raw_counts[:, s, r * N + t * P:r * N + (t + 1) * P],
                                              ident[:])
                mm.then_inc(counts_turned, 1)

            def l0_gnn():
                count_edges()
                pe.wait_ge(counts_ready, seen.upto(counts_ready))
                pe.wait_ge(query_landed, seen.upto(query_landed, 16))
                product_cols(query_cols, B * L, lambda f: psum[:, f, 0:512], tile_done)
                pe.wait_ge(gate_hidden_ready, seen.upto(gate_hidden_ready, 6))
                for layer in range(2):
                    if layer == 0:
                        turn_rows(rows)
                        source = cols
                    else:
                        pe.wait_ge(rows_back, seen.upto(rows_back, 3))
                        source = hidden

                    def aggregate_nodes(r):
                        for f in range(K):
                            for s in range(T):
                                mm = pe.matmul(col_tile(f), rows[:, s, f * P:(f + 1) * P],
                                               mean_counts[:, s, r * N:(r + 1) * N], start=s == 0, stop=s == T - 1)
                            if f % 2 == 1:
                                mm.then_inc(aggregated, 1)

                    halves = ((0, 3), (3, 6))
                    aggregate_nodes(0)
                    product_rows(source, halves, D, last=False)
                    for r in range(REL):
                        pe.wait_ge(aggregate_ready, seen.upto(aggregate_ready, 3))
                        if r + 1 < REL:
                            aggregate_nodes(r + 1)
                        product_rows(aggregate[r % 2], halves, D, first=False, last=r == REL - 1)
                    turn_rows(rows)
                    product_cols(cols, N, col_tile, tile_done)
                    seen.upto(gate_hidden_ready, 3)

                    def fold(q):
                        pe.wait_ge(chunk_weighted, seen.upto(chunk_weighted))
                        for s in range(L // 16):
                            mm = pe.matmul(psum[:, q, 0:(GROUP - WHOLE) * 16]
                                           .rearrange("p (n l) -> p n l", n=GROUP - WHOLE), ident[:],
                                           chunk[q][:, WHOLE:, 16 * s:16 * s + 16], start=s == 0,
                                           stop=s == L // 16 - 1)
                        mm.then_inc(chunk_folded, 1)

                    for c in range(CHUNK_RING):
                        fold(c)
                    with seen.loop(pe, CHUNKS // CHUNK_RING - 1,
                                   {chunk_weighted: CHUNK_RING, chunk_reduced: CHUNK_RING}):
                        for q in range(CHUNK_RING):
                            pe.wait_ge(chunk_reduced, seen.upto(chunk_reduced))
                            fold(q)
                    pe.wait_ge(chunk_reduced, seen.upto(chunk_reduced, CHUNK_RING))
                    for half in range(2):
                        hidden_part, query_part = piece(), piece(ahead=1)
                        for f in range(3):
                            for part, (weights, source) in enumerate(((hidden_part, cols), (query_part, hidden_gate))):
                                for k in range(K):
                                    mm = pe.matmul(col_tile(3 * half + f),
                                                   weights[:, k * HALF + f * P:k * HALF + (f + 1) * P],
                                                   source[:, k, :], start=part == 0 and k == 0,
                                                   stop=part == 1 and k == K - 1)
                            if (3 * half + f) % 2 == 1:
                                mm.then_inc(tile_done, 1)
                        signal(ring_taken, 2)
                        use(2)
                    pe.wait_ge(hidden_ready, seen.upto(hidden_ready))
                    turn_cols_back(hidden)

            def experts(layer):
                units, count, start = UNITS[layer], EXPERTS[layer], place[0]
                turn_rows(rows)
                at, _ = SMALL[f"router{layer}"]
                for t in range(T):
                    for k in range(K):
                        mm = pe.matmul(psum[:, 3, t * 16:t * 16 + count], cols[:, k, node_tile(t)],
                                       small[:, at + k * count:at + (k + 1) * count], start=k == 0, stop=k == K - 1)
                mm.then_inc(logits_done, 1)
                pe.wait_ge(cols_split, seen.upto(cols_split))

                def await_split(turn, ahead):
                    if turn is None:
                        pe.wait_ge(ring_taken, start + ahead + 1)
                    else:
                        pe.wait_ge(ring_taken, turn * RING + (start + ahead + 1))

                def gate_or_up(part, turn, ahead):
                    await_split(turn, ahead)
                    for f in range(3):
                        for k in range(K):
                            at = slice(k * HALF + f * P, k * HALF + (f + 1) * P)
                            for n, (weights, source) in enumerate(((high, cols_high), (high, cols_low),
                                                                   (low, cols_high))):
                                mm = pe.matmul(unit_tile(part, f), weights[part][:, at], source[:, k, :],
                                               start=k == 0 and n == 0, stop=k == K - 1 and n == 2)
                        if f > 0:
                            mm.then_inc(gate_done if part == GATE else up_done, 1)

                def down(turn, ahead):
                    await_split(turn, ahead)
                    pe.wait_ge(act_ready, seen.upto(act_ready))
                    for f in range(3):
                        for t in range(T):
                            for n, (source, weights) in enumerate(((act_high, high), (act_high, low),
                                                                   (act_low, high))):
                                for j, c, size in row_parts(D):
                                    mm = pe.matmul(row_bank(t, j, size), source[:, f, node_tile(t)],
                                                   weights[DOWN][:, f * D + c:f * D + c + size],
                                                   start=f == 0 and n == 0 and opens(t, j, size),
                                                   stop=f == 2 and n == 2, skip_group_check=True)
                    mm.then_inc(down_done, 1)

                gate_read = gate_clipped if layer == 0 else squashed

                def step(turn, ahead, first=False):
                    pe.wait_ge(gate_read, seen.upto(gate_read, 2))
                    gate_or_up(GATE, turn, ahead)
                    if first:
                        pe.wait_ge(logits_taken, seen.upto(logits_taken))
                    else:
                        pe.wait_ge(down_taken, seen.upto(down_taken))
                    down(turn, ahead + 1)
                    gate_or_up(UP, turn, ahead + 2)

                gate_or_up(GATE, None, 0)
                gate_or_up(UP, None, 1)
                step(None, 2, first=True)
                turns, rest = divmod(units - 2, RING // 3)
                with seen.loop(pe, turns, {gate_read: 2 * RING // 3, down_taken: RING // 3, act_ready: RING // 3}) as i:
                    for u in range(RING // 3):
                        step(i, 5 + 3 * u)
                for u in range(rest):
                    step(None, 5 + turns * RING + 3 * u)
                pe.wait_ge(gate_read, seen.upto(gate_read, 2))
                pe.wait_ge(down_taken, seen.upto(down_taken))
                down(None, 3 * units - 1)
                pe.wait_ge(down_taken, seen.upto(down_taken))
                if layer == 0:
                    pe.wait_ge(combine_ready, seen.upto(combine_ready))
                    for t in range(T):
                        mm = pe.transpose(psum[0:count, 6, t * P:(t + 1) * P], combine[:, t, 0:count], ident[:])
                    mm.then_inc(combine_turned, 1)
                    pe.wait_ge(combine_cols_ready, seen.upto(combine_cols_ready))
                    pe.wait_ge(bd_landed, seen.upto(bd_landed, 16))
                    for t in range(T):
                        for j, c, n in row_parts(D):
                            mm = pe.matmul(row_bank(t, j, n), combine_cols[0:count, node_tile(t)],
                                           bd_rows[0:count, c:c + n], start=opens(t, j, n), stop=True,
                                           skip_group_check=True)
                    mm.then_inc(down_done, 1)
                    pe.wait_ge(down_taken, seen.upto(down_taken))
                use(3 * units)

            def edge_layer(n):
                layer = EDGE_LAYERS[n]
                rel, heads, width = layer["rel"], layer["heads"], layer["width"]
                out_width = heads * width
                tiles = out_width // P
                source = wide_cols if n == 1 else cols
                messages = message_rows(layer)
                turn_rows(wide_rows if n == 1 else rows, 8 if n == 1 else K)
                at, _ = SMALL[layer["att"]]
                for r in range(rel + 1):
                    if r > 0:
                        pe.wait_ge(rows_ready, seen.upto(rows_ready))
                    if r < rel:
                        product_rows(source, layer["pieces"], out_width)
                    if r > 0:
                        turn_rows(messages[:, r - 1], tiles, awaited=True)
                        for t in range(T):
                            for k in range(tiles):
                                to = (t * rel + r - 1) * 16
                                mm = pe.matmul(psum[:, 7, to:to + 2 * heads], wide_cols[:, k, node_tile(t)],
                                               small[:, at + k * 2 * heads:at + (k + 1) * 2 * heads],
                                               start=k == 0, stop=k == tiles - 1)
                mm.then_inc(query_keys_done, 1)
                pe.wait_ge(keys_ready, seen.upto(keys_ready))
                count = rel * heads
                for t in range(T):
                    mm = pe.transpose(psum[0:count, 7, t * P:(t + 1) * P], keys[:, t, 0:count], ident[:])
                mm.then_inc(keys_turned, 1)
                pe.wait_ge(key_rows_ready, seen.upto(key_rows_ready))
                items = [(t, h) for h in range(heads) for t in range(T)]

                def pick_keys(i):
                    if i >= 2:
                        pe.wait_ge(lifted, seen.upto(lifted))
                    t, h = items[i]
                    for r in range(rel):
                        at = i % 2 * 1024 + r * N
                        row = r * heads + h
                        mm = pe.matmul(flat[:, at:at + N], ident[0:count, row:row + 1].broadcast_to([count, P]),
                                       key_rows[0:count, :],
                                       start=True, stop=True)
                    mm.then_inc(picked, 1)

                def turn_edges(i):
                    pe.wait_ge(edge_weighted, seen.upto(edge_weighted))
                    for m in range(rel * T):
                        at = 4 * 512 + m * P
                        mm = pe.transpose(flat[:, at:at + P], edge_exp[i % 2][:, m * P:(m + 1) * P], ident[:])
                    mm.then_inc(edges_turned, 1)

                def mix(i):
                    t, h = items[i]
                    pe.wait_ge(edges_copied, seen.upto(edges_copied))
                    if width > 512:
                        if i >= 1:
                            pe.wait_ge(stored, seen.upto(stored))
                    elif i >= 2:
                        pe.wait_ge(stored, seen.upto(stored))
                    for j, c, size in row_parts(width):
                        bank = 6 + j if width > 512 else 6 + i % 2
                        for m in range(rel * T):
                            r, s = divmod(m, T)
                            mm = pe.matmul(psum[:, bank, 0:size], edge_turned[i % 2][:, m, :],
                                           messages[:, r, s, h * width + c:h * width + c + size],
                                           start=m == 0, stop=m == rel * T - 1)
                    mm.then_inc(mixed, 1)

                last = len(items)
                for s in range(last + 3):
                    if s < last:
                        pick_keys(s)
                    if 0 <= s - 3 < last:
                        mix(s - 3)
                    if 0 <= s - 2 < last:
                        turn_edges(s - 2)
                pe.wait_ge(lifted, seen.upto(lifted, 2))
                pe.wait_ge(stored, seen.upto(stored, 1 if width > 512 else 2))

            def self_attention():
                turn_rows(normed)
                product_cols(cols, N, col_tile, tile_done)
                pe.wait_ge(heads_ready, seen.upto(heads_ready, 3))
                product_cols(cols, N, col_tile, tile_done)
                product_rows(cols, ((0, 3), (3, 6)), D)
                pe.wait_ge(heads_ready, seen.upto(heads_ready, 3))
                pe.wait_ge(rows_ready, seen.upto(rows_ready))

                def scores(h):
                    if h >= 2:
                        pe.wait_ge(probs_exp, seen.upto(probs_exp))
                    at = h % 2 * HEAD
                    for t in range(T):
                        mm = pe.matmul(psum[:, h % 2, t * N:(t + 1) * N], head_q[at:at + HEAD, h // 2, node_tile(t)],
                                       head_k[at:at + HEAD, h // 2, :], start=True, stop=True)
                    mm.then_inc(scored, 1)

                def turn_probs(h):
                    pe.wait_ge(probs_ready, seen.upto(probs_ready))
                    for s in range(T):
                        for t in range(T):
                            mm = pe.transpose(psum[:, 2 + h % 2, s * N + t * P:s * N + (t + 1) * P],
                                              probs[h % 2][:, t, s * P:(s + 1) * P], ident[:])
                    mm.then_inc(probs_done, 1)

                def mix_values(h):
                    pe.wait_ge(probs_copied, seen.upto(probs_copied))
                    if h >= 2:
                        pe.wait_ge(context_ready, seen.upto(context_ready))
                    at = h % 2 * HEAD
                    for s in range(T):
                        mm = pe.matmul(psum[at:at + HEAD, 4 + h % 2, 0:N], values[:, s, h * HEAD:(h + 1) * HEAD],
                                       probs_turned[h % 2][:, s, :], start=s == 0, stop=s == T - 1)
                    mm.then_inc(context_done, 1)

                for s in range(HEADS + 2):
                    if s < HEADS:
                        scores(s)
                    if 0 <= s - 1 < HEADS:
                        turn_probs(s - 1)
                    if 0 <= s - 2 < HEADS:
                        mix_values(s - 2)
                pe.wait_ge(probs_exp, seen.upto(probs_exp, 2))
                pe.wait_ge(context_ready, seen.upto(context_ready, 2))
                product_rows(context, ((0, 3), (3, 6)), D)

            def l1_gnn():
                edge_layer(0)
                edge_layer(1)

            def l1_ffn():
                self_attention()
                experts(1)

            def l2_gnn():
                edge_layer(2)
                edge_layer(3)

            def l3_gnn():
                turn_rows(rows)
                product_rows(cols, ((0, 3), (3, 6)), D)
                pe.wait_ge(rows_ready, seen.upto(rows_ready))
                for t in range(T):
                    for j, c, n in row_parts(D):
                        for s in range(T):
                            mm = pe.matmul(row_bank(t, j, n), loop_counts[:, s, node_tile(t)], rows[:, s, c:c + n],
                                           start=s == 0 and opens(t, j, n), stop=s == T - 1, skip_group_check=True)
                mm.then_inc(rows_done, 1)

            def l3_ffn():
                pe.wait_ge(phi_squared, seen.upto(phi_squared))
                for k in range(K):
                    mm = pe.matmul(psum[:, 7, 0:SLOTS], ones[:], phi_squares[:, k, :], start=k == 0, stop=k == K - 1)
                mm.then_inc(phi_summed, 1)
                turn_rows(rows)
                pe.wait_ge(phi_ready, seen.upto(phi_ready))
                for t in range(T):
                    for k in range(K):
                        pe.matmul(psum[:, 3, t * SLOTS:(t + 1) * SLOTS], cols[:, k, node_tile(t)], phi[:, k, :],
                                  start=k == 0, stop=k == K - 1)
                for k in range(K):
                    mm = pe.matmul(psum[0:SLOTS, 4, 0:N], phi[:, k, :], cols[:, k, :], start=k == 0, stop=k == K - 1)
                mm.then_inc(slot_logits_done, 1)
                pe.wait_ge(soft_ready, seen.upto(soft_ready))
                for t in range(T):
                    pe.transpose(psum[0:SLOT_PAIR, 5, t * P:(t + 1) * P],
                                 mixing_pair[:, t].rearrange("p h n -> p (h n)"), ident[:])
                    mm = pe.transpose(psum[:, 6, t * SLOTS:(t + 1) * SLOTS], dispatch[:, node_tile(t)],
                                      ident[0:SLOTS, 0:SLOTS])
                mm.then_inc(soft_turned, 1)
                pe.wait_ge(soft_copied, seen.upto(soft_copied))
                for f in range(K):
                    for s in range(T):
                        mm = pe.matmul(psum[:, 7, f * SLOTS:(f + 1) * SLOTS], rows[:, s, f * P:(f + 1) * P],
                                       dispatch_rows[:, s, :], start=s == 0, stop=s == T - 1)
                mm.then_inc(slot_in_done, 1)

                def slot_products(tiles, width):
                    def one(q, first=False, last=False):
                        pe.wait_ge(mask_ready, seen.upto(mask_ready))
                        for k in range(tiles):
                            for weights in (slot_high, slot_low):
                                for j, c, n in row_parts(width):
                                    at = k * width + c
                                    mm = pe.matmul(psum[:, 3 + j, 0:n], slot_mask[q][:, k, :],
                                                   weights[q][:, at:at + n],
                                                   start=first and k == 0 and weights is slot_high,
                                                   stop=last and k == tiles - 1 and weights is slot_low)
                        mm.then_inc(slot_used, 1)

                    start = place[0] - SLOTS_AT
                    one(start % 3, first=True)
                    with seen.loop(pe, (SLOTS - 4) // 3, {mask_ready: 3}):
                        for a in range(3):
                            one((start + 1 + a) % 3)
                    for a in range(SLOTS - 3, SLOTS):
                        one((start + a) % 3, last=a == SLOTS - 1)
                    use(SLOTS)

                assert place[0] == SLOTS_AT and (SLOTS - 4) % 3 == 0
                slot_products(K, SLOT_HIDDEN)
                signal(slot_sums_done, 1)
                pe.wait_ge(slot_sums_ready, seen.upto(slot_sums_ready))
                for k in range(3):
                    mm = pe.matmul(psum[:, 5, k * SLOTS:(k + 1) * SLOTS], slot_sum[:, k * P:(k + 1) * P],
                                   slot_fold[:], start=True, stop=True)
                mm.then_inc(slot_folded, 1)
                slot_products(3, D)
                signal(slot_out_done, 1)
                pe.wait_ge(slot_out_ready, seen.upto(slot_out_ready))
                for t in range(T):
                    for j, c, n in row_parts(D):
                        mm = pe.matmul(row_bank(t, j, n), mixing_cols[:, node_tile(t)], slot_out[:, c:c + n],
                                       start=opens(t, j, n), stop=True, skip_group_check=True)
                mm.then_inc(rows_done, 1)

            for stage in (l0_gnn, lambda: experts(0), l1_gnn, l1_ffn, l2_gnn, lambda: experts(2), l3_gnn,
                          l3_ffn):
                stage()

        @block.scalar
        def _(act):
            seen = Counts()
            act.dma_start(edge_ints[:], edges).then_inc(edges_landed, 16)
            act.dma_start(small[:], small_in).then_inc(small_landed, 16)
            act.dma_start(query_cols[:], query).then_inc(query_landed, 16)
            act.wait_ge(small_landed, seen.upto(small_landed, 16))

            def take_root(n, p=P):
                act.wait_ge(root_asked, seen.upto(root_asked))
                act.activation(root[0:p, 0:n], root[0:p, 0:n], ACT.Sqrt).then_inc(root_ready, 1)

            def copy_turned(target, tiles=K, relu=False, scale=None):
                for b in range(tiles // 2):
                    act.wait_ge(turned, seen.upto(turned))
                    for f in ((2 * b,) if scale is None else (2 * b, 2 * b + 1)):
                        n = 2 if scale is None else 1
                        to = target[:, f:f + n, :].rearrange("p k n -> p (k n)")
                        of = flat[:, f * N:(f + n) * N]
                        if scale is None:
                            ins = act.activation(to, of, ACT.Relu if relu else ACT.Copy)
                        else:
                            ins = act.activation(to, of, ACT.Identity, scale=small_at(scale, f))
                    ins.then_inc(cols_ready, 1)
                return seen.upto(cols_ready, tiles // 2)

            def l0_gnn():
                for f in range(K):
                    act.wait_ge(tile_done, seen.upto(tile_done))
                    act.activation(query_gate[:, f, :], psum[:, f, :], ACT.Identity, bias=small_at("bg", f))\
                        .then_inc(gate_hidden_ready, 1)
                take_root(T)
                for layer in range(2):
                    if layer == 0:
                        copy_turned(cols)
                    for r in range(REL):
                        for b in range(3):
                            act.wait_ge(aggregated, seen.upto(aggregated))
                            act.activation(aggregate[r % 2][:, 2 * b:2 * b + 2, :].rearrange("p k n -> p (k n)"),
                                           psum[:, b, :], ACT.Copy).then_inc(aggregate_ready, 1)
                    copy_turned(cols, relu=True)
                    for b in range(3):
                        act.wait_ge(tile_done, seen.upto(tile_done))
                        act.activation(flat_gate[:, 512 * b:512 * b + 512], psum[:, b, :], ACT.Copy)\
                            .then_inc(gate_hidden_ready, 1)
                    with seen.loop(act, CHUNKS // CHUNK_RING, {chunk_summed: CHUNK_RING}) as i:
                        for q in range(CHUNK_RING):
                            c = i * CHUNK_RING + q
                            act.wait_ge(chunk_summed, seen.upto(chunk_summed))
                            for n in range(BIASED):
                                act.activation(chunk[q][:, n, :],
                                               query_gate[:].rearrange("p k q -> p (k q)")[:, bass.ds(c * L, L)],
                                               ACT.Sigmoid, bias=flat_gate[:, bass.ds(c * GROUP + n, 1)])
                            act.activation(chunk[q][:, BIASED:, :], chunk[q][:, BIASED:, :], ACT.Sigmoid)\
                                .then_inc(chunk_squashed, 1)
                    act.wait_ge(chunk_reduced, seen.upto(chunk_reduced, CHUNKS))
                    act.activation(flat_hidden, flat_gate, ACT.Tanh).then_inc(tanh_ready, 1)
                    for f in range(K):
                        if f % 2 == 0:
                            act.wait_ge(tile_done, seen.upto(tile_done))
                        act.activation(alpha[:, f, :], col_tile(f), ACT.Sigmoid, bias=small_at("bq", f))\
                            .then_inc(alpha_ready, 1)
                    if layer == 0:
                        for b in range(3):
                            act.wait_ge(turned_back, seen.upto(turned_back))
                            act.activation(flat_rows[:, 512 * b:512 * b + 512], psum[:, b, :], ACT.Copy)\
                                .then_inc(rows_back, 1)

            def take_high(tile, n, turn=None):
                slot, rounds = n % RING, n // RING + 1
                act.wait_ge(piece_landed[slot], 16 * rounds if turn is None else turn * 16 + 16 * rounds)
                act.activation(tile[:], ring[slot][:], ACT.Copy).then_inc(high_ready, 1)

            def experts(layer):
                units, start = UNITS[layer], UNITS_AT[layer]
                take_root(T)
                take_high(high[GATE], start)
                copied = copy_turned(cols, scale="norm2" if layer == 1 else None)
                act.wait_ge(cols_ready, copied)
                act.activation(cols_high[:], cols[:], ACT.Copy).then_inc(cols_high_ready, 1)
                take_high(high[UP], start + 1)

                def squash_gate():
                    for last, tiles in ((0, slice(0, 2)), (1, slice(2, 3))):
                        to = squash[:, tiles, :].rearrange("p f n -> p (f n)")
                        if layer == 0:
                            act.wait_ge(gate_clipped, seen.upto(gate_clipped))
                            of = gate_part[:, tiles, :].rearrange("p f n -> p (f n)")
                            act.activation(to, of, ACT.Sigmoid, scale=1.702).then_inc(squashed, 1)
                        else:
                            act.wait_ge(gate_done, seen.upto(gate_done))
                            act.activation(to, unit_bank(0, last), ACT.Silu).then_inc(squashed, 1)

                squash_gate()
                take_high(high[GATE], start + 2)
                take_high(high[DOWN], start + 3)
                act.wait_ge(exp_asked, seen.upto(exp_asked))
                if layer == 0:
                    act.activation(gap[:], gap[:], ACT.Exp).then_inc(exp_ready, 1)
                else:
                    act.activation(logits[:, :, 0:EXPERTS[layer]], logits[:, :, 0:EXPERTS[layer]], ACT.Exp)\
                        .then_inc(exp_ready, 1)

                def step(turn, ahead, last=False):
                    act.wait_ge(up_done, seen.upto(up_done, 2))
                    take_high(high[UP], start + ahead, turn)
                    act.wait_ge(act_ready, seen.upto(act_ready))
                    squash_gate()
                    if not last:
                        take_high(high[GATE], start + ahead + 1, turn)
                    act.wait_ge(down_done, seen.upto(down_done))
                    take_high(high[DOWN], start + ahead + (1 if last else 2), turn)

                turns, rest = divmod(units - 2, RING // 3)
                per = RING // 3
                with seen.loop(act, turns, {up_done: 2 * per, act_ready: per, down_done: per,
                                            gate_clipped if layer == 0 else gate_done: 2 * per}) as i:
                    for u in range(per):
                        step(i, 4 + 3 * u)
                for u in range(rest):
                    step(None, 4 + turns * RING + 3 * u)
                step(None, 3 * units - 2, last=True)
                seen.upto(up_done, 2)
                seen.upto(act_ready)
                seen.upto(down_done, 2 if layer == 0 else 1)
                if layer == 0:
                    seen.upto(gate_done, 2 * UNITS[0])

            def edge_layer(n):
                layer = EDGE_LAYERS[n]
                rel, heads, width = layer["rel"], layer["heads"], layer["width"]
                tiles = heads * width // P
                if n % 2 == 0:
                    take_root(T)
                if n == 1:
                    copy_turned(wide_cols, 8, relu=True)
                else:
                    copy_turned(cols)
                for _ in range(rel):
                    copy_turned(wide_cols, tiles)
                count = rel * heads
                act.wait_ge(keys_turned, seen.upto(keys_turned))
                act.activation(key_rows[0:count, :], psum[0:count, 7, 0:N], ACT.Copy).then_inc(key_rows_ready, 1)
                items = [(t, h) for h in range(heads) for t in range(T)]
                act.wait_ge(keys_ready, seen.upto(keys_ready))

                def lift(i):
                    t, h = items[i]
                    act.wait_ge(picked, seen.upto(picked))
                    if i >= 2:
                        act.wait_ge(edge_exp_ready, seen.upto(edge_exp_ready))
                    for r in range(rel):
                        at = i % 2 * 1024 + r * N
                        ins = act.activation(edge_scores[i % 2][:, r * N:(r + 1) * N], flat[:, at:at + N],
                                             ACT.Identity, bias=queries_keys[:, t, r, h:h + 1])
                    ins.then_inc(lifted, 1)

                def exp_edges(i):
                    act.wait_ge(edge_max_ready, seen.upto(edge_max_ready))
                    act.activation(edge_exp[i % 2][:, 0:rel * N], edge_scores[i % 2][:, 0:rel * N], ACT.Exp,
                                   bias=edge_negmax[:, i % 2:i % 2 + 1]).then_inc(edge_exp_ready, 1)

                def copy_edges(i):
                    act.wait_ge(edges_turned, seen.upto(edges_turned))
                    at = 4 * 512
                    act.activation(edge_turned[i % 2][:, 0:rel * T, :].rearrange("p m n -> p (m n)"),
                                   flat[:, at:at + rel * T * P], ACT.Copy).then_inc(edges_copied, 1)

                last = len(items)
                for s in range(last + 2):
                    if s < last:
                        lift(s)
                    if 0 <= s - 1 < last:
                        exp_edges(s - 1)
                    if 0 <= s - 2 < last:
                        copy_edges(s - 2)
                act.wait_ge(edge_exp_ready, seen.upto(edge_exp_ready, 2))
                if n == 2:
                    act.wait_ge(exp_asked, seen.upto(exp_asked))
                    act.activation(wide_rows[:, :, 0:D], wide_rows[:, :, 0:D], ACT.Exp).then_inc(exp_ready, 1)

            def self_attention():
                take_root(T)
                take_root(T)
                copy_turned(cols, scale="norm1")
                for target in (head_q, head_k):
                    for b in range(3):
                        act.wait_ge(tile_done, seen.upto(tile_done))
                        act.activation(target[:, 2 * b:2 * b + 2, :].rearrange("p k n -> p (k n)"), psum[:, b, :],
                                       ACT.Copy).then_inc(heads_ready, 1)

                def exps(h):
                    act.wait_ge(head_max_ready, seen.upto(head_max_ready))
                    for t in range(T):
                        ins = act.activation(probs[h % 2][:, t, :], psum[:, h % 2, t * N:(t + 1) * N], ACT.Exp,
                                             bias=head_negmax[:, h % 2, t:t + 1], scale=HEAD ** -0.5,
                                             accum_out=head_sum[:, h % 2, t:t + 1])
                    ins.then_inc(probs_exp, 1)

                def copy_probs(h):
                    act.wait_ge(probs_done, seen.upto(probs_done))
                    act.activation(probs_turned[h % 2][:].rearrange("p t n -> p (t n)"), psum[:, 2 + h % 2, :],
                                   ACT.Copy).then_inc(probs_copied, 1)

                for s in range(HEADS + 1):
                    if s < HEADS:
                        exps(s)
                    if 0 <= s - 1 < HEADS:
                        copy_probs(s - 1)

            def l1_gnn():
                edge_layer(0)
                edge_layer(1)

            def l1_ffn():
                self_attention()
                experts(1)

            def l2_gnn():
                edge_layer(2)
                edge_layer(3)

            def l3_gnn():
                take_root(T)
                take_root(T)
                copy_turned(cols)

            def l3_ffn():
                take_root(T)
                take_root(T)
                take_root(SLOTS)
                copy_turned(cols)
                for target in (mixing[:], dispatch[:]):
                    act.wait_ge(exp_asked, seen.upto(exp_asked))
                    act.activation(target, target, ACT.Exp).then_inc(exp_ready, 1)

                def take_slot(n, turn=None, first=False):
                    if not first:
                        act.wait_ge(slot_used, seen.upto(slot_used))
                    take_high(slot_high[n % 3], SLOTS_AT + n, turn)

                for n in range(3):
                    take_slot(n, first=True)
                turns, rest = divmod(SLOTS - 3, RING)
                with seen.loop(act, turns, {slot_used: RING}) as i:
                    for a in range(RING):
                        take_slot(3 + a, i)
                for n in range(SLOTS - rest, SLOTS + 3):
                    take_slot(n)
                act.wait_ge(slot_pre, seen.upto(slot_pre))
                act.activation(slot_hidden[:], slot_hidden[:], ACT.Gelu).then_inc(slot_act, 1)
                with seen.loop(act, turns, {slot_used: RING}) as i:
                    for a in range(RING):
                        take_slot(SLOTS + 3 + a, i)
                for n in range(2 * SLOTS - rest, 2 * SLOTS):
                    take_slot(n)

            for stage in (l0_gnn, lambda: experts(0), l1_gnn, l1_ffn, l2_gnn, lambda: experts(2), l3_gnn,
                          l3_ffn):
                stage()

        @block.vector
        def _(dve):
            seen = Counts()

            def ask_root(n, p=P):
                dve.sem_inc(root_asked, 1)
                dve.wait_ge(root_ready, seen.upto(root_ready))

            def layernorm(target):
                for t in range(T):
                    for h in range(2):
                        dve.bn_stats(stats[:, t, h, :], x[:, t, h * HALF:(h + 1) * HALF]).then_inc(vector_wrote, 1)
                        dve.wait_ge(vector_wrote, seen.upto(vector_wrote))
                for t in range(T):
                    dve.bn_aggr(moments[:, t, :], stats[:, t, :, :].rearrange("p a b -> p (a b)"))\
                        .then_inc(vector_wrote, 1)
                    dve.wait_ge(vector_wrote, seen.upto(vector_wrote))
                dve.tensor_scalar(root[:, 0:T], moments[:, :, 1], 1e-5, None, ALU.add).then_inc(root_asked, 1)
                dve.wait_ge(root_ready, seen.upto(root_ready))
                dve.reciprocal(inverse[:], root[:, 0:T]).then_inc(vector_wrote, 1)
                dve.wait_ge(vector_wrote, seen.upto(vector_wrote))
                for t in range(T):
                    ins = dve.tensor_scalar(target[:, t, 0:D], x[:, t, :], moments[:, t, 0:1], inverse[:, t:t + 1],
                                            ALU.subtract, ALU.mult)
                return ins

            def count_edges():
                dve.wait_ge(edges_landed, seen.upto(edges_landed, 16))
                for n, target in ((0, edge_src), (1, edge_dst), (2, edge_key)):
                    dve.tensor_copy(target[:], edge_ints[:, n, :]).then_inc(vector_wrote, 1)
                    dve.wait_ge(vector_wrote, seen.upto(vector_wrote))
                dve.scalar_tensor_tensor(edge_key[:], edge_key[:], float(N), edge_dst[:], ALU.mult, ALU.add)\
                    .then_inc(vector_wrote, 1)
                dve.wait_ge(vector_wrote, seen.upto(vector_wrote))

                def hots(c, q):
                    dve.tensor_scalar(src_hot[q][:], key_iota[:, 0:N], edge_src[:, bass.ds(c, 1)], None, ALU.is_equal)
                    dve.tensor_scalar(key_hot[q][:], key_iota[:], edge_key[:, bass.ds(c, 1)], None, ALU.is_equal)\
                        .then_inc(hot_ready, 1)

                hots(0, 0)
                hots(1, 1)
                with seen.loop(dve, EDGE_TILES // 2 - 1, {hot_used: 2}) as i:
                    for q in range(2):
                        dve.wait_ge(hot_used, seen.upto(hot_used))
                        hots(i * 2 + (2 + q), q)
                seen.upto(hot_used, 2)
                dve.wait_ge(counted, seen.upto(counted))
                for t in range(T):
                    for j, c, n in row_parts(REL * N):
                        ins = dve.tensor_copy(raw_counts[:, t, c:c + n], row_bank(t, j, n))
                ins.then_inc(vector_wrote, 1)
                dve.wait_ge(vector_wrote, seen.upto(vector_wrote))
                dve.sem_inc(raw_ready, 1)
                for t in range(T):
                    dve.tensor_tensor(loop_counts[:, t, :], raw_counts[:, t, 0:N], raw_counts[:, t, N:2 * N],
                                      ALU.add).then_inc(vector_wrote, 1)
                    dve.wait_ge(vector_wrote, seen.upto(vector_wrote))
                    dve.tensor_tensor(loop_counts[:, t, :], loop_counts[:, t, :], raw_counts[:, t, 2 * N:3 * N],
                                      ALU.add).then_inc(vector_wrote, 1)
                    dve.wait_ge(vector_wrote, seen.upto(vector_wrote))
                    dve.tensor_tensor(loop_counts[:, t, node_tile(t)], loop_counts[:, t, node_tile(t)], ident[:],
                                      ALU.add).then_inc(vector_wrote, 1)
                    dve.wait_ge(vector_wrote, seen.upto(vector_wrote))
                dve.wait_ge(degree_done, seen.upto(degree_done))
                for j, c, n in row_parts(REL * N):
                    dve.tensor_scalar(in_degree[:, c:c + n], row_bank(0, j, n), 1.0, None, ALU.max)\
                        .then_inc(vector_wrote, 1)
                    dve.wait_ge(vector_wrote, seen.upto(vector_wrote))
                dve.reciprocal(in_degree[:], in_degree[:]).then_inc(vector_wrote, 1)
                dve.wait_ge(vector_wrote, seen.upto(vector_wrote))
                for t in range(T):
                    dve.tensor_tensor(mean_counts[:, t, :], raw_counts[:, t, :], in_degree[:], ALU.mult)\
                        .then_inc(vector_wrote, 1)
                    dve.wait_ge(vector_wrote, seen.upto(vector_wrote))
                dve.wait_ge(counts_turned, seen.upto(counts_turned))
                for b in range(3):
                    ins = dve.tensor_copy(flat_counts[:, 512 * b:512 * b + 512], psum[:, b, :])
                ins.then_inc(vector_wrote, 1)
                dve.wait_ge(vector_wrote, seen.upto(vector_wrote))
                dve.sem_inc(counts_ready, 1)

            def l0_gnn():
                dve.memset(tiny[:], 0.0).then_inc(vector_wrote, 1)
                dve.wait_ge(vector_wrote, seen.upto(vector_wrote))
                dve.memset(ones[:], 1.0).then_inc(ones_ready, 1)
                dve.wait_ge(constants_ready, seen.upto(constants_ready, 3))
                dve.wait_ge(small_landed, seen.upto(small_landed, 16))
                count_edges()
                dve.wait_ge(x_landed, seen.upto(x_landed, 16))
                layernorm(rows).then_inc(rows_ready, 1)
                dve.wait_ge(query_landed, seen.upto(query_landed, 16))
                for layer in range(2):
                    dve.wait_ge(rows_done, seen.upto(rows_done))
                    dve.wait_ge(bias_landed, seen.upto(bias_landed, 16))
                    for t in range(T):
                        for j, c, n in row_parts(D):
                            ins = dve.tensor_tensor(rows[:, t, c:c + n], row_bank(t, j, n), bias[:, c:c + n], ALU.add)
                    ins.then_inc(vector_wrote, 1)
                    dve.wait_ge(vector_wrote, seen.upto(vector_wrote))
                    dve.sem_inc(bias_used, 1)
                    dve.sem_inc(rows_ready, 1)

                    def weigh(c, q):
                        dve.wait_ge(chunk_squashed, seen.upto(chunk_squashed))
                        by_query = query_cols[:].rearrange("p k q -> p (k q)")[:, bass.ds(c * L, L)]\
                            .unsqueeze(1).broadcast_to([P, GROUP, L])
                        dve.tensor_tensor(chunk[q][:], chunk[q][:], by_query, ALU.mult).then_inc(chunk_weighted, 1)

                    def reduce(c, q):
                        dve.wait_ge(chunk_folded, seen.upto(chunk_folded))
                        dve.tensor_reduce(flat_gate[:, bass.ds(c * GROUP, WHOLE)], chunk[q][:, 0:WHOLE, :], AX_X,
                                          ALU.add)
                        nodes = GROUP - WHOLE
                        dve.tensor_reduce(flat_gate[:, bass.ds(c * GROUP + WHOLE, nodes)],
                                          psum[:, q, 0:nodes * 16].rearrange("p (n l) -> p n l", n=nodes), AX_X,
                                          ALU.add).then_inc(chunk_reduced, 1)

                    for c in range(2):
                        weigh(c, c)
                    with seen.loop(dve, CHUNKS // CHUNK_RING - 1,
                                   {chunk_squashed: CHUNK_RING, chunk_folded: CHUNK_RING}) as i:
                        for q in range(CHUNK_RING):
                            weigh(i * CHUNK_RING + (q + 2), (q + 2) % CHUNK_RING)
                            reduce(i * CHUNK_RING + q, q)
                    for c in range(CHUNKS - CHUNK_RING, CHUNKS):
                        if c + 2 < CHUNKS:
                            weigh(c + 2, (c + 2) % CHUNK_RING)
                        reduce(c, c % CHUNK_RING)
                    dve.wait_ge(tanh_ready, seen.upto(tanh_ready))
                    dve.tensor_tensor(flat_hidden, flat_hidden, flat_cols, ALU.subtract).then_inc(vector_wrote, 1)
                    dve.wait_ge(vector_wrote, seen.upto(vector_wrote))
                    dve.wait_ge(alpha_ready, seen.upto(alpha_ready, 6))
                    dve.tensor_tensor(flat_hidden, flat_hidden, alpha[:].rearrange("p k n -> p (k n)"), ALU.mult)\
                        .then_inc(vector_wrote, 1)
                    dve.wait_ge(vector_wrote, seen.upto(vector_wrote))
                    dve.tensor_tensor(flat_hidden, flat_hidden, flat_cols, ALU.add).then_inc(vector_wrote, 1)
                    dve.wait_ge(vector_wrote, seen.upto(vector_wrote))
                    dve.sem_inc(hidden_ready, 1)
                dve.wait_ge(turned_back, seen.upto(turned_back, 6))
                for b in range(3):
                    ins = dve.tensor_tensor(flat_x[:, 512 * b:512 * b + 512], flat_x[:, 512 * b:512 * b + 512],
                                            psum[:, b, :], ALU.add)
                ins.then_inc(vector_wrote, 1)
                dve.wait_ge(vector_wrote, seen.upto(vector_wrote))
                dve.sem_inc(arena_free, 1)

            def take_low(to, of, n):
                dve.wait_ge(high_ready, seen.upto(high_ready))
                dve.tensor_tensor(to[:], ring[n % RING][:], of[:].bitcast(F32), ALU.subtract).then_inc(ring_taken, 1)

            def take_logits(layer):
                count = EXPERTS[layer]
                scores = logits[:, :, 0:count]
                dve.wait_ge(logits_done, seen.upto(logits_done))
                of = psum[:, 3, 0:32].rearrange("p (t e) -> p t e", t=T)[:, :, 0:count]
                if layer == 0:
                    dve.tensor_tensor(scores, of, small_at("br", 0, 8).unsqueeze(1).broadcast_to([P, T, 8]),
                                      ALU.add).then_inc(vector_wrote, 1)
                    dve.wait_ge(vector_wrote, seen.upto(vector_wrote))
                    dve.sem_inc(logits_taken, 1)
                else:
                    dve.tensor_copy(scores, of).then_inc(vector_wrote, 1)
                    dve.wait_ge(vector_wrote, seen.upto(vector_wrote))
                    dve.sem_inc(logits_taken, 1)

            def route(layer):
                count = EXPERTS[layer]
                scores = logits[:, :, 0:count]
                if layer != 0:
                    dve.tensor_reduce(row_max[:], scores, AX_X, ALU.max).then_inc(vector_wrote, 1)
                    dve.wait_ge(vector_wrote, seen.upto(vector_wrote))
                    for t in range(T):
                        ins = dve.tensor_scalar(logits[:, t, 0:count], logits[:, t, 0:count], row_max[:, t:t + 1],
                                                None, ALU.subtract)
                    ins.then_inc(exp_asked, 1)
                    dve.wait_ge(exp_ready, seen.upto(exp_ready))
                    dve.tensor_reduce(row_sum[:], scores, AX_X, ALU.add).then_inc(vector_wrote, 1)
                    dve.wait_ge(vector_wrote, seen.upto(vector_wrote))
                    dve.reciprocal(row_sum[:], row_sum[:]).then_inc(vector_wrote, 1)
                    dve.wait_ge(vector_wrote, seen.upto(vector_wrote))
                    for t in range(T):
                        dve.tensor_scalar(logits[:, t, 0:count], logits[:, t, 0:count], row_sum[:, t:t + 1],
                                          None, ALU.mult).then_inc(vector_wrote, 1)
                        dve.wait_ge(vector_wrote, seen.upto(vector_wrote))
                for t in range(T):
                    dve.max(top[:, t, :], logits[:, t, 0:count]).then_inc(vector_wrote, 1)
                    dve.wait_ge(vector_wrote, seen.upto(vector_wrote))
                    dve.max_index(top_at[:, t, :], top[:, t, :], logits[:, t, 0:count]).then_inc(vector_wrote, 1)
                    dve.wait_ge(vector_wrote, seen.upto(vector_wrote))
                dve.tensor_copy(top_place[:], top_at[:]).then_inc(vector_wrote, 1)
                dve.wait_ge(vector_wrote, seen.upto(vector_wrote))
                if layer == 0:
                    dve.tensor_tensor(gap[:], top[:, :, 1], top[:, :, 0], ALU.subtract).then_inc(exp_asked, 1)
                    dve.wait_ge(exp_ready, seen.upto(exp_ready))
                    dve.tensor_scalar(row_sum[:], gap[:], 1.0, None, ALU.add).then_inc(vector_wrote, 1)
                    dve.wait_ge(vector_wrote, seen.upto(vector_wrote))
                    dve.reciprocal(top_weight[:, :, 0], row_sum[:]).then_inc(vector_wrote, 1)
                    dve.wait_ge(vector_wrote, seen.upto(vector_wrote))
                    dve.tensor_tensor(top_weight[:, :, 1], gap[:], top_weight[:, :, 0], ALU.mult)\
                        .then_inc(vector_wrote, 1)
                    dve.wait_ge(vector_wrote, seen.upto(vector_wrote))
                else:
                    dve.tensor_tensor(row_sum[:], top[:, :, 0], top[:, :, 1], ALU.add).then_inc(vector_wrote, 1)
                    dve.wait_ge(vector_wrote, seen.upto(vector_wrote))
                    dve.tensor_scalar(row_sum[:], row_sum[:], 1e-20 if layer == 1 else 1e-8, None, ALU.add)\
                        .then_inc(vector_wrote, 1)
                    dve.wait_ge(vector_wrote, seen.upto(vector_wrote))
                    dve.reciprocal(row_sum[:], row_sum[:]).then_inc(vector_wrote, 1)
                    dve.wait_ge(vector_wrote, seen.upto(vector_wrote))
                    for n in range(2):
                        dve.tensor_tensor(top_weight[:, :, n], top[:, :, n], row_sum[:], ALU.mult)\
                            .then_inc(vector_wrote, 1)
                        dve.wait_ge(vector_wrote, seen.upto(vector_wrote))
                for t in range(T):
                    for n, target in ((0, combine), (1, second)):
                        dve.tensor_scalar(target[:, t, 0:count], iota[:, 0:count], top_place[:, t, n:n + 1],
                                          top_weight[:, t, n:n + 1], ALU.is_equal, ALU.mult).then_inc(vector_wrote, 1)
                        dve.wait_ge(vector_wrote, seen.upto(vector_wrote))
                dve.tensor_tensor(combine[:, :, 0:count], combine[:, :, 0:count], second[:, :, 0:count], ALU.add)\
                    .then_inc(vector_wrote, 1)
                dve.wait_ge(vector_wrote, seen.upto(vector_wrote))
                if layer == 0:
                    pairs = unit_weight[:, :, 0:16].rearrange("p t (e h) -> p t e h", h=2)
                    for h in range(2):
                        dve.tensor_copy(pairs[:, :, :, h], combine[:, :, 0:8]).then_inc(vector_wrote, 1)
                        dve.wait_ge(vector_wrote, seen.upto(vector_wrote))
                    dve.sem_inc(combine_ready, 1)
                else:
                    dve.tensor_copy(unit_weight[:, :, 0:count], combine[:, :, 0:count]).then_inc(vector_wrote, 1)
                    dve.wait_ge(vector_wrote, seen.upto(vector_wrote))
                    dve.memset(unit_weight[:, :, count:count + 2], 1.0 if layer == 1 else 0.5)\
                        .then_inc(vector_wrote, 1)
                    dve.wait_ge(vector_wrote, seen.upto(vector_wrote))

            def experts(layer):
                if layer != 1:
                    layernorm(rows).then_inc(vector_wrote, 1)
                    dve.wait_ge(vector_wrote, seen.upto(vector_wrote))
                    dve.sem_inc(rows_ready, 1)
                units, start, per = UNITS[layer], UNITS_AT[layer], RING // 3
                take_low(low[GATE], high[GATE], start)
                dve.wait_ge(cols_high_ready, seen.upto(cols_high_ready))
                dve.tensor_tensor(cols_low[:], cols[:], cols_high[:].bitcast(F32), ALU.subtract)\
                    .then_inc(cols_split, 1)
                take_low(low[UP], high[UP], start + 1)
                take_logits(layer)

                def clip_gate(u):
                    for f in range(3):
                        if f != 1:
                            dve.wait_ge(gate_done, seen.upto(gate_done))
                        ins = dve.tensor_scalar(gate_part[:, f, :], unit_tile(0, f),
                                                small[:, bass.ds(u * 6 + (SMALL["unit_bias"][0] + f), 1)], 7.0,
                                                ALU.add, ALU.min)
                        if f > 0:
                            ins.then_inc(gate_clipped, 1)

                def activate(u):
                    if layer == 0:
                        for f in range(3):
                            if f != 1:
                                dve.wait_ge(up_done, seen.upto(up_done))
                            ins = dve.tensor_scalar(up_part[:, f, :], unit_tile(1, f),
                                                    small[:, bass.ds(u * 6 + (SMALL["unit_bias"][0] + 3 + f), 1)],
                                                    7.0, ALU.add, ALU.min)
                        ins.then_inc(vector_wrote, 1)
                        dve.wait_ge(vector_wrote, seen.upto(vector_wrote))
                        dve.tensor_scalar(up_part[:], up_part[:], -7.0, 1.0, ALU.max, ALU.add)
                        dve.wait_ge(squashed, seen.upto(squashed, 2))
                        dve.tensor_tensor(gate_part[:], gate_part[:], squash[:], ALU.mult).then_inc(vector_wrote, 1)
                        dve.wait_ge(vector_wrote, seen.upto(vector_wrote))
                        dve.tensor_tensor(act_cols[:], gate_part[:], up_part[:], ALU.mult).then_inc(vector_wrote, 1)
                    else:
                        for last, tiles in ((0, slice(0, 2)), (1, slice(2, 3))):
                            dve.wait_ge(squashed, seen.upto(squashed))
                            dve.wait_ge(up_done, seen.upto(up_done))
                            ins = dve.tensor_tensor(act_cols[:, tiles, :].rearrange("p f n -> p (f n)"),
                                                    squash[:, tiles, :].rearrange("p f n -> p (f n)"),
                                                    unit_bank(1, last), ALU.mult)
                        ins.then_inc(vector_wrote, 1)
                    dve.wait_ge(vector_wrote, seen.upto(vector_wrote))
                    dve.tensor_copy(act_high[:], act_cols[:]).then_inc(vector_wrote, 1)
                    dve.wait_ge(vector_wrote, seen.upto(vector_wrote))
                    dve.tensor_tensor(act_low[:], act_cols[:], act_high[:].bitcast(F32), ALU.subtract)\
                        .then_inc(act_ready, 1)

                def add_unit(u):
                    for t in range(T):
                        for j, c, n in row_parts(D):
                            ins = dve.scalar_tensor_tensor(x[:, t, c:c + n], row_bank(t, j, n),
                                                           unit_weight[:, t, bass.ds(u, 1)], x[:, t, c:c + n],
                                                           ALU.mult, ALU.add)
                    ins.then_inc(down_taken, 1)

                def step(u, ahead, last=False):
                    take_low(low[UP], high[UP], start + ahead)
                    if layer == 0:
                        clip_gate(u + 1)
                    if not last:
                        take_low(low[GATE], high[GATE], start + ahead + 1)
                    dve.wait_ge(down_done, seen.upto(down_done))
                    take_low(low[DOWN], high[DOWN], start + ahead + (1 if last else 2))
                    add_unit(u)
                    activate(u + 1)

                if layer == 0:
                    clip_gate(0)
                take_low(low[GATE], high[GATE], start + 2)
                take_low(low[DOWN], high[DOWN], start + 3)
                activate(0)
                route(layer)
                turns, rest = divmod(units - 2, per)
                grows = {squashed: 2 * per, up_done: 2 * per, down_done: per, high_ready: 3 * per}
                if layer == 0:
                    grows |= {gate_done: 2 * per, vector_wrote: 4 * per}
                else:
                    grows |= {vector_wrote: 2 * per}
                with seen.loop(dve, turns, grows) as i:
                    for q in range(per):
                        step(i * per + q, 4 + 3 * q)
                for u in range(turns * per, units - 2):
                    step(u, 4 + 3 * u)
                step(units - 2, 3 * units - 2, last=True)
                dve.wait_ge(down_done, seen.upto(down_done))
                add_unit(units - 1)
                if layer == 0:
                    dve.wait_ge(combine_turned, seen.upto(combine_turned))
                    dve.tensor_copy(combine_cols[0:8, :], psum[0:8, 6, 0:N]).then_inc(combine_cols_ready, 1)
                    dve.wait_ge(down_done, seen.upto(down_done))
                    for t in range(T):
                        for j, c, n in row_parts(D):
                            ins = dve.tensor_tensor(x[:, t, c:c + n], x[:, t, c:c + n], row_bank(t, j, n), ALU.add)
                    ins.then_inc(down_taken, 1)
                dve.wait_ge(down_taken, seen.upto(down_taken, units + (1 if layer == 0 else 0)))
                if layer == 2:
                    dve.sem_inc(arena_free, 1)

            def edge_layer(n):
                layer = EDGE_LAYERS[n]
                rel, heads, width = layer["rel"], layer["heads"], layer["width"]
                out_width = heads * width
                messages = message_rows(layer)
                if n == 0:
                    for t in range(T):
                        dve.tensor_tensor(all_counts[:, t, :], counts[:, t, 0, :], counts[:, t, 1, :], ALU.add)\
                            .then_inc(vector_wrote, 1)
                        dve.wait_ge(vector_wrote, seen.upto(vector_wrote))
                        dve.tensor_tensor(all_counts[:, t, :], all_counts[:, t, :], counts[:, t, 2, :], ALU.add)\
                            .then_inc(vector_wrote, 1)
                        dve.wait_ge(vector_wrote, seen.upto(vector_wrote))
                        dve.tensor_scalar(absent[:, t, 0:N], all_counts[:, t, :], 0.0, LOW, ALU.is_equal,
                                          ALU.mult).then_inc(vector_wrote, 1)
                        dve.wait_ge(vector_wrote, seen.upto(vector_wrote))
                        dve.tensor_reduce(dinv[:, t:t + 1], all_counts[:, t, :], AX_X, ALU.add)\
                            .then_inc(vector_wrote, 1)
                        dve.wait_ge(vector_wrote, seen.upto(vector_wrote))
                    dve.tensor_scalar(dinv[:], dinv[:], 1.0, None, ALU.add).then_inc(vector_wrote, 1)
                    dve.wait_ge(vector_wrote, seen.upto(vector_wrote))
                if n == 2:
                    for t in range(T):
                        dve.tensor_scalar(absent[:, t, :], counts[:, t].rearrange("p r n -> p (r n)"), 0.0, LOW,
                                          ALU.is_equal, ALU.mult).then_inc(vector_wrote, 1)
                        dve.wait_ge(vector_wrote, seen.upto(vector_wrote))
                if n % 2 == 0:
                    layernorm(rows).then_inc(vector_wrote, 1)
                    dve.wait_ge(vector_wrote, seen.upto(vector_wrote))
                    dve.sem_inc(rows_ready, 1)
                for r in range(rel):
                    dve.wait_ge(rows_done, seen.upto(rows_done))
                    for t in range(T):
                        for j, c, size in row_parts(out_width):
                            ins = dve.tensor_copy(messages[:, r, t, c:c + size], row_bank(t, j, size))
                    ins.then_inc(vector_wrote, 1)
                    dve.wait_ge(vector_wrote, seen.upto(vector_wrote))
                    dve.sem_inc(rows_ready, 1)
                dve.wait_ge(query_keys_done, seen.upto(query_keys_done))
                dve.tensor_copy(queries_keys[:, :, 0:rel, 0:2 * heads],
                                psum[:, 7, 0:T * rel * 16].rearrange("p (t r c) -> p t r c", t=T, r=rel)
                                [:, :, :, 0:2 * heads]).then_inc(vector_wrote, 1)
                dve.wait_ge(vector_wrote, seen.upto(vector_wrote))
                for t in range(T):
                    dve.tensor_copy(keys[:, t, 0:rel * heads].rearrange("p (r h) -> p r h", r=rel),
                                    queries_keys[:, t, 0:rel, heads:2 * heads]).then_inc(vector_wrote, 1)
                    dve.wait_ge(vector_wrote, seen.upto(vector_wrote))
                dve.sem_inc(keys_ready, 1)
                dve.wait_ge(bias_landed, seen.upto(bias_landed, 16))
                target = wide_rows if n == 0 else rows
                items = [(t, h) for h in range(heads) for t in range(T)]

                def highest(i):
                    t, h = items[i]
                    scores = edge_scores[i % 2][:, 0:rel * N]
                    dve.wait_ge(lifted, seen.upto(lifted))
                    dve.scalar_tensor_tensor(scores, scores, 0.2, scores, ALU.mult, ALU.max).then_inc(vector_wrote, 1)
                    dve.wait_ge(vector_wrote, seen.upto(vector_wrote))
                    dve.tensor_tensor_reduce(scores, scores, absent[:, t, 0:rel * N], 1.0, -3e38, ALU.add,
                                             ALU.max, edge_max[:, i % 2:i % 2 + 1]).then_inc(vector_wrote, 1)
                    dve.wait_ge(vector_wrote, seen.upto(vector_wrote))
                    dve.tensor_scalar(edge_negmax[:, i % 2:i % 2 + 1], edge_max[:, i % 2:i % 2 + 1], -1.0, None,
                                      ALU.mult).then_inc(edge_max_ready, 1)

                def weigh(i):
                    t, h = items[i]
                    by = all_counts[:, t, :] if rel == 1 else counts[:, t].rearrange("p r n -> p (r n)")
                    q = i % 4
                    dve.wait_ge(edge_exp_ready, seen.upto(edge_exp_ready))
                    dve.tensor_tensor_reduce(edge_exp[i % 2][:, 0:rel * N], edge_exp[i % 2][:, 0:rel * N], by,
                                             1.0, 0.0, ALU.mult, ALU.add, edge_sum[:, q:q + 1])\
                        .then_inc(vector_wrote, 1)
                    dve.wait_ge(vector_wrote, seen.upto(vector_wrote))
                    dve.sem_inc(edge_weighted, 1)
                    dve.tensor_scalar(edge_sum[:, q:q + 1], edge_sum[:, q:q + 1], 1e-16, None, ALU.add)\
                        .then_inc(vector_wrote, 1)
                    dve.wait_ge(vector_wrote, seen.upto(vector_wrote))
                    dve.reciprocal(edge_inverse[:, q:q + 1], edge_sum[:, q:q + 1]).then_inc(vector_wrote, 1)
                    dve.wait_ge(vector_wrote, seen.upto(vector_wrote))

                def store(i):
                    t, h = items[i]
                    q = i % 4
                    dve.wait_ge(mixed, seen.upto(mixed))
                    for j, c, size in row_parts(width):
                        bank = 6 + j if width > 512 else 6 + i % 2
                        at = h * width + c
                        ins = dve.scalar_tensor_tensor(target[:, t, at:at + size], psum[:, bank, 0:size],
                                                       edge_inverse[:, q:q + 1], bias[:, at:at + size], ALU.mult,
                                                       ALU.add)
                    ins.then_inc(vector_wrote, 1)
                    dve.wait_ge(vector_wrote, seen.upto(vector_wrote))
                    dve.sem_inc(stored, 1)

                last = len(items)
                for s in range(last + 3):
                    if s < last:
                        highest(s)
                    if 0 <= s - 1 < last:
                        weigh(s - 1)
                    if 0 <= s - 3 < last:
                        store(s - 3)
                dve.sem_inc(bias_used, 1)
                if n == 0:
                    dve.sem_inc(rows_ready, 1)
                elif n == 2:
                    dve.tensor_scalar(wide_rows[:, :, 0:D], rows[:], 0.0, None, ALU.min).then_inc(exp_asked, 1)
                    dve.tensor_scalar(rows[:], rows[:], 0.0, None, ALU.max).then_inc(vector_wrote, 1)
                    dve.wait_ge(vector_wrote, seen.upto(vector_wrote))
                    dve.wait_ge(exp_ready, seen.upto(exp_ready))
                    dve.scalar_tensor_tensor(rows[:], wide_rows[:, :, 0:D], -1.0, rows[:], ALU.add, ALU.add)\
                        .then_inc(vector_wrote, 1)
                    dve.wait_ge(vector_wrote, seen.upto(vector_wrote))
                    dve.sem_inc(rows_ready, 1)
                else:
                    dve.tensor_tensor(x[:], x[:], rows[:], ALU.add).then_inc(vector_wrote, 1)
                    dve.wait_ge(vector_wrote, seen.upto(vector_wrote))

            def rms_rows(target, source):
                for t in range(T):
                    dve.tensor_tensor_reduce(normed[:, t, :], source[:, t, :], source[:, t, :], 1.0, 0.0,
                                             ALU.mult, ALU.add, root[:, t:t + 1]).then_inc(vector_wrote, 1)
                    dve.wait_ge(vector_wrote, seen.upto(vector_wrote))
                dve.tensor_scalar(root[:, 0:T], root[:, 0:T], 1.0 / D, 1e-6, ALU.mult, ALU.add)\
                    .then_inc(root_asked, 1)
                dve.wait_ge(root_ready, seen.upto(root_ready))
                dve.reciprocal(inverse[:], root[:, 0:T]).then_inc(vector_wrote, 1)
                dve.wait_ge(vector_wrote, seen.upto(vector_wrote))
                for t in range(T):
                    dve.tensor_scalar(target[:, t, :], source[:, t, :], inverse[:, t:t + 1], None, ALU.mult)\
                        .then_inc(vector_wrote, 1)
                    dve.wait_ge(vector_wrote, seen.upto(vector_wrote))
                dve.sem_inc(rows_ready, 1)

            def self_attention():
                layernorm(rows).then_inc(vector_wrote, 1)
                dve.wait_ge(vector_wrote, seen.upto(vector_wrote))
                rms_rows(normed, rows)
                dve.wait_ge(rows_done, seen.upto(rows_done))
                for t in range(T):
                    for j, c, n in row_parts(D):
                        ins = dve.tensor_copy(values[:, t, c:c + n], row_bank(t, j, n))
                ins.then_inc(vector_wrote, 1)
                dve.wait_ge(vector_wrote, seen.upto(vector_wrote))
                dve.sem_inc(rows_ready, 1)

                def highest(h):
                    q = h % 2
                    dve.wait_ge(scored, seen.upto(scored))
                    dve.tensor_reduce(head_max[:, q, :], psum[:, q, :].rearrange("p (t n) -> p t n", t=T), AX_X,
                                      ALU.max).then_inc(vector_wrote, 1)
                    dve.wait_ge(vector_wrote, seen.upto(vector_wrote))
                    dve.tensor_scalar(head_negmax[:, q, :], head_max[:, q, :], -HEAD ** -0.5, None, ALU.mult)\
                        .then_inc(head_max_ready, 1)

                def normalise(h):
                    q = h % 2
                    dve.wait_ge(probs_exp, seen.upto(probs_exp))
                    dve.reciprocal(head_inverse[:, q, :], head_sum[:, q, :]).then_inc(vector_wrote, 1)
                    dve.wait_ge(vector_wrote, seen.upto(vector_wrote))
                    for t in range(T):
                        ins = dve.tensor_scalar(probs[q][:, t, :], probs[q][:, t, :], head_inverse[:, q, t:t + 1],
                                                None, ALU.mult)
                    ins.then_inc(probs_ready, 1)

                def store(h):
                    at = h % 2 * HEAD
                    dve.wait_ge(context_done, seen.upto(context_done))
                    dve.tensor_copy(context[at:at + HEAD, h // 2, :], psum[at:at + HEAD, 4 + h % 2, 0:N])\
                        .then_inc(vector_wrote, 1)
                    dve.wait_ge(vector_wrote, seen.upto(vector_wrote))
                    dve.sem_inc(context_ready, 1)

                for s in range(HEADS + 2):
                    if s < HEADS:
                        highest(s)
                    if 0 <= s - 1 < HEADS:
                        normalise(s - 1)
                    if 0 <= s - 2 < HEADS:
                        store(s - 2)
                dve.wait_ge(rows_done, seen.upto(rows_done))
                for t in range(T):
                    for j, c, n in row_parts(D):
                        ins = dve.tensor_tensor(rows[:, t, c:c + n], rows[:, t, c:c + n], row_bank(t, j, n), ALU.add)
                ins.then_inc(vector_wrote, 1)
                dve.wait_ge(vector_wrote, seen.upto(vector_wrote))
                dve.tensor_tensor(x[:], x[:], rows[:], ALU.add).then_inc(vector_wrote, 1)
                dve.wait_ge(vector_wrote, seen.upto(vector_wrote))
                rms_rows(rows, rows)

            def l1_gnn():
                edge_layer(0)
                edge_layer(1)

            def l1_ffn():
                self_attention()
                experts(1)

            def l2_gnn():
                edge_layer(2)
                edge_layer(3)

            def l3_gnn():
                dve.tensor_copy(root[:, 0:T], dinv[:]).then_inc(vector_wrote, 1)
                dve.wait_ge(vector_wrote, seen.upto(vector_wrote))
                dve.sem_inc(root_asked, 1)
                dve.wait_ge(root_ready, seen.upto(root_ready))
                dve.reciprocal(dinv[:], root[:, 0:T]).then_inc(vector_wrote, 1)
                dve.wait_ge(vector_wrote, seen.upto(vector_wrote))
                layernorm(rows).then_inc(vector_wrote, 1)
                dve.wait_ge(vector_wrote, seen.upto(vector_wrote))
                dve.sem_inc(rows_ready, 1)
                dve.wait_ge(rows_done, seen.upto(rows_done))
                for t in range(T):
                    for j, c, n in row_parts(D):
                        ins = dve.tensor_scalar(rows[:, t, c:c + n], row_bank(t, j, n), dinv[:, t:t + 1], None,
                                                ALU.mult)
                ins.then_inc(vector_wrote, 1)
                dve.wait_ge(vector_wrote, seen.upto(vector_wrote))
                dve.sem_inc(rows_ready, 1)
                dve.wait_ge(rows_done, seen.upto(rows_done))
                dve.wait_ge(bias_landed, seen.upto(bias_landed, 16))
                for t in range(T):
                    for j, c, n in row_parts(D):
                        ins = dve.scalar_tensor_tensor(rows[:, t, c:c + n], row_bank(t, j, n), dinv[:, t:t + 1],
                                                       bias[:, c:c + n], ALU.mult, ALU.add)
                ins.then_inc(vector_wrote, 1)
                dve.wait_ge(vector_wrote, seen.upto(vector_wrote))
                dve.sem_inc(bias_used, 1)
                dve.tensor_tensor(x[:], x[:], rows[:], ALU.add).then_inc(vector_wrote, 1)
                dve.wait_ge(vector_wrote, seen.upto(vector_wrote))

            def l3_ffn():
                layernorm(rows).then_inc(vector_wrote, 1)
                dve.wait_ge(vector_wrote, seen.upto(vector_wrote))
                for t in range(T):
                    dve.tensor_tensor_reduce(squares[:], rows[:, t, :], rows[:, t, :], 1.0, 0.0, ALU.mult,
                                             ALU.add, root[:, t:t + 1]).then_inc(vector_wrote, 1)
                    dve.wait_ge(vector_wrote, seen.upto(vector_wrote))
                dve.sem_inc(root_asked, 1)
                dve.wait_ge(root_ready, seen.upto(root_ready))
                dve.tensor_scalar(root[:, 0:T], root[:, 0:T], 1e-12, None, ALU.max).then_inc(vector_wrote, 1)
                dve.wait_ge(vector_wrote, seen.upto(vector_wrote))
                dve.reciprocal(inverse[:], root[:, 0:T]).then_inc(vector_wrote, 1)
                dve.wait_ge(vector_wrote, seen.upto(vector_wrote))
                for t in range(T):
                    dve.tensor_scalar(rows[:, t, :], rows[:, t, :], inverse[:, t:t + 1], None, ALU.mult)\
                        .then_inc(vector_wrote, 1)
                    dve.wait_ge(vector_wrote, seen.upto(vector_wrote))
                dve.sem_inc(rows_ready, 1)
                dve.wait_ge(slots_landed, seen.upto(slots_landed, 48))
                dve.tensor_tensor(phi_squares[:], phi[:], phi[:], ALU.mult).then_inc(vector_wrote, 1)
                dve.wait_ge(vector_wrote, seen.upto(vector_wrote))
                dve.sem_inc(phi_squared, 1)
                dve.wait_ge(phi_summed, seen.upto(phi_summed))
                dve.tensor_copy(root[:], psum[:, 7, 0:SLOTS]).then_inc(root_asked, 1)
                dve.wait_ge(root_ready, seen.upto(root_ready))
                dve.tensor_scalar(phi_scale[:], root[:], 1e-12, None, ALU.max).then_inc(vector_wrote, 1)
                dve.wait_ge(vector_wrote, seen.upto(vector_wrote))
                dve.reciprocal(phi_scale[:], phi_scale[:]).then_inc(vector_wrote, 1)
                dve.wait_ge(vector_wrote, seen.upto(vector_wrote))
                dve.tensor_scalar(phi_scale[:], phi_scale[:], small_at("scale"), None, ALU.mult)\
                    .then_inc(vector_wrote, 1)
                dve.wait_ge(vector_wrote, seen.upto(vector_wrote))
                dve.tensor_tensor(phi[:], phi[:], phi_scale[:].unsqueeze(1).broadcast_to([P, K, SLOTS]),
                                  ALU.mult).then_inc(vector_wrote, 1)
                dve.wait_ge(vector_wrote, seen.upto(vector_wrote))
                dve.sem_inc(phi_ready, 1)
                dve.wait_ge(slot_logits_done, seen.upto(slot_logits_done))
                dve.tensor_reduce(soft[:, 0:2], psum[:, 3, 0:T * SLOTS].rearrange("p (t n) -> p t n", t=T), AX_X,
                                  ALU.max).then_inc(vector_wrote, 1)
                dve.wait_ge(vector_wrote, seen.upto(vector_wrote))
                for t in range(T):
                    ins = dve.tensor_scalar(mixing[:, t, :], psum[:, 3, t * SLOTS:(t + 1) * SLOTS], soft[:, t:t + 1],
                                            None, ALU.subtract)
                ins.then_inc(vector_wrote, 1)
                dve.wait_ge(vector_wrote, seen.upto(vector_wrote))
                dve.sem_inc(exp_asked, 1)
                dve.tensor_reduce(soft[0:SLOTS, 2:3], psum[0:SLOTS, 4, 0:N], AX_X, ALU.max).then_inc(vector_wrote, 1)
                dve.wait_ge(vector_wrote, seen.upto(vector_wrote))
                dve.tensor_scalar(dispatch[:], psum[0:SLOTS, 4, 0:N], soft[0:SLOTS, 2:3], None, ALU.subtract)\
                    .then_inc(exp_asked, 1)
                dve.wait_ge(exp_ready, seen.upto(exp_ready))
                dve.tensor_reduce(soft[:, 4:6], mixing[:], AX_X, ALU.add).then_inc(vector_wrote, 1)
                dve.wait_ge(vector_wrote, seen.upto(vector_wrote))
                dve.reciprocal(soft[:, 4:6], soft[:, 4:6]).then_inc(vector_wrote, 1)
                dve.wait_ge(vector_wrote, seen.upto(vector_wrote))
                for t in range(T):
                    for h in range(2):
                        dve.tensor_scalar(mixing_pair[:, t, h, :], mixing[:, t, :], soft[:, 4 + t:5 + t], None,
                                          ALU.mult)
                dve.wait_ge(exp_ready, seen.upto(exp_ready))
                dve.tensor_reduce(soft[0:SLOTS, 6:7], dispatch[:], AX_X, ALU.add).then_inc(vector_wrote, 1)
                dve.wait_ge(vector_wrote, seen.upto(vector_wrote))
                dve.reciprocal(soft[0:SLOTS, 6:7], soft[0:SLOTS, 6:7]).then_inc(vector_wrote, 1)
                dve.wait_ge(vector_wrote, seen.upto(vector_wrote))
                dve.tensor_scalar(dispatch[:], dispatch[:], soft[0:SLOTS, 6:7], None, ALU.mult)\
                    .then_inc(soft_ready, 1)
                dve.wait_ge(soft_turned, seen.upto(soft_turned))
                dve.tensor_copy(mixing_cols[:], psum[0:SLOT_PAIR, 5, 0:N])
                dve.tensor_copy(dispatch_rows[:].rearrange("p t n -> p (t n)"), psum[:, 6, 0:T * SLOTS])\
                    .then_inc(soft_copied, 1)
                dve.wait_ge(slot_in_done, seen.upto(slot_in_done))
                dve.tensor_copy(slot_in[:].rearrange("p k n -> p (k n)"), psum[:, 7, 0:K * SLOTS])\
                    .then_inc(vector_wrote, 1)
                dve.wait_ge(vector_wrote, seen.upto(vector_wrote))

                dve.tensor_tensor(slot_fold[:], ident[:, 0:SLOTS], ident[:, SLOTS:SLOT_PAIR], ALU.add)

                def pair(source, tiles):
                    dve.tensor_copy(slot_pair[:, 0:tiles, 0:SLOTS], source[:]).then_inc(vector_wrote, 1)
                    dve.wait_ge(vector_wrote, seen.upto(vector_wrote))
                    dve.tensor_tensor(slot_pair[:, 0:tiles, SLOTS:SLOT_PAIR], source[:],
                                      slot_pair[:, 0:tiles, 0:SLOTS].bitcast(F32), ALU.subtract)\
                        .then_inc(vector_wrote, 1)
                    dve.wait_ge(vector_wrote, seen.upto(vector_wrote))

                def mask(slot, q, tiles):
                    both = "p k (h n) -> p (k h) n"
                    dve.scalar_tensor_tensor(slot_mask[q][:, 0:tiles, :].rearrange(both, h=2),
                                             iota[:].unsqueeze(1).broadcast_to([P, 2 * tiles, SLOTS]),
                                             iota[:, bass.ds(slot, 1)],
                                             slot_pair[:, 0:tiles, :].bitcast(F32).rearrange(both, h=2),
                                             ALU.is_equal, ALU.mult).then_inc(mask_ready, 1)

                def take_slot(n, first=False):
                    if not first:
                        dve.wait_ge(slot_used, seen.upto(slot_used))
                    take_low(slot_low[n % 3], slot_high[n % 3], SLOTS_AT + n)

                turns, rest = divmod(SLOTS - 3, RING)

                def slots(at, tiles):
                    with seen.loop(dve, turns, {slot_used: RING, high_ready: RING}) as i:
                        for a in range(RING):
                            take_slot(at + 3 + a)
                            mask(i * RING + (3 + a), (at + a) % 3, tiles)
                    for n in range(SLOTS - rest, SLOTS):
                        take_slot(at + n)
                        mask(n, (at + n) % 3, tiles)

                pair(slot_in, K)
                for n in range(3):
                    take_slot(n, first=True)
                    mask(n, n, K)
                slots(0, K)
                for n in range(3):
                    take_slot(SLOTS + n)
                dve.wait_ge(slot_sums_done, seen.upto(slot_sums_done))
                dve.tensor_copy(slot_sum[:], psum[:, 3, 0:SLOT_HIDDEN]).then_inc(slot_sums_ready, 1)
                dve.wait_ge(slot_folded, seen.upto(slot_folded))
                dve.tensor_tensor(slot_hidden[:].rearrange("p k n -> p (k n)"), psum[:, 5, 0:3 * SLOTS],
                                  slot_b1[:].rearrange("p k n -> p (k n)"), ALU.add).then_inc(slot_pre, 1)
                dve.wait_ge(slot_act, seen.upto(slot_act))
                pair(slot_hidden, 3)
                for n in range(3):
                    mask(n, (SLOTS + n) % 3, 3)
                slots(SLOTS, 3)
                dve.wait_ge(slot_out_done, seen.upto(slot_out_done))
                for j, c, n in row_parts(D):
                    ins = dve.tensor_tensor(slot_out[:, c:c + n], psum[:, 3 + j, 0:n], slot_b2[:, c:c + n], ALU.add)
                ins.then_inc(slot_out_ready, 1)
                dve.wait_ge(rows_done, seen.upto(rows_done))
                for t in range(T):
                    for j, c, n in row_parts(D):
                        ins = dve.tensor_tensor(x[:, t, c:c + n], x[:, t, c:c + n], row_bank(t, j, n), ALU.add)
                ins.then_inc(vector_wrote, 1)
                dve.wait_ge(vector_wrote, seen.upto(vector_wrote))

            for stage in (l0_gnn, lambda: experts(0), l1_gnn, l1_ffn, l2_gnn, lambda: experts(2), l3_gnn,
                          l3_ffn):
                stage()
            dve.sem_inc(x_final, 1)



def _by_columns(w):
    w = w.reshape(K, P, D)
    return [w[:, :, h * HALF:(h + 1) * HALF].transpose(1, 0, 2).reshape(P, -1) for h in range(2)]


def _by_rows(w, pieces=((0, 3), (3, 6))):
    w = w.reshape(-1, P, w.shape[1])
    return [w[a:b].transpose(1, 0, 2).reshape(P, -1) for a, b in pieces]


def _unit(gate, up, down):
    return [gate.reshape(K, P, HALF).transpose(1, 0, 2).reshape(P, -1),
            up.reshape(K, P, HALF).transpose(1, 0, 2).reshape(P, -1)] + _by_rows(down, ((0, 3),))


def _in_order(units):
    pieces = [units[0][GATE], units[0][UP]]
    for unit, after in zip(units, units[1:]):
        pieces += [after[GATE], unit[DOWN], after[UP]]
    return pieces + [units[-1][DOWN]]


def _stream(a):
    pieces = _by_columns(a["L0_gnn_Wg"][:, D:].T)
    for n in (1, 2):
        pieces += _by_rows(a[f"L0_gnn_W_root{n}"])
        for r in range(REL):
            pieces += _by_rows(a[f"L0_gnn_W_rel{n}"][r])
        pieces += _by_columns(a["L0_gnn_Wg"][:, :D].T)
        hidden, query = _by_columns(a["L0_gnn_Wq"][:, :D].T), _by_columns(a["L0_gnn_Wq"][:, D:].T)
        pieces += [hidden[0], query[0], hidden[1], query[1]]
    units = []
    for e in range(8):
        for h in range(2):
            cut = slice(h * HALF, (h + 1) * HALF)
            units.append(_unit(a["L0_ffn_Wgu"][e][:, :D][:, cut], a["L0_ffn_Wgu"][e][:, D:][:, cut],
                               a["L0_ffn_Wd"][e][cut]))
    pieces += _in_order(units)
    pieces += _by_rows(a["L1_gnn_W1"].T, EDGE_LAYERS[0]["pieces"])
    pieces += _by_rows(a["L1_gnn_W2"].T, EDGE_LAYERS[1]["pieces"])
    pieces += _by_columns(a["L1_ffn_Wq"].T) + _by_columns(a["L1_ffn_Wk"].T)
    pieces += _by_rows(a["L1_ffn_Wv"].T) + _by_rows(a["L1_ffn_Wo"].T)
    units = []
    for e in range(8):
        units.append(_unit(a["L1_ffn_Weg"][e].T, a["L1_ffn_Weu"][e].T, a["L1_ffn_Wed"][e].T))
    for h in range(2):
        cut = slice(h * HALF, (h + 1) * HALF)
        units.append(_unit(a["L1_ffn_Wsg"][cut].T, a["L1_ffn_Wsu"][cut].T, a["L1_ffn_Wsd"].T[cut]))
    pieces += _in_order(units)
    for n in (1, 2):
        for r in range(REL):
            pieces += _by_rows(a[f"L2_gnn_W{n}"][r])
    units = [_unit(a["L2_ffn_wg"][e], a["L2_ffn_wu"][e], a["L2_ffn_wd"][e]) for e in range(16)]
    units += [_unit(a["L2_ffn_shared_wg"][e], a["L2_ffn_shared_wu"][e], a["L2_ffn_shared_wd"][e]) for e in range(2)]
    pieces += _in_order(units)
    pieces += _by_rows(a["L3_gnn_W"])
    for n in range(SLOTS):
        pieces += [a["L3_ffn_w1"][n].reshape(K, P, SLOT_HIDDEN).transpose(1, 0, 2).reshape(P, -1)]
    for n in range(SLOTS):
        pieces += _by_rows(a["L3_ffn_w2"][n], ((0, 3),))
    return pieces


def _small(a, np):
    def cols(v):
        return v.reshape(-1, P).T

    def tiled(m):
        return m.reshape(-1, P, m.shape[1]).transpose(1, 0, 2).reshape(P, -1)

    bgu = a["L0_ffn_bgu"].reshape(8, 2, 2, 3, P)
    att = np.zeros((8, P, 16), np.float32)
    for h in range(8):
        att[h, :, h] = a["L1_gnn_att_dst1"][h]
        att[h, :, 8 + h] = a["L1_gnn_att_src1"][h]
    parts = {
        "bg": cols(a["L0_gnn_bg"]), "bq": cols(a["L0_gnn_bq"]),
        "unit_bias": bgu.transpose(4, 0, 2, 1, 3).reshape(P, -1),
        "norm1": cols(a["L1_ffn_norm1_w"]), "norm2": cols(a["L1_ffn_norm2_w"]),
        "router0": tiled(a["L0_ffn_Wr"]), "router1": tiled(a["L1_ffn_gate_w"].T),
        "router2": tiled(a["L2_ffn_gate_w"].T),
        "br": np.broadcast_to(a["L0_ffn_br"], (P, 8)), "scale": np.broadcast_to(a["L3_ffn_scale"], (P, 1)),
        "att0": att.transpose(1, 0, 2).reshape(P, -1),
        "att1": tiled(np.stack([a["L1_gnn_att_dst2"][0], a["L1_gnn_att_src2"][0]], axis=1)),
        "att2": tiled(np.concatenate([a["L2_gnn_q1"], a["L2_gnn_k1"]], axis=1)),
        "att3": tiled(np.concatenate([a["L2_gnn_q2"], a["L2_gnn_k2"]], axis=1)),
    }
    assert all(parts[n].shape == (P, width) for n, (_, width) in SMALL.items())
    return np.concatenate([parts[n] for n in SMALL], axis=1)


def kernel(**inputs):
    import concourse.bacc as bacc
    import numpy as np
    from concourse.bass_utils import run_bass_kernel_spmd

    a = {name: np.asarray(value) for name, value in inputs.items()}
    pieces = _stream(a)
    assert len(pieces) == STREAM
    stream = np.zeros((STREAM, P, PIECE), np.float32)
    for n, piece in enumerate(pieces):
        stream[n, :, :piece.shape[1]] = piece
    edges = np.stack([a["src"], a["dst"], a["edge_type_3"]]).reshape(3, EDGE_TILES, P).transpose(2, 0, 1)
    query = a["L0_gnn_query_embs"].reshape(B * L, K, P).transpose(2, 1, 0)
    rows = [a[n] for n in ("L0_gnn_b1", "L0_gnn_b2", "L1_gnn_b1", "L1_gnn_b2", "L2_gnn_b1", "L2_gnn_b2", "L3_gnn_b")]
    arrays = {
        "x_in": a["x"], "edges": edges, "query": query, "small_in": _small(a, np),
        "bias_in": np.concatenate(rows)[None], "bd_in": a["L0_ffn_bd"],
        "phi_in": a["L3_ffn_phi"].reshape(K, P, SLOTS).transpose(1, 0, 2),
        "slot_b1_in": a["L3_ffn_b1"].reshape(SLOTS, 3, P).transpose(2, 1, 0),
        "slot_b2_in": np.concatenate([a["L3_ffn_b2"], np.zeros((SLOTS, D), np.float32)]), "stream": stream,
    }
    arrays = {name: np.ascontiguousarray(value) for name, value in arrays.items()}
    nc = bacc.Bacc("TRN2", target_bir_lowering=False, num_devices=1)
    tensors = [nc.dram_tensor(name, v.shape, mybir.dt.from_np(v.dtype), kind="ExternalInput").ap()
               for name, v in arrays.items()]
    out = nc.dram_tensor("out", (N, D), F32, kind="ExternalOutput").ap()
    build(nc, *tensors, out)
    result = run_bass_kernel_spmd(nc, [arrays], core_ids=[0])
    return result.results[0]["out"]
```

```python
from contextlib import ExitStack, contextmanager

import concourse.bass as bass
from concourse import mybir

F32 = mybir.dt.float32
F32R = mybir.dt.float32r
BF16 = mybir.dt.bfloat16
I32 = mybir.dt.int32
U32 = mybir.dt.uint32
ALU = mybir.AluOpType
ACT = mybir.ActivationFunctionType
AX_X = mybir.AxisListType.X

P = 128
N = 256
T = N // P
D = 768
K = D // P
E = 4096
EDGE_TILES = E // P
REL = 3
B, L = 8, 64
GROUP = N // B
PIECE = 2304
RING = 3
HALF = 384
LOW = -1e30
HEADS, HEAD = 12, 64
SLOTS, SLOT_HIDDEN = 64, 384
CHUNKS = K * B
CHUNK_RING = 6
BIASED = 4
WHOLE = 4
GATE, UP, DOWN = range(3)

GATE_PIECES = 2 + 4
RGCN_PIECES = 8
L0_GNN_PIECES = 2 + 2 * (RGCN_PIECES + GATE_PIECES)
UNITS = (16, 10, 18)
EXPERTS = (8, 8, 16)
SLOT_PAIR = 2 * SLOTS
STREAM = (L0_GNN_PIECES + 3 * sum(UNITS) + 3 + 3 + 8 + 2 * REL * 2 + 2 + 2 * SLOTS)

SMALL = {}
_at = 0
for _name, _width in (("bg", K), ("bq", K), ("unit_bias", UNITS[0] * 6), ("norm1", K), ("norm2", K),
                      ("router0", K * 8), ("router1", K * 8), ("router2", K * 16), ("br", 8), ("scale", 1),
                      ("att0", 8 * 16), ("att1", K * 2), ("att2", K * 8), ("att3", K * 2)):
    SMALL[_name] = (_at, _width)
    _at += _width
SMALL_WIDTH = _at
BIAS_ROWS = (D, D, 1024, D, D, D, D)
BIAS_AT = [sum(BIAS_ROWS[:i]) for i in range(len(BIAS_ROWS))]

EDGE_LAYERS = (
    dict(rel=1, heads=8, width=128, pieces=((0, 2), (2, 4), (4, 6)), att="att0"),
    dict(rel=1, heads=1, width=768, pieces=((0, 3), (3, 6), (6, 8)), att="att1"),
    dict(rel=REL, heads=4, width=192, pieces=((0, 3), (3, 6)), att="att2"),
    dict(rel=REL, heads=1, width=768, pieces=((0, 3), (3, 6)), att="att3"),
)


class Counts:

    def __init__(self):
        self.count, self.grows, self.inner, self.i = {}, {}, {}, None

    def upto(self, sem, more=1):
        if self.i is None:
            self.count[sem] = self.count.get(sem, 0) + more
            return self.count[sem]
        self.inner[sem] = self.inner.get(sem, 0) + more
        return self.i * self.grows[sem] + (self.count.get(sem, 0) + self.inner[sem])

    @contextmanager
    def loop(self, engine, trips, grows):
        with engine.Fori(0, trips) as i:
            self.i, self.grows, self.inner = i, grows, {}
            yield i
        assert self.inner == grows, (self.inner, grows)
        self.i = None
        for sem, per in grows.items():
            self.count[sem] = self.count.get(sem, 0) + trips * per


UNITS_AT = (L0_GNN_PIECES, L0_GNN_PIECES + 3 * UNITS[0] + 3 + 3 + 8,
            L0_GNN_PIECES + 3 * UNITS[0] + 3 + 3 + 8 + 3 * UNITS[1] + 2 * REL * 2)
SLOTS_AT = STREAM - 2 * SLOTS
EDGES_AT = (UNITS_AT[0] + 3 * UNITS[0], UNITS_AT[0] + 3 * UNITS[0] + 3, UNITS_AT[1] + 3 * UNITS[1],
            UNITS_AT[1] + 3 * UNITS[1] + 2 * REL)
HEADS_AT = EDGES_AT[1] + 3
ROOT_AT = (2, 2 + RGCN_PIECES + GATE_PIECES)
ALPHA_AT = tuple(at + RGCN_PIECES + 2 for at in ROOT_AT)


def build(nc, x_in, edges, query, small_in, bias_in, bd_in, phi_in, slot_b1_in, slot_b2_in, stream, out):
    with ExitStack() as ctx:
        def sb(name, shape, dt=F32, where=ctx):
            return where.enter_context(nc.sbuf_tensor(name, shape, dt))

        def sem(name):
            return ctx.enter_context(nc.semaphore(name))

        ring = [sb(f"ring{i}", [P, PIECE]) for i in range(RING)]
        with ExitStack() as part:
            chunk_space = [[sb(f"chunk_space{n}{i}", [P, PIECE], F32, part) for i in range(RING)] for n in range(2)]
        high = [sb(f"high{i}", [P, PIECE], F32R) for i in range(RING)]
        low = [sb(f"low{i}", [P, PIECE], F32R) for i in range(RING)]
        cols_high = sb("cols_high", [P, K, N], F32R)
        cols_low = sb("cols_low", [P, K, N], F32R)
        x = sb("x", [P, T, D])
        rows = sb("rows", [P, T, D])
        cols = sb("cols", [P, K, N])
        counts = sb("counts", [P, T, REL, N])
        loop_counts = sb("loop_counts", [P, T, N])
        bias = sb("bias", [P, 1024])
        ident = sb("ident", [P, P])
        ones = sb("ones", [P, P])
        tiny = sb("tiny", [P, 2], BF16)
        iota = sb("iota", [P, SLOTS])
        small = sb("small", [P, SMALL_WIDTH])
        stats = sb("stats", [P, T, 2, 6])
        moments = sb("moments", [P, T, 2])
        root = sb("root", [P, SLOTS])
        inverse = sb("inverse", [P, T])
        dinv = sb("dinv", [P, T])

        with ExitStack() as l0:
            query_cols = sb("query_cols", [P, K, B * L], F32, l0)
            query_gate = sb("query_gate", [P, K, B * L], F32, l0)
            hidden_gate = sb("hidden_gate", [P, K, N], F32, l0)
            mean_counts = sb("mean_counts", [P, T, REL * N], F32, l0)
            hidden = sb("hidden", [P, K, N], F32, l0)
            with ExitStack() as part:
                query_high = sb("query_high", [P, K, B * L], F32R, part)
                query_low = sb("query_low", [P, K, B * L], F32R, part)
                edge_ints = sb("edge_ints", [P, 3, EDGE_TILES], I32, part)
                edge_src = sb("edge_src", [P, EDGE_TILES], F32, part)
                edge_dst = sb("edge_dst", [P, EDGE_TILES], F32, part)
                edge_key = sb("edge_key", [P, EDGE_TILES], F32, part)
                key_iota = sb("key_iota", [P, REL * N], F32, part)
                src_hot = [sb(f"src_hot{i}", [P, N], BF16, part) for i in range(2)]
                key_hot = [sb(f"key_hot{i}", [P, REL * N], BF16, part) for i in range(2)]
                raw_counts = sb("raw_counts", [P, T, REL * N], F32, part)
                in_degree = key_iota
            with ExitStack() as part:
                aggregate_high = [sb(f"aggregate_high{i}", [P, K, N], F32R, part) for i in range(2)]
                aggregate_low = [sb(f"aggregate_low{i}", [P, K, N], F32R, part) for i in range(2)]
            with ExitStack() as part:
                alpha = sb("alpha", [P, K, N], F32, part)
                attended_high = sb("attended_high", [P, K, N], F32R, part)
                attended_low = sb("attended_low", [P, K, N], F32R, part)

        def chunk_buffer(q, first):
            space = chunk_space[q % 2][(first + q // 2) % RING]
            return space[:, 0:GROUP * L].rearrange("p (n l) -> p n l", n=GROUP)

        with ExitStack() as part:
            logits = sb("logits", [P, T, 16], F32, part)
            row_max = sb("row_max", [P, T], F32, part)
            row_sum = sb("row_sum", [P, T], F32, part)
            top = sb("top", [P, T, 8], F32, part)
            top_at = sb("top_at", [P, T, 8], U32, part)
            top_place = sb("top_place", [P, T, 8], F32, part)
            top_weight = sb("top_weight", [P, T, 2], F32, part)
            gap = sb("gap", [P, T], F32, part)
            combine = sb("combine", [P, T, 16], F32, part)
            second = sb("second", [P, T, 16], F32, part)
            combine_cols = sb("combine_cols", [16, N], F32, part)
            unit_weight = sb("unit_weight", [P, T, 18], F32, part)
            bd_rows = sb("bd_rows", [8, D], F32, part)
            act_high = sb("act_high", [P, 3, N], F32R, part)
            act_low = sb("act_low", [P, 3, N], F32R, part)
            gate_part = sb("gate_part", [P, 3, N], F32, part)
            up_part = sb("up_part", [P, 3, N], F32, part)
            squash = sb("squash", [P, 3, N], F32, part)
            act_cols = sb("act_cols", [P, 3, N], F32, part)

        with ExitStack() as part:
            message = sb("message", [P, REL * T * D], F32, part)
            wide_rows = sb("wide_rows", [P, T, 1024], F32, part)
            wide_cols = sb("wide_cols", [P, 8, N], F32, part)
            wide_high = sb("wide_high", [P, 8, N], F32R, part)
            wide_low = sb("wide_low", [P, 8, N], F32R, part)
            edge_scores = [sb(f"edge_scores{i}", [P, REL * N], F32, part) for i in range(2)]
            edge_exp = [sb(f"edge_exp{i}", [P, REL * N], F32, part) for i in range(2)]
            edge_turned = [sb(f"edge_turned{i}", [P, REL * T, P], F32, part) for i in range(2)]
            absent = sb("absent", [P, T, REL * N], F32, part)
            all_counts = sb("all_counts", [P, T, N], F32, part)
            queries_keys = sb("queries_keys", [P, T, REL, 16], F32, part)
            keys = sb("keys", [P, T, 16], F32, part)
            key_rows = sb("key_rows", [12, N], F32, part)
            edge_max = sb("edge_max", [P, 2], F32, part)
            edge_negmax = sb("edge_negmax", [P, 2], F32, part)
            edge_sum = sb("edge_sum", [P, 4], F32, part)
            edge_inverse = sb("edge_inverse", [P, 4], F32, part)

        with ExitStack() as part:
            head_q = sb("head_q", [P, K, N], F32, part)
            head_k = sb("head_k", [P, K, N], F32, part)
            values = sb("values", [P, T, D], F32, part)
            context = sb("context", [P, K, N], F32, part)
            context_high = sb("context_high", [P, K, N], F32R, part)
            context_low = sb("context_low", [P, K, N], F32R, part)
            normed = sb("normed", [P, T, D], F32, part)
            probs = [sb(f"probs{i}", [P, T, N], F32, part) for i in range(2)]
            probs_turned = [sb(f"probs_turned{i}", [P, T, N], F32, part) for i in range(2)]
            head_max = sb("head_max", [P, 2, T], F32, part)
            head_negmax = sb("head_negmax", [P, 2, T], F32, part)
            head_sum = sb("head_sum", [P, 2, T], F32, part)
            head_inverse = sb("head_inverse", [P, 2, T], F32, part)

        with ExitStack() as part:
            phi = sb("phi", [P, K, SLOTS], F32, part)
            phi_squares = sb("phi_squares", [P, K, SLOTS], F32, part)
            phi_scale = sb("phi_scale", [P, SLOTS], F32, part)
            dispatch = sb("dispatch", [SLOTS, N], F32, part)
            dispatch_rows = sb("dispatch_rows", [P, T, SLOTS], F32, part)
            mixing = sb("mixing", [P, T, SLOTS], F32, part)
            mixing_pair = sb("mixing_pair", [P, T, 2, SLOTS], F32, part)
            mixing_cols = sb("mixing_cols", [SLOT_PAIR, N], F32, part)
            soft = sb("soft", [P, 8], F32, part)
            slot_in = sb("slot_in", [P, K, SLOTS], F32, part)
            slot_pair = sb("slot_pair", [P, K, SLOT_PAIR], F32R, part)
            slot_mask = [sb(f"slot_mask{i}", [P, K, SLOT_PAIR], F32R, part) for i in range(3)]
            slot_fold = sb("slot_fold", [SLOT_PAIR, SLOTS], F32, part)
            slot_sum = sb("slot_sum", [SLOT_PAIR, SLOT_HIDDEN], F32, part)
            slot_b1 = sb("slot_b1", [P, 3, SLOTS], F32, part)
            slot_b2 = sb("slot_b2", [SLOT_PAIR, D], F32, part)
            slot_hidden = sb("slot_hidden", [P, 3, SLOTS], F32, part)
            slot_out = sb("slot_out", [SLOT_PAIR, D], F32, part)
            squares = sb("squares", [P, D], F32, part)

        psum = ctx.enter_context(nc.psum_tensor("psum", [P, 8, 512], F32))
        flat = psum[:].rearrange("p b c -> p (b c)")

        small_landed, x_landed, edges_landed, query_landed = (
            sem(n) for n in ("small_landed", "x_landed", "edges_landed", "query_landed"))
        piece_landed = [sem(f"piece_landed{i}") for i in range(RING)]
        ring_taken = sem("ring_taken")
        piece_used = sem("piece_used")
        bias_landed, bias_used = sem("bias_landed"), sem("bias_used")
        bd_landed, slots_landed = sem("bd_landed"), sem("slots_landed")
        arena_free = sem("arena_free")
        pool_wrote, vector_wrote = sem("pool_wrote"), sem("vector_wrote")
        constants_ready, ones_ready = sem("constants_ready"), sem("ones_ready")
        root_asked, root_ready = sem("root_asked"), sem("root_ready")
        exp_asked, exp_ready = sem("exp_asked"), sem("exp_ready")
        rows_ready, turned, cols_ready, rows_done = (
            sem(n) for n in ("rows_ready", "turned", "cols_ready", "rows_done"))
        tile_done = sem("tile_done")
        hot_ready, hot_used, counted = sem("hot_ready"), sem("hot_used"), sem("counted")
        raw_ready, degree_done, counts_turned, counts_ready = (
            sem(n) for n in ("raw_ready", "degree_done", "counts_turned", "counts_ready"))
        mean_counts_ready = sem("mean_counts_ready")
        aggregated, aggregate_ready = sem("aggregated"), sem("aggregate_ready")
        gate_hidden_ready, chunk_summed, chunk_squashed, chunk_weighted, chunk_folded, chunk_reduced = (
            sem(n) for n in ("gate_hidden_ready", "chunk_summed", "chunk_squashed", "chunk_weighted",
                             "chunk_folded", "chunk_reduced"))
        attended_high_ready, attended_split = sem("attended_high_ready"), sem("attended_split")
        tanh_ready, alpha_ready, hidden_ready, turned_back, rows_back = (
            sem(n) for n in ("tanh_ready", "alpha_ready", "hidden_ready", "turned_back", "rows_back"))
        logits_taken = sem("logits_taken")
        high_ready = sem("high_ready")
        cols_high_ready, cols_split = sem("cols_high_ready"), sem("cols_split")
        aggregate_high_ready, query_high_ready, query_split = (
            sem(n) for n in ("aggregate_high_ready", "query_high_ready", "query_split"))
        logits_done, combine_ready, combine_turned, combine_cols_ready = (
            sem(n) for n in ("logits_done", "combine_ready", "combine_turned", "combine_cols_ready"))
        gate_done, gate_clipped, squashed, up_done, act_ready, down_done, down_taken = (
            sem(n) for n in ("gate_done", "gate_clipped", "squashed", "up_done", "act_ready", "down_done",
                             "down_taken"))
        query_keys_done, keys_ready, keys_turned, key_rows_ready = (
            sem(n) for n in ("query_keys_done", "keys_ready", "keys_turned", "key_rows_ready"))
        picked, lifted, edge_max_ready, edge_exp_ready, edge_weighted, edges_turned, edges_copied, mixed, stored = (
            sem(n) for n in ("picked", "lifted", "edge_max_ready", "edge_exp_ready", "edge_weighted",
                             "edges_turned", "edges_copied", "mixed", "stored"))
        heads_ready, scored, head_max_ready, probs_exp, probs_ready, probs_done, probs_copied, context_done, \
            context_ready = (sem(n) for n in ("heads_ready", "scored", "head_max_ready", "probs_exp", "probs_ready",
                                              "probs_done", "probs_copied", "context_done", "context_ready"))
        phi_squared, phi_summed, phi_ready, slot_logits_done, soft_ready, soft_turned, soft_copied = (
            sem(n) for n in ("phi_squared", "phi_summed", "phi_ready", "slot_logits_done", "soft_ready",
                             "soft_turned", "soft_copied"))
        slot_in_done, mask_ready, slot_sums_done, slot_sums_ready, slot_folded, slot_pre, slot_act, \
            slot_out_done, slot_out_ready = (
                sem(n) for n in ("slot_in_done", "mask_ready", "slot_sums_done", "slot_sums_ready", "slot_folded",
                                 "slot_pre", "slot_act", "slot_out_done", "slot_out_ready"))
        x_final, out_stored = sem("x_final"), sem("out_stored")

        def row_parts(width):
            return [(0, 0, min(width, 512))] + ([(1, 512, width - 512)] if width > 512 else [])

        def row_bank(t, j, n):
            if j == 0:
                return psum[:, 3 + t, 0:n]
            return psum[:, 5, t * N:t * N + n] if n == N else psum[:, 5 + t, 0:n]

        def opens(t, j, n):
            return t == 0 or j == 0 or n != N

        def col_tile(f):
            return flat[:, f * N:(f + 1) * N]

        UNIT_BANKS = ((0, 1), (2, 6))

        def unit_bank(part, last):
            return psum[:, UNIT_BANKS[part][last], 0:N if last else 2 * N]

        def unit_tile(part, f):
            return psum[:, UNIT_BANKS[part][f // 2], f % 2 * N:(f % 2 + 1) * N]

        def node_tile(t):
            return slice(t * P, (t + 1) * P)

        def small_at(name, i=0, n=1):
            return small[:, SMALL[name][0] + i:SMALL[name][0] + i + n]

        flat_x = x[:].rearrange("p t d -> p (t d)")
        flat_rows = rows[:].rearrange("p t d -> p (t d)")
        flat_cols = cols[:].rearrange("p k n -> p (k n)")
        flat_hidden = hidden[:].rearrange("p k n -> p (k n)")
        flat_gate = hidden_gate[:].rearrange("p k n -> p (k n)")
        flat_counts = counts[:].rearrange("p t r n -> p (t r n)")

        def message_rows(layer):
            width = layer["heads"] * layer["width"]
            n = layer["rel"] * T * width
            return message[:, 0:n].rearrange("p (r t d) -> p r t d", r=layer["rel"], t=T)

        block = ctx.enter_context(nc.Block())

        @block.sync
        def _(sp):
            seen = Counts()
            sp.dma_start(x[:], x_in.rearrange("(t p) d -> p t d", p=P)).then_inc(x_landed, 16)
            for i in range(RING):
                sp.dma_start(ring[i][:], stream[i]).then_inc(piece_landed[i], 16)
            assert STREAM % RING == 0
            with seen.loop(sp, STREAM // RING - 1, {ring_taken: RING}) as i:
                for s in range(RING):
                    sp.wait_ge(ring_taken, seen.upto(ring_taken))
                    piece = stream[bass.ds(i * RING + (RING + s), 1)].rearrange("a p c -> (a p) c")
                    sp.dma_start(ring[s][:], piece).then_inc(piece_landed[s], 16)
            sp.wait_ge(x_final, 1)
            sp.dma_start(out.rearrange("(t p) d -> p t d", p=P), x[:]).then_inc(out_stored, 16)
            sp.wait_ge(out_stored, 16)

        @block.gpsimd
        def _(pool):
            seen = Counts()
            pool.memset(ident[:], 0.0).then_inc(pool_wrote, 1)
            pool.wait_ge(pool_wrote, seen.upto(pool_wrote))
            pool.affine_select(out=ident[:], in_=ident[:], compare_op=ALU.not_equal, fill=1.0, base=0,
                               pattern=[[-1, P]], channel_multiplier=1).then_inc(constants_ready, 1)
            pool.iota(iota[:], [[1, SLOTS]], base=0, channel_multiplier=0,
                      allow_small_or_imprecise_dtypes=True).then_inc(constants_ready, 1)
            pool.iota(key_iota[:], [[1, REL * N]], base=0, channel_multiplier=0,
                      allow_small_or_imprecise_dtypes=True).then_inc(constants_ready, 1)

            def load_bias(n):
                if n:
                    pool.wait_ge(bias_used, seen.upto(bias_used))
                at, width = BIAS_AT[n], BIAS_ROWS[n]
                pool.dma_start(bias[:, 0:width], bias_in[:, at:at + width].broadcast_to([P, width]))\
                    .then_inc(bias_landed, 16)

            def sum_chunk(c, chunk):
                nodes = GROUP - BIASED
                by_node = flat_gate[:, bass.ds(c * GROUP + BIASED, nodes)].unsqueeze(2).broadcast_to([P, nodes, L])
                by_query = query_gate[:].rearrange("p k q -> p (k q)")[:, bass.ds(c * L, L)]\
                    .unsqueeze(1).broadcast_to([P, nodes, L])
                pool.tensor_tensor(chunk[:, BIASED:, :], by_node, by_query, ALU.add).then_inc(chunk_summed, 1)

            load_bias(0)
            pool.wait_ge(query_high_ready, seen.upto(query_high_ready))
            pool.tensor_tensor(query_low[:], query_cols[:], query_high[:].bitcast(F32), ALU.subtract)\
                .then_inc(query_split, 1)
            for layer in range(2):
                pool.wait_ge(gate_hidden_ready, seen.upto(gate_hidden_ready, 6 + 1 if layer == 0 else 1))
                chunk = [chunk_buffer(q, ALPHA_AT[layer]) for q in range(CHUNK_RING)]
                for c in range(CHUNK_RING):
                    if c == 2:
                        pool.wait_ge(gate_hidden_ready, seen.upto(gate_hidden_ready, 2))
                    sum_chunk(c, chunk[c])
                with seen.loop(pool, CHUNKS // CHUNK_RING - 1, {chunk_reduced: CHUNK_RING}) as i:
                    for s in range(CHUNK_RING):
                        pool.wait_ge(chunk_reduced, seen.upto(chunk_reduced))
                        sum_chunk(i * CHUNK_RING + (CHUNK_RING + s), chunk[s])
                seen.upto(chunk_reduced, CHUNK_RING)
                load_bias(layer + 1)
            pool.wait_ge(arena_free, seen.upto(arena_free))
            pool.dma_start(bd_rows[:], bd_in).then_inc(bd_landed, 16)
            for n in range(3, len(BIAS_ROWS)):
                load_bias(n)
            pool.wait_ge(arena_free, seen.upto(arena_free))
            pool.dma_start(phi[:], phi_in).then_inc(slots_landed, 16)
            pool.dma_start(slot_b1[:], slot_b1_in).then_inc(slots_landed, 16)
            pool.dma_start(slot_b2[:], slot_b2_in).then_inc(slots_landed, 16)

        @block.tensor
        def _(pe):
            seen = Counts()
            place = [0]

            def signal(what, n=1):
                pe.matmul(psum[0:2, 7, 508:510], tiny[:], tiny[:], start=True, stop=True).then_inc(what, n)

            def piece(turn=None, ahead=0):
                n = place[0] + ahead
                pe.wait_ge(ring_taken, n + 1 if turn is None else turn * RING + (n + 1))
                return high[n % RING], low[n % RING]

            def use(n=1):
                place[0] += n

            TERMS = ((0, 0), (0, 1), (1, 0))

            def product_rows(source, pieces, width, first=True, last=True, fresh=None):
                end = pieces[-1][1] - 1
                for k0, k1 in pieces:
                    weights = piece()
                    for k in range(k0, k1):
                        if fresh is not None and k % 2 == 0:
                            pe.wait_ge(fresh, seen.upto(fresh))
                        for t in range(T):
                            for n, (a, b) in enumerate(TERMS):
                                for j, c, size in row_parts(width):
                                    at = (k - k0) * width + c
                                    mm = pe.matmul(row_bank(t, j, size), source[a][:, k, node_tile(t)],
                                                   weights[b][:, at:at + size],
                                                   start=first and k == 0 and n == 0 and opens(t, j, size),
                                                   stop=last and k == end and n == 2, skip_group_check=True)
                    mm.then_inc(piece_used, 1)
                    use()
                if last:
                    signal(rows_done, 1)

            def product_cols(source, n, tile, done, fresh=None):
                for half in range(2):
                    weights = piece()
                    for f in range(3):
                        for k in range(K):
                            if fresh is not None and half == 0 and f == 0 and k % 2 == 0:
                                pe.wait_ge(fresh, seen.upto(fresh))
                            for m, (a, b) in enumerate(TERMS):
                                mm = pe.matmul(tile(3 * half + f),
                                               weights[b][:, k * HALF + f * P:k * HALF + (f + 1) * P],
                                               source[a][:, k, 0:n], start=k == 0 and m == 0,
                                               stop=k == K - 1 and m == 2)
                        if f == 2:
                            mm.then_inc(piece_used, 1)
                        if n == 512 or (3 * half + f) % 2 == 1:
                            signal(done)
                    use()

            def turn_rows(source, tiles=K, awaited=False):
                if not awaited:
                    pe.wait_ge(rows_ready, seen.upto(rows_ready))
                for k in range(tiles):
                    for t in range(T):
                        mm = pe.transpose(flat[:, k * N + t * P:k * N + (t + 1) * P],
                                          source[:, t, k * P:(k + 1) * P], ident[:])
                    if k % 2 == 1:
                        mm.then_inc(turned, 1)

            def await_cols(tiles=K):
                pe.wait_ge(cols_ready, seen.upto(cols_ready, tiles // 2))

            def turn_cols_back(source):
                for t in range(T):
                    for k in range(K):
                        at = t * D + k * P
                        mm = pe.transpose(flat[:, at:at + P], source[:, k, node_tile(t)], ident[:])
                        if (at + P) % 512 == 0:
                            mm.then_inc(turned_back, 1)

            pe.wait_ge(constants_ready, seen.upto(constants_ready, 3))
            pe.wait_ge(ones_ready, seen.upto(ones_ready))
            pe.wait_ge(small_landed, seen.upto(small_landed, 16))

            def count_edges():
                def tile(q, first, last):
                    pe.wait_ge(hot_ready, seen.upto(hot_ready))
                    for t in range(T):
                        for j, c, n in row_parts(REL * N):
                            mm = pe.matmul(row_bank(t, j, n), src_hot[q][:, node_tile(t)], key_hot[q][:, c:c + n],
                                           start=first and opens(t, j, n), stop=last, skip_group_check=True)
                    mm.then_inc(hot_used, 1)

                tile(0, True, False)
                tile(1, False, False)
                with seen.loop(pe, EDGE_TILES // 2 - 2, {hot_ready: 2}):
                    tile(0, False, False)
                    tile(1, False, False)
                tile(0, False, False)
                tile(1, False, True)
                signal(counted, 1)
                pe.wait_ge(raw_ready, seen.upto(raw_ready))

            def sum_counts():
                for j, c, n in row_parts(REL * N):
                    for t in range(T):
                        mm = pe.matmul(psum[:, 6 + j, 0:n], ones[:], raw_counts[:, t, c:c + n],
                                       start=t == 0, stop=t == T - 1)
                mm.then_inc(degree_done, 1)
                for t in range(T):
                    for r in range(REL):
                        for s in range(T):
                            at = t * REL * N + r * N + s * P
                            mm = pe.transpose(flat[:, at:at + P], raw_counts[:, s, r * N + t * P:r * N + (t + 1) * P],
                                              ident[:])
                mm.then_inc(counts_turned, 1)

            def l0_gnn():
                count_edges()
                pe.wait_ge(query_split, seen.upto(query_split))
                product_cols((query_high, query_low), B * L, lambda f: psum[:, f, 0:512], tile_done)
                pe.wait_ge(gate_hidden_ready, seen.upto(gate_hidden_ready, 6))
                sum_counts()
                pe.wait_ge(counts_ready, seen.upto(counts_ready))
                split_cols = (cols_high, cols_low)
                for layer in range(2):
                    assert place[0] == ROOT_AT[layer]
                    if layer == 0:
                        turn_rows(rows)
                        await_cols()
                    else:
                        pe.wait_ge(rows_back, seen.upto(rows_back, 3))

                    def aggregate_nodes(r):
                        for f in range(K):
                            for s in range(T):
                                mm = pe.matmul(col_tile(f), rows[:, s, f * P:(f + 1) * P],
                                               mean_counts[:, s, r * N:(r + 1) * N], start=s == 0, stop=s == T - 1)
                            if f % 2 == 1:
                                mm.then_inc(aggregated, 1)

                    halves = ((0, 3), (3, 6))
                    if layer == 1:
                        aggregate_nodes(0)
                    product_rows(split_cols, halves, D, last=False, fresh=cols_split)
                    if layer == 0:
                        pe.wait_ge(mean_counts_ready, seen.upto(mean_counts_ready))
                        aggregate_nodes(0)
                    for r in range(REL):
                        pe.wait_ge(aggregate_ready, seen.upto(aggregate_ready, 3))
                        if r + 1 < REL:
                            aggregate_nodes(r + 1)
                        product_rows((aggregate_high[r % 2], aggregate_low[r % 2]), halves, D, first=False,
                                     last=r == REL - 1)
                    turn_rows(rows)
                    await_cols()
                    product_cols(split_cols, N, col_tile, tile_done, fresh=cols_split)
                    seen.upto(gate_hidden_ready, 3)
                    chunk = [chunk_buffer(q, ALPHA_AT[layer]) for q in range(CHUNK_RING)]

                    def fold(q):
                        pe.wait_ge(chunk_weighted, seen.upto(chunk_weighted))
                        for s in range(L // 16):
                            mm = pe.matmul(psum[:, q, 0:(GROUP - WHOLE) * 16]
                                           .rearrange("p (n l) -> p n l", n=GROUP - WHOLE), ident[:],
                                           chunk[q][:, WHOLE:, 16 * s:16 * s + 16], start=s == 0,
                                           stop=s == L // 16 - 1)
                        mm.then_inc(chunk_folded, 1)

                    for c in range(CHUNK_RING):
                        fold(c)
                    with seen.loop(pe, CHUNKS // CHUNK_RING - 1,
                                   {chunk_weighted: CHUNK_RING, chunk_reduced: CHUNK_RING}):
                        for q in range(CHUNK_RING):
                            pe.wait_ge(chunk_reduced, seen.upto(chunk_reduced))
                            fold(q)
                    pe.wait_ge(chunk_reduced, seen.upto(chunk_reduced, CHUNK_RING))
                    assert place[0] == ALPHA_AT[layer]
                    for half in range(2):
                        for part, source in enumerate((split_cols, (attended_high, attended_low))):
                            weights = piece()
                            for f in range(3):
                                to = 3 * half + f
                                for k in range(K):
                                    if half == 0 and part == 1 and f == 0 and k % 2 == 0:
                                        pe.wait_ge(attended_split, seen.upto(attended_split))
                                    for m, (a, b) in enumerate(TERMS):
                                        opening = part == 0 and k == 0 and m == 0 and to not in (1, 5)
                                        mm = pe.matmul(col_tile(to),
                                                       weights[b][:, k * HALF + f * P:k * HALF + (f + 1) * P],
                                                       source[a][:, k, :], start=opening,
                                                       stop=part == 1 and k == K - 1 and m == 2,
                                                       skip_group_check=True)
                                if part == 1 and to % 2 == 1:
                                    mm.then_inc(tile_done, 1)
                            signal(piece_used)
                            use()
                    pe.wait_ge(hidden_ready, seen.upto(hidden_ready))
                    turn_cols_back(hidden)

            def experts(layer):
                units, count = UNITS[layer], EXPERTS[layer]
                assert place[0] == UNITS_AT[layer]
                split_cols = (cols_high, cols_low)
                turn_rows(rows)
                await_cols()
                at, _ = SMALL[f"router{layer}"]
                for t in range(T):
                    for k in range(K):
                        mm = pe.matmul(psum[:, 3, t * 16:t * 16 + count], cols[:, k, node_tile(t)],
                                       small[:, at + k * count:at + (k + 1) * count], start=k == 0, stop=k == K - 1)
                mm.then_inc(logits_done, 1)

                def gate_or_up(part, turn, ahead, fresh=False):
                    weights = piece(turn, ahead)
                    for f in range(3):
                        for k in range(K):
                            if fresh and f == 0 and k % 2 == 0:
                                pe.wait_ge(cols_split, seen.upto(cols_split))
                            at = slice(k * HALF + f * P, k * HALF + (f + 1) * P)
                            for n, (a, b) in enumerate(TERMS):
                                mm = pe.matmul(unit_tile(part, f), weights[b][:, at], split_cols[a][:, k, :],
                                               start=k == 0 and n == 0, stop=k == K - 1 and n == 2)
                        if f > 0:
                            mm.then_inc(gate_done if part == GATE else up_done, 1)
                    signal(piece_used)

                def down(turn, ahead):
                    weights = piece(turn, ahead)
                    pe.wait_ge(act_ready, seen.upto(act_ready))
                    for f in range(3):
                        for t in range(T):
                            for n, (a, b) in enumerate(TERMS):
                                for j, c, size in row_parts(D):
                                    mm = pe.matmul(row_bank(t, j, size), (act_high, act_low)[a][:, f, node_tile(t)],
                                                   weights[b][:, f * D + c:f * D + c + size],
                                                   start=f == 0 and n == 0 and opens(t, j, size),
                                                   stop=f == 2 and n == 2, skip_group_check=True)
                    mm.then_inc(down_done, 1)
                    signal(piece_used)

                gate_read = gate_clipped if layer == 0 else squashed
                if layer == 0:
                    seen.upto(squashed, 2 * units)

                def add_biases():
                    pe.wait_ge(combine_ready, seen.upto(combine_ready))
                    for t in range(T):
                        mm = pe.transpose(psum[0:count, 7, t * P:(t + 1) * P], combine[:, t, 0:count], ident[:])
                    mm.then_inc(combine_turned, 1)
                    pe.wait_ge(combine_cols_ready, seen.upto(combine_cols_ready))
                    pe.wait_ge(bd_landed, seen.upto(bd_landed, 16))
                    pe.wait_ge(down_taken, seen.upto(down_taken))
                    for t in range(T):
                        for j, c, n in row_parts(D):
                            mm = pe.matmul(row_bank(t, j, n), combine_cols[0:count, node_tile(t)],
                                           bd_rows[0:count, c:c + n], start=opens(t, j, n), stop=True,
                                           skip_group_check=True)
                    mm.then_inc(down_done, 1)

                def step(turn, ahead, first=False, biases=False):
                    pe.wait_ge(gate_read, seen.upto(gate_read, 2))
                    gate_or_up(GATE, turn, ahead)
                    if biases:
                        add_biases()
                    if first:
                        pe.wait_ge(logits_taken, seen.upto(logits_taken))
                    else:
                        pe.wait_ge(down_taken, seen.upto(down_taken))
                    down(turn, ahead + 1)
                    gate_or_up(UP, turn, ahead + 2)

                gate_or_up(GATE, None, 0, fresh=True)
                gate_or_up(UP, None, 1)
                step(None, 2, first=True)
                assert RING == 3
                step(None, 5, biases=layer == 0)
                with seen.loop(pe, units - 3, {gate_read: 2, down_taken: 1, act_ready: 1}) as i:
                    step(i, 8)
                pe.wait_ge(gate_read, seen.upto(gate_read, 2))
                pe.wait_ge(down_taken, seen.upto(down_taken))
                down(None, 3 * units - 1)
                pe.wait_ge(down_taken, seen.upto(down_taken))
                use(3 * units)

            def edge_layer(n):
                layer = EDGE_LAYERS[n]
                rel, heads, width = layer["rel"], layer["heads"], layer["width"]
                out_width = heads * width
                tiles = out_width // P
                source = (wide_high, wide_low) if n == 1 else (cols_high, cols_low)
                messages = message_rows(layer)
                turn_rows(wide_rows if n == 1 else rows, 8 if n == 1 else K)
                await_cols(8 if n == 1 else K)
                at, _ = SMALL[layer["att"]]
                for r in range(rel + 1):
                    if r > 0:
                        pe.wait_ge(rows_ready, seen.upto(rows_ready))
                    if r < rel:
                        product_rows(source, layer["pieces"], out_width, fresh=cols_split if r == 0 else None)
                    if r > 0:
                        turn_rows(messages[:, r - 1], tiles, awaited=True)
                        await_cols(tiles)
                        for t in range(T):
                            for k in range(tiles):
                                to = (t * rel + r - 1) * 16
                                mm = pe.matmul(psum[:, 7, to:to + 2 * heads], wide_cols[:, k, node_tile(t)],
                                               small[:, at + k * 2 * heads:at + (k + 1) * 2 * heads],
                                               start=k == 0, stop=k == tiles - 1)
                mm.then_inc(query_keys_done, 1)
                pe.wait_ge(keys_ready, seen.upto(keys_ready))
                count = rel * heads
                for t in range(T):
                    mm = pe.transpose(psum[0:count, 7, t * P:(t + 1) * P], keys[:, t, 0:count], ident[:])
                mm.then_inc(keys_turned, 1)
                pe.wait_ge(key_rows_ready, seen.upto(key_rows_ready))
                items = [(t, h) for h in range(heads) for t in range(T)]

                def pick_keys(i):
                    if i >= 2:
                        pe.wait_ge(lifted, seen.upto(lifted))
                    t, h = items[i]
                    for r in range(rel):
                        at = i % 2 * 1024 + r * N
                        row = r * heads + h
                        mm = pe.matmul(flat[:, at:at + N], ident[0:count, row:row + 1].broadcast_to([count, P]),
                                       key_rows[0:count, :],
                                       start=True, stop=True)
                    mm.then_inc(picked, 1)

                def turn_edges(i):
                    pe.wait_ge(edge_weighted, seen.upto(edge_weighted))
                    for m in range(rel * T):
                        at = 4 * 512 + m * P
                        mm = pe.transpose(flat[:, at:at + P], edge_exp[i % 2][:, m * P:(m + 1) * P], ident[:])
                    mm.then_inc(edges_turned, 1)

                def mix(i):
                    t, h = items[i]
                    pe.wait_ge(edges_copied, seen.upto(edges_copied))
                    if width > 512:
                        if i >= 1:
                            pe.wait_ge(stored, seen.upto(stored))
                    elif i >= 2:
                        pe.wait_ge(stored, seen.upto(stored))
                    for j, c, size in row_parts(width):
                        bank = 6 + j if width > 512 else 6 + i % 2
                        for m in range(rel * T):
                            r, s = divmod(m, T)
                            mm = pe.matmul(psum[:, bank, 0:size], edge_turned[i % 2][:, m, :],
                                           messages[:, r, s, h * width + c:h * width + c + size],
                                           start=m == 0, stop=m == rel * T - 1)
                    mm.then_inc(mixed, 1)

                last = len(items)
                for s in range(last + 3):
                    if s < last:
                        pick_keys(s)
                    if 0 <= s - 3 < last:
                        mix(s - 3)
                    if 0 <= s - 2 < last:
                        turn_edges(s - 2)
                pe.wait_ge(lifted, seen.upto(lifted, 2))
                pe.wait_ge(stored, seen.upto(stored, 1 if width > 512 else 2))

            def self_attention():
                split_cols = (cols_high, cols_low)
                turn_rows(normed)
                await_cols()
                product_cols(split_cols, N, col_tile, tile_done, fresh=cols_split)
                pe.wait_ge(heads_ready, seen.upto(heads_ready, 3))
                product_cols(split_cols, N, col_tile, tile_done)
                product_rows(split_cols, ((0, 3), (3, 6)), D)
                pe.wait_ge(heads_ready, seen.upto(heads_ready, 3))
                pe.wait_ge(rows_ready, seen.upto(rows_ready))

                def scores(h):
                    if h >= 2:
                        pe.wait_ge(probs_exp, seen.upto(probs_exp))
                    at = h % 2 * HEAD
                    for t in range(T):
                        mm = pe.matmul(psum[:, h % 2, t * N:(t + 1) * N], head_q[at:at + HEAD, h // 2, node_tile(t)],
                                       head_k[at:at + HEAD, h // 2, :], start=True, stop=True)
                    mm.then_inc(scored, 1)

                def turn_probs(h):
                    pe.wait_ge(probs_ready, seen.upto(probs_ready))
                    for s in range(T):
                        for t in range(T):
                            mm = pe.transpose(psum[:, 2 + h % 2, s * N + t * P:s * N + (t + 1) * P],
                                              probs[h % 2][:, t, s * P:(s + 1) * P], ident[:])
                    mm.then_inc(probs_done, 1)

                def mix_values(h):
                    pe.wait_ge(probs_copied, seen.upto(probs_copied))
                    if h >= 2:
                        pe.wait_ge(context_ready, seen.upto(context_ready))
                    at = h % 2 * HEAD
                    for s in range(T):
                        mm = pe.matmul(psum[at:at + HEAD, 4 + h % 2, 0:N], values[:, s, h * HEAD:(h + 1) * HEAD],
                                       probs_turned[h % 2][:, s, :], start=s == 0, stop=s == T - 1)
                    mm.then_inc(context_done, 1)

                for s in range(HEADS + 2):
                    if s < HEADS:
                        scores(s)
                    if 0 <= s - 1 < HEADS:
                        turn_probs(s - 1)
                    if 0 <= s - 2 < HEADS:
                        mix_values(s - 2)
                pe.wait_ge(probs_exp, seen.upto(probs_exp, 2))
                pe.wait_ge(context_ready, seen.upto(context_ready, 2))
                product_rows((context_high, context_low), ((0, 3), (3, 6)), D, fresh=cols_split)

            def l1_gnn():
                edge_layer(0)
                edge_layer(1)

            def l1_ffn():
                self_attention()
                experts(1)

            def l2_gnn():
                edge_layer(2)
                edge_layer(3)

            def l3_gnn():
                turn_rows(rows)
                await_cols()
                product_rows((cols_high, cols_low), ((0, 3), (3, 6)), D, fresh=cols_split)
                pe.wait_ge(phi_squared, seen.upto(phi_squared))
                for k in range(K):
                    mm = pe.matmul(psum[:, 7, 0:SLOTS], ones[:], phi_squares[:, k, :], start=k == 0, stop=k == K - 1)
                mm.then_inc(phi_summed, 1)
                pe.wait_ge(rows_ready, seen.upto(rows_ready))
                for t in range(T):
                    for j, c, n in row_parts(D):
                        for s in range(T):
                            mm = pe.matmul(row_bank(t, j, n), loop_counts[:, s, node_tile(t)], rows[:, s, c:c + n],
                                           start=s == 0 and opens(t, j, n), stop=s == T - 1, skip_group_check=True)
                mm.then_inc(rows_done, 1)

            def l3_ffn():
                turn_rows(rows)
                await_cols()
                pe.wait_ge(phi_ready, seen.upto(phi_ready))
                for t in range(T):
                    for k in range(K):
                        pe.matmul(psum[:, 3, t * SLOTS:(t + 1) * SLOTS], cols[:, k, node_tile(t)], phi[:, k, :],
                                  start=k == 0, stop=k == K - 1)
                for k in range(K):
                    mm = pe.matmul(psum[0:SLOTS, 4, 0:N], phi[:, k, :], cols[:, k, :], start=k == 0, stop=k == K - 1)
                mm.then_inc(slot_logits_done, 1)
                pe.wait_ge(soft_ready, seen.upto(soft_ready))
                for t in range(T):
                    pe.transpose(psum[0:SLOT_PAIR, 5, t * P:(t + 1) * P],
                                 mixing_pair[:, t].rearrange("p h n -> p (h n)"), ident[:])
                    mm = pe.transpose(psum[:, 6, t * SLOTS:(t + 1) * SLOTS], dispatch[:, node_tile(t)],
                                      ident[0:SLOTS, 0:SLOTS])
                mm.then_inc(soft_turned, 1)
                pe.wait_ge(soft_copied, seen.upto(soft_copied))
                for f in range(K):
                    for s in range(T):
                        mm = pe.matmul(psum[:, 7, f * SLOTS:(f + 1) * SLOTS], rows[:, s, f * P:(f + 1) * P],
                                       dispatch_rows[:, s, :], start=s == 0, stop=s == T - 1)
                mm.then_inc(slot_in_done, 1)

                def slot_products(tiles, width):
                    def one(q, first=False, last=False):
                        pe.wait_ge(mask_ready, seen.upto(mask_ready))
                        for k in range(tiles):
                            for weights in (high, low):
                                for j, c, n in row_parts(width):
                                    at = k * width + c
                                    mm = pe.matmul(psum[:, 3 + j, 0:n], slot_mask[q][:, k, :],
                                                   weights[q][:, at:at + n],
                                                   start=first and k == 0 and weights is high,
                                                   stop=last and k == tiles - 1 and weights is low)
                        mm.then_inc(piece_used, 1)

                    start = place[0]
                    one(start % RING, first=True)
                    with seen.loop(pe, (SLOTS - 4) // RING, {mask_ready: RING}):
                        for a in range(RING):
                            one((start + 1 + a) % RING)
                    for a in range(SLOTS - 3, SLOTS):
                        one((start + a) % RING, last=a == SLOTS - 1)
                    use(SLOTS)

                assert place[0] == SLOTS_AT and (SLOTS - 4) % RING == 0
                slot_products(K, SLOT_HIDDEN)
                signal(slot_sums_done, 1)
                pe.wait_ge(slot_sums_ready, seen.upto(slot_sums_ready))
                for k in range(3):
                    mm = pe.matmul(psum[:, 5, k * SLOTS:(k + 1) * SLOTS], slot_sum[:, k * P:(k + 1) * P],
                                   slot_fold[:], start=True, stop=True)
                mm.then_inc(slot_folded, 1)
                slot_products(3, D)
                signal(slot_out_done, 1)
                pe.wait_ge(slot_out_ready, seen.upto(slot_out_ready))
                for t in range(T):
                    for j, c, n in row_parts(D):
                        mm = pe.matmul(row_bank(t, j, n), mixing_cols[:, node_tile(t)], slot_out[:, c:c + n],
                                       start=opens(t, j, n), stop=True, skip_group_check=True)
                mm.then_inc(rows_done, 1)

            for stage in (l0_gnn, lambda: experts(0), l1_gnn, l1_ffn, l2_gnn, lambda: experts(2), l3_gnn,
                          l3_ffn):
                stage()

        @block.scalar
        def _(act):
            seen = Counts()
            act.dma_start(edge_ints[:], edges).then_inc(edges_landed, 16)
            act.dma_start(small[:], small_in).then_inc(small_landed, 16)
            act.dma_start(query_cols[:], query).then_inc(query_landed, 16)
            act.wait_ge(small_landed, seen.upto(small_landed, 16))
            place = [0]

            def take_high(turn=None, ahead=0):
                n = place[0] + ahead
                slot, rounds = n % RING, n // RING + 1
                if n >= RING:
                    act.wait_ge(piece_used, n - RING + 1 if turn is None else turn * RING + (n - RING + 1))
                act.wait_ge(piece_landed[slot], 16 * rounds if turn is None else turn * 16 + 16 * rounds)
                act.activation(high[slot][:], ring[slot][:], ACT.Copy).then_inc(high_ready, 1)
                if turn is None:
                    place[0] += 1

            def catch_up(at):
                while place[0] < at:
                    take_high()

            def take_root(n, p=P):
                act.wait_ge(root_asked, seen.upto(root_asked))
                act.activation(root[0:p, 0:n], root[0:p, 0:n], ACT.Sqrt).then_inc(root_ready, 1)

            def split_cols(source, to, b):
                act.activation(to[:, 2 * b:2 * b + 2, :], source[:, 2 * b:2 * b + 2, :], ACT.Copy)\
                    .then_inc(cols_high_ready, 1)

            def copy_turned(target, tiles=K, relu=False, scale=None, parts=None):
                def split(b, copied):
                    act.wait_ge(cols_ready, copied)
                    split_cols(target, parts, b)

                copied = 0
                for b in range(tiles // 2):
                    act.wait_ge(turned, seen.upto(turned))
                    for f in ((2 * b,) if scale is None else (2 * b, 2 * b + 1)):
                        n = 2 if scale is None else 1
                        to = target[:, f:f + n, :].rearrange("p k n -> p (k n)")
                        of = flat[:, f * N:(f + n) * N]
                        if scale is None:
                            ins = act.activation(to, of, ACT.Relu if relu else ACT.Copy)
                        else:
                            ins = act.activation(to, of, ACT.Identity, scale=small_at(scale, f))
                    ins.then_inc(cols_ready, 1)
                    if parts is not None and b > 0:
                        split(b - 1, copied)
                    copied = seen.upto(cols_ready)
                if parts is not None:
                    split(tiles // 2 - 1, copied)

            def l0_gnn():
                act.wait_ge(query_landed, seen.upto(query_landed, 16))
                act.activation(query_high[:], query_cols[:], ACT.Copy).then_inc(query_high_ready, 1)
                catch_up(3)
                take_root(T)
                for f in range(K):
                    act.wait_ge(tile_done, seen.upto(tile_done))
                    act.activation(query_gate[:, f, :], psum[:, f, :], ACT.Identity, bias=small_at("bg", f))\
                        .then_inc(gate_hidden_ready, 1)
                    if f == 2:
                        take_high()
                take_high()
                for layer in range(2):
                    chunk = [chunk_buffer(q, ALPHA_AT[layer]) for q in range(CHUNK_RING)]
                    if layer == 0:
                        copy_turned(cols, parts=cols_high)
                    for r in range(REL):
                        for b in range(3):
                            act.wait_ge(aggregated, seen.upto(aggregated))
                            act.activation(aggregate_high[r % 2][:, 2 * b:2 * b + 2, :].rearrange("p k n -> p (k n)"),
                                           psum[:, b, :], ACT.Copy).then_inc(aggregate_high_ready, 1)
                        take_high()
                        take_high()
                    take_high()
                    assert place[0] == ALPHA_AT[layer]
                    copy_turned(cols, relu=True, parts=cols_high)
                    for b in range(3):
                        act.wait_ge(tile_done, seen.upto(tile_done))
                        act.activation(flat_gate[:, 512 * b:512 * b + 512], psum[:, b, :], ACT.Copy)\
                            .then_inc(gate_hidden_ready, 1)
                    with seen.loop(act, CHUNKS // CHUNK_RING, {chunk_summed: CHUNK_RING}) as i:
                        for q in range(CHUNK_RING):
                            c = i * CHUNK_RING + q
                            act.wait_ge(chunk_summed, seen.upto(chunk_summed))
                            for n in range(BIASED):
                                act.activation(chunk[q][:, n, :],
                                               query_gate[:].rearrange("p k q -> p (k q)")[:, bass.ds(c * L, L)],
                                               ACT.Sigmoid, bias=flat_gate[:, bass.ds(c * GROUP + n, 1)])
                            act.activation(chunk[q][:, BIASED:, :], chunk[q][:, BIASED:, :], ACT.Sigmoid)\
                                .then_inc(chunk_squashed, 1)
                    act.wait_ge(chunk_reduced, seen.upto(chunk_reduced, CHUNKS - CHUNK_RING + 1))
                    take_high()
                    act.wait_ge(chunk_reduced, seen.upto(chunk_reduced, CHUNK_RING - 1))
                    for b in range(3):
                        act.activation(attended_high[:, 2 * b:2 * b + 2, :].rearrange("p k n -> p (k n)"),
                                       flat_gate[:, 512 * b:512 * b + 512], ACT.Copy).then_inc(attended_high_ready, 1)
                    take_high()
                    take_high()
                    act.activation(flat_hidden, flat_gate, ACT.Tanh).then_inc(tanh_ready, 1)
                    take_high()
                    take_high()
                    for f in range(K):
                        if f % 2 == 0:
                            act.wait_ge(tile_done, seen.upto(tile_done))
                        act.activation(alpha[:, f, :], col_tile(f), ACT.Sigmoid, bias=small_at("bq", f))\
                            .then_inc(alpha_ready, 1)
                        if f == 1:
                            take_high()
                    take_high()
                    if layer == 0:
                        for b in range(3):
                            act.wait_ge(turned_back, seen.upto(turned_back))
                            act.activation(flat_rows[:, 512 * b:512 * b + 512], psum[:, b, :], ACT.Copy)\
                                .then_inc(rows_back, 1)
                        act.wait_ge(hidden_ready, seen.upto(hidden_ready))
                        for b in range(3):
                            split_cols(hidden, cols_high, b)

            def experts(layer):
                units = UNITS[layer]
                catch_up(UNITS_AT[layer] + 3)
                take_root(T)
                copy_turned(cols, scale="norm2" if layer == 1 else None, parts=cols_high)

                def squash_gate():
                    for last, tiles in ((0, slice(0, 2)), (1, slice(2, 3))):
                        to = squash[:, tiles, :].rearrange("p f n -> p (f n)")
                        if layer == 0:
                            act.wait_ge(gate_clipped, seen.upto(gate_clipped))
                            of = gate_part[:, tiles, :].rearrange("p f n -> p (f n)")
                            act.activation(to, of, ACT.Sigmoid, scale=1.702).then_inc(squashed, 1)
                        else:
                            act.wait_ge(gate_done, seen.upto(gate_done))
                            act.activation(to, unit_bank(0, last), ACT.Silu).then_inc(squashed, 1)

                squash_gate()
                take_high()
                take_high()
                take_high()
                act.wait_ge(act_ready, seen.upto(act_ready))
                squash_gate()
                act.wait_ge(exp_asked, seen.upto(exp_asked))
                if layer == 0:
                    act.activation(gap[:], gap[:], ACT.Exp).then_inc(exp_ready, 1)
                else:
                    act.activation(logits[:, :, 0:EXPERTS[layer]], logits[:, :, 0:EXPERTS[layer]], ACT.Exp)\
                        .then_inc(exp_ready, 1)

                def step(turn):
                    take_high(turn)
                    take_high(turn, 1)
                    act.wait_ge(act_ready, seen.upto(act_ready))
                    squash_gate()
                    take_high(turn, 2)

                take_high()
                with seen.loop(act, units - 3, {act_ready: 1, gate_clipped if layer == 0 else gate_done: 2}) as i:
                    step(i)
                place[0] += 3 * (units - 3)
                take_high()
                act.wait_ge(act_ready, seen.upto(act_ready))
                squash_gate()
                catch_up(UNITS_AT[layer] + 3 * units + 2)
                seen.upto(act_ready)
                if layer == 0:
                    seen.upto(gate_done, 2 * UNITS[0])

            def edge_layer(n):
                layer = EDGE_LAYERS[n]
                rel, heads, width = layer["rel"], layer["heads"], layer["width"]
                tiles = heads * width // P
                catch_up(EDGES_AT[n] + 3)
                if n % 2 == 0:
                    take_root(T)
                if n == 1:
                    copy_turned(wide_cols, 8, relu=True, parts=wide_high)
                else:
                    copy_turned(cols, parts=cols_high)
                if rel == 1:
                    catch_up(EDGES_AT[n] + 6)
                    copy_turned(wide_cols, tiles)
                else:
                    for at in (7, 9, 9):
                        catch_up(EDGES_AT[n] + at)
                        copy_turned(wide_cols, tiles)
                count = rel * heads
                act.wait_ge(keys_turned, seen.upto(keys_turned))
                act.activation(key_rows[0:count, :], psum[0:count, 7, 0:N], ACT.Copy).then_inc(key_rows_ready, 1)
                items = [(t, h) for h in range(heads) for t in range(T)]
                act.wait_ge(keys_ready, seen.upto(keys_ready))

                def lift(i):
                    t, h = items[i]
                    act.wait_ge(picked, seen.upto(picked))
                    if i >= 2:
                        act.wait_ge(edge_exp_ready, seen.upto(edge_exp_ready))
                    for r in range(rel):
                        at = i % 2 * 1024 + r * N
                        ins = act.activation(edge_scores[i % 2][:, r * N:(r + 1) * N], flat[:, at:at + N],
                                             ACT.Identity, bias=queries_keys[:, t, r, h:h + 1])
                    ins.then_inc(lifted, 1)

                def exp_edges(i):
                    act.wait_ge(edge_max_ready, seen.upto(edge_max_ready))
                    act.activation(edge_exp[i % 2][:, 0:rel * N], edge_scores[i % 2][:, 0:rel * N], ACT.Exp,
                                   bias=edge_negmax[:, i % 2:i % 2 + 1]).then_inc(edge_exp_ready, 1)

                def copy_edges(i):
                    act.wait_ge(edges_turned, seen.upto(edges_turned))
                    at = 4 * 512
                    act.activation(edge_turned[i % 2][:, 0:rel * T, :].rearrange("p m n -> p (m n)"),
                                   flat[:, at:at + rel * T * P], ACT.Copy).then_inc(edges_copied, 1)

                last = len(items)
                for s in range(last + 2):
                    if s < last:
                        lift(s)
                    if 0 <= s - 1 < last:
                        exp_edges(s - 1)
                    if 0 <= s - 2 < last:
                        copy_edges(s - 2)
                act.wait_ge(edge_exp_ready, seen.upto(edge_exp_ready, 2))
                if n == 2:
                    act.wait_ge(exp_asked, seen.upto(exp_asked))
                    act.activation(wide_rows[:, :, 0:D], wide_rows[:, :, 0:D], ACT.Exp).then_inc(exp_ready, 1)

            def self_attention():
                catch_up(HEADS_AT + 3)
                take_root(T)
                take_root(T)
                copy_turned(cols, scale="norm1", parts=cols_high)
                for target in (head_q, head_k):
                    for b in range(3):
                        act.wait_ge(tile_done, seen.upto(tile_done))
                        act.activation(target[:, 2 * b:2 * b + 2, :].rearrange("p k n -> p (k n)"), psum[:, b, :],
                                       ACT.Copy).then_inc(heads_ready, 1)
                        if b != 1:
                            take_high()
                catch_up(HEADS_AT + 9)

                def exps(h):
                    act.wait_ge(head_max_ready, seen.upto(head_max_ready))
                    for t in range(T):
                        ins = act.activation(probs[h % 2][:, t, :], psum[:, h % 2, t * N:(t + 1) * N], ACT.Exp,
                                             bias=head_negmax[:, h % 2, t:t + 1], scale=HEAD ** -0.5,
                                             accum_out=head_sum[:, h % 2, t:t + 1])
                    ins.then_inc(probs_exp, 1)

                def copy_probs(h):
                    act.wait_ge(probs_done, seen.upto(probs_done))
                    act.activation(probs_turned[h % 2][:].rearrange("p t n -> p (t n)"), psum[:, 2 + h % 2, :],
                                   ACT.Copy).then_inc(probs_copied, 1)

                for s in range(HEADS + 1):
                    if s < HEADS:
                        exps(s)
                    if 0 <= s - 1 < HEADS:
                        copy_probs(s - 1)
                act.wait_ge(context_ready, seen.upto(context_ready, HEADS))
                for b in range(3):
                    split_cols(context, context_high, b)

            def l1_gnn():
                edge_layer(0)
                edge_layer(1)

            def l1_ffn():
                self_attention()
                experts(1)

            def l2_gnn():
                edge_layer(2)
                edge_layer(3)

            def l3_gnn():
                catch_up(SLOTS_AT + 1)
                take_root(T)
                copy_turned(cols, parts=cols_high)
                take_root(T)
                catch_up(SLOTS_AT + 3)
                take_root(SLOTS)

            def l3_ffn():
                take_root(T)
                take_root(T)
                copy_turned(cols)
                for target in (mixing[:], dispatch[:]):
                    act.wait_ge(exp_asked, seen.upto(exp_asked))
                    act.activation(target, target, ACT.Exp).then_inc(exp_ready, 1)

                def take_slots(at):
                    rounds = (at - place[0]) // RING
                    with act.Fori(0, rounds) as i:
                        for a in range(RING):
                            take_high(i, a)
                    place[0] += rounds * RING
                    catch_up(at)

                take_slots(SLOTS_AT + SLOTS + 3)
                act.wait_ge(slot_pre, seen.upto(slot_pre))
                act.activation(slot_hidden[:], slot_hidden[:], ACT.Gelu).then_inc(slot_act, 1)
                take_slots(STREAM)

            for stage in (l0_gnn, lambda: experts(0), l1_gnn, l1_ffn, l2_gnn, lambda: experts(2), l3_gnn,
                          l3_ffn):
                stage()

        @block.vector
        def _(dve):
            seen = Counts()
            place = [0]

            def take_low(turn=None, ahead=0):
                n = place[0] + ahead
                dve.wait_ge(high_ready, n + 1 if turn is None else turn * RING + (n + 1))
                dve.tensor_tensor(low[n % RING][:], ring[n % RING][:], high[n % RING][:].bitcast(F32), ALU.subtract)\
                    .then_inc(ring_taken, 1)
                if turn is None:
                    place[0] += 1

            def catch_up(at):
                while place[0] < at:
                    take_low()

            def split_cols(source, parts, tiles=K):
                for b in range(tiles // 2):
                    two = slice(2 * b, 2 * b + 2)
                    dve.wait_ge(cols_high_ready, seen.upto(cols_high_ready))
                    dve.tensor_tensor(parts[1][:, two, :], source[:, two, :], parts[0][:, two, :].bitcast(F32),
                                      ALU.subtract).then_inc(cols_split, 1)

            def ask_root(n, p=P):
                dve.sem_inc(root_asked, 1)
                dve.wait_ge(root_ready, seen.upto(root_ready))

            def row_stats(t):
                for h in range(2):
                    ins = dve.bn_stats(stats[:, t, h, :], x[:, t, h * HALF:(h + 1) * HALF])
                return ins

            def layernorm(target, first=0):
                for t in range(first, T):
                    ins = row_stats(t)
                ins.then_inc(vector_wrote, 1)
                dve.wait_ge(vector_wrote, seen.upto(vector_wrote))
                for t in range(T):
                    ins = dve.bn_aggr(moments[:, t, :], stats[:, t, :, :].rearrange("p a b -> p (a b)"))
                ins.then_inc(vector_wrote, 1)
                dve.wait_ge(vector_wrote, seen.upto(vector_wrote))
                dve.tensor_scalar(root[:, 0:T], moments[:, :, 1], 1e-5, None, ALU.add).then_inc(root_asked, 1)
                dve.wait_ge(root_ready, seen.upto(root_ready))
                dve.reciprocal(inverse[:], root[:, 0:T]).then_inc(vector_wrote, 1)
                dve.wait_ge(vector_wrote, seen.upto(vector_wrote))
                for t in range(T):
                    ins = dve.tensor_scalar(target[:, t, 0:D], x[:, t, :], moments[:, t, 0:1], inverse[:, t:t + 1],
                                            ALU.subtract, ALU.mult)
                return ins

            def count_edges():
                dve.wait_ge(edges_landed, seen.upto(edges_landed, 16))
                for n, target in ((0, edge_src), (1, edge_dst), (2, edge_key)):
                    dve.tensor_copy(target[:], edge_ints[:, n, :]).then_inc(vector_wrote, 1)
                    dve.wait_ge(vector_wrote, seen.upto(vector_wrote))
                dve.scalar_tensor_tensor(edge_key[:], edge_key[:], float(N), edge_dst[:], ALU.mult, ALU.add)\
                    .then_inc(vector_wrote, 1)
                dve.wait_ge(vector_wrote, seen.upto(vector_wrote))

                def hots(c, q):
                    dve.tensor_scalar(src_hot[q][:], key_iota[:, 0:N], edge_src[:, bass.ds(c, 1)], None, ALU.is_equal)
                    dve.tensor_scalar(key_hot[q][:], key_iota[:], edge_key[:, bass.ds(c, 1)], None, ALU.is_equal)\
                        .then_inc(hot_ready, 1)

                hots(0, 0)
                hots(1, 1)
                with seen.loop(dve, EDGE_TILES // 2 - 1, {hot_used: 2}) as i:
                    for q in range(2):
                        dve.wait_ge(hot_used, seen.upto(hot_used))
                        hots(i * 2 + (2 + q), q)
                seen.upto(hot_used, 2)
                take_low()
                dve.wait_ge(counted, seen.upto(counted))
                for t in range(T):
                    for j, c, n in row_parts(REL * N):
                        ins = dve.tensor_copy(raw_counts[:, t, c:c + n], row_bank(t, j, n))
                ins.then_inc(vector_wrote, 1)
                dve.wait_ge(vector_wrote, seen.upto(vector_wrote))
                dve.sem_inc(raw_ready, 1)
                for t in range(T):
                    dve.tensor_tensor(loop_counts[:, t, :], raw_counts[:, t, 0:N], raw_counts[:, t, N:2 * N],
                                      ALU.add).then_inc(vector_wrote, 1)
                    dve.wait_ge(vector_wrote, seen.upto(vector_wrote))
                    dve.tensor_tensor(loop_counts[:, t, :], loop_counts[:, t, :], raw_counts[:, t, 2 * N:3 * N],
                                      ALU.add).then_inc(vector_wrote, 1)
                    dve.wait_ge(vector_wrote, seen.upto(vector_wrote))
                    dve.tensor_tensor(loop_counts[:, t, node_tile(t)], loop_counts[:, t, node_tile(t)], ident[:],
                                      ALU.add).then_inc(vector_wrote, 1)
                    dve.wait_ge(vector_wrote, seen.upto(vector_wrote))

            def copy_counts():
                dve.wait_ge(counts_turned, seen.upto(counts_turned))
                for b in range(3):
                    ins = dve.tensor_copy(flat_counts[:, 512 * b:512 * b + 512], psum[:, b, :])
                ins.then_inc(vector_wrote, 1)
                dve.wait_ge(vector_wrote, seen.upto(vector_wrote))
                dve.sem_inc(counts_ready, 1)

            def average_counts():
                dve.wait_ge(degree_done, seen.upto(degree_done))
                for j, c, n in row_parts(REL * N):
                    ins = dve.tensor_scalar(in_degree[:, c:c + n], psum[:, 6 + j, 0:n], 1.0, None, ALU.max)
                ins.then_inc(vector_wrote, 1)
                dve.wait_ge(vector_wrote, seen.upto(vector_wrote))
                dve.reciprocal(in_degree[:], in_degree[:]).then_inc(vector_wrote, 1)
                dve.wait_ge(vector_wrote, seen.upto(vector_wrote))
                for t in range(T):
                    ins = dve.tensor_tensor(mean_counts[:, t, :], raw_counts[:, t, :], in_degree[:], ALU.mult)
                ins.then_inc(mean_counts_ready, 1)

            def l0_gnn():
                dve.memset(tiny[:], 0.0).then_inc(vector_wrote, 1)
                dve.wait_ge(vector_wrote, seen.upto(vector_wrote))
                dve.memset(ones[:], 1.0).then_inc(ones_ready, 1)
                dve.wait_ge(constants_ready, seen.upto(constants_ready, 3))
                dve.wait_ge(small_landed, seen.upto(small_landed, 16))
                count_edges()
                catch_up(3)
                dve.wait_ge(x_landed, seen.upto(x_landed, 16))
                layernorm(rows).then_inc(rows_ready, 1)
                copy_counts()
                for layer in range(2):
                    chunk = [chunk_buffer(q, ALPHA_AT[layer]) for q in range(CHUNK_RING)]
                    split_cols(cols if layer == 0 else hidden, (cols_high, cols_low))
                    if layer == 0:
                        catch_up(5)
                        average_counts()
                    for r in range(REL):
                        for b in range(3):
                            two = slice(2 * b, 2 * b + 2)
                            dve.wait_ge(aggregate_high_ready, seen.upto(aggregate_high_ready))
                            dve.tensor_tensor(aggregate_low[r % 2][:, two, :].rearrange("p k n -> p (k n)"),
                                              psum[:, b, :],
                                              aggregate_high[r % 2][:, two, :].bitcast(F32)
                                              .rearrange("p k n -> p (k n)"), ALU.subtract)\
                                .then_inc(aggregate_ready, 1)
                        take_low()
                        take_low()
                    take_low()
                    assert place[0] == ALPHA_AT[layer]
                    dve.wait_ge(rows_done, seen.upto(rows_done))
                    dve.wait_ge(bias_landed, seen.upto(bias_landed, 16))
                    for t in range(T):
                        for j, c, n in row_parts(D):
                            ins = dve.tensor_tensor(rows[:, t, c:c + n], row_bank(t, j, n), bias[:, c:c + n], ALU.add)
                    ins.then_inc(vector_wrote, 1)
                    dve.wait_ge(vector_wrote, seen.upto(vector_wrote))
                    dve.sem_inc(bias_used, 1)
                    dve.sem_inc(rows_ready, 1)
                    split_cols(cols, (cols_high, cols_low))

                    def weigh(c, q):
                        dve.wait_ge(chunk_squashed, seen.upto(chunk_squashed))
                        by_query = query_cols[:].rearrange("p k q -> p (k q)")[:, bass.ds(c * L, L)]\
                            .unsqueeze(1).broadcast_to([P, GROUP, L])
                        dve.tensor_tensor(chunk[q][:], chunk[q][:], by_query, ALU.mult).then_inc(chunk_weighted, 1)

                    def reduce(c, q):
                        dve.wait_ge(chunk_folded, seen.upto(chunk_folded))
                        dve.tensor_reduce(flat_gate[:, bass.ds(c * GROUP, WHOLE)], chunk[q][:, 0:WHOLE, :], AX_X,
                                          ALU.add)
                        nodes = GROUP - WHOLE
                        dve.tensor_reduce(flat_gate[:, bass.ds(c * GROUP + WHOLE, nodes)],
                                          psum[:, q, 0:nodes * 16].rearrange("p (n l) -> p n l", n=nodes), AX_X,
                                          ALU.add).then_inc(chunk_reduced, 1)

                    for c in range(2):
                        weigh(c, c)
                    with seen.loop(dve, CHUNKS // CHUNK_RING - 1,
                                   {chunk_squashed: CHUNK_RING, chunk_folded: CHUNK_RING}) as i:
                        for q in range(CHUNK_RING):
                            weigh(i * CHUNK_RING + (q + 2), (q + 2) % CHUNK_RING)
                            reduce(i * CHUNK_RING + q, q)
                    for c in range(CHUNKS - CHUNK_RING, CHUNKS):
                        if c + 2 < CHUNKS:
                            weigh(c + 2, (c + 2) % CHUNK_RING)
                        reduce(c, c % CHUNK_RING)
                        if c == CHUNKS - 3:
                            dve.wait_ge(chunk_reduced, seen.upto(chunk_reduced, CHUNKS - 4))
                            take_low()
                    for b in range(3):
                        two = slice(2 * b, 2 * b + 2)
                        dve.wait_ge(attended_high_ready, seen.upto(attended_high_ready))
                        dve.tensor_tensor(attended_low[:, two, :].rearrange("p k n -> p (k n)"),
                                          flat_gate[:, 512 * b:512 * b + 512],
                                          attended_high[:, two, :].bitcast(F32).rearrange("p k n -> p (k n)"),
                                          ALU.subtract).then_inc(attended_split, 1)
                    dve.wait_ge(chunk_reduced, seen.upto(chunk_reduced, 4))
                    take_low()
                    take_low()
                    dve.wait_ge(tanh_ready, seen.upto(tanh_ready))
                    dve.tensor_tensor(flat_hidden, flat_hidden, flat_cols, ALU.subtract).then_inc(vector_wrote, 1)
                    dve.wait_ge(vector_wrote, seen.upto(vector_wrote))
                    for _ in range(3):
                        take_low()
                    dve.wait_ge(alpha_ready, seen.upto(alpha_ready, 6))
                    dve.tensor_tensor(flat_hidden, flat_hidden, alpha[:].rearrange("p k n -> p (k n)"), ALU.mult)\
                        .then_inc(vector_wrote, 1)
                    dve.wait_ge(vector_wrote, seen.upto(vector_wrote))
                    dve.tensor_tensor(flat_hidden, flat_hidden, flat_cols, ALU.add).then_inc(vector_wrote, 1)
                    dve.wait_ge(vector_wrote, seen.upto(vector_wrote))
                    dve.sem_inc(hidden_ready, 1)
                    take_low()
                dve.wait_ge(turned_back, seen.upto(turned_back, 6))
                for b in range(3):
                    ins = dve.tensor_tensor(flat_x[:, 512 * b:512 * b + 512], flat_x[:, 512 * b:512 * b + 512],
                                            psum[:, b, :], ALU.add)
                ins.then_inc(vector_wrote, 1)
                dve.wait_ge(vector_wrote, seen.upto(vector_wrote))
                dve.sem_inc(arena_free, 1)

            def take_logits(layer):
                count = EXPERTS[layer]
                scores = logits[:, :, 0:count]
                dve.wait_ge(logits_done, seen.upto(logits_done))
                of = psum[:, 3, 0:32].rearrange("p (t e) -> p t e", t=T)[:, :, 0:count]
                if layer == 0:
                    dve.tensor_tensor(scores, of, small_at("br", 0, 8).unsqueeze(1).broadcast_to([P, T, 8]),
                                      ALU.add).then_inc(vector_wrote, 1)
                    dve.wait_ge(vector_wrote, seen.upto(vector_wrote))
                    dve.sem_inc(logits_taken, 1)
                else:
                    dve.tensor_copy(scores, of).then_inc(vector_wrote, 1)
                    dve.wait_ge(vector_wrote, seen.upto(vector_wrote))
                    dve.sem_inc(logits_taken, 1)

            def route(layer):
                count = EXPERTS[layer]
                scores = logits[:, :, 0:count]
                if layer != 0:
                    dve.tensor_reduce(row_max[:], scores, AX_X, ALU.max).then_inc(vector_wrote, 1)
                    dve.wait_ge(vector_wrote, seen.upto(vector_wrote))
                    for t in range(T):
                        ins = dve.tensor_scalar(logits[:, t, 0:count], logits[:, t, 0:count], row_max[:, t:t + 1],
                                                None, ALU.subtract)
                    ins.then_inc(exp_asked, 1)
                    dve.wait_ge(exp_ready, seen.upto(exp_ready))
                    dve.tensor_reduce(row_sum[:], scores, AX_X, ALU.add).then_inc(vector_wrote, 1)
                    dve.wait_ge(vector_wrote, seen.upto(vector_wrote))
                    dve.reciprocal(row_sum[:], row_sum[:]).then_inc(vector_wrote, 1)
                    dve.wait_ge(vector_wrote, seen.upto(vector_wrote))
                    for t in range(T):
                        dve.tensor_scalar(logits[:, t, 0:count], logits[:, t, 0:count], row_sum[:, t:t + 1],
                                          None, ALU.mult).then_inc(vector_wrote, 1)
                        dve.wait_ge(vector_wrote, seen.upto(vector_wrote))
                for t in range(T):
                    dve.max(top[:, t, :], logits[:, t, 0:count]).then_inc(vector_wrote, 1)
                    dve.wait_ge(vector_wrote, seen.upto(vector_wrote))
                    dve.max_index(top_at[:, t, :], top[:, t, :], logits[:, t, 0:count]).then_inc(vector_wrote, 1)
                    dve.wait_ge(vector_wrote, seen.upto(vector_wrote))
                dve.tensor_copy(top_place[:], top_at[:]).then_inc(vector_wrote, 1)
                dve.wait_ge(vector_wrote, seen.upto(vector_wrote))
                if layer == 0:
                    dve.tensor_tensor(gap[:], top[:, :, 1], top[:, :, 0], ALU.subtract).then_inc(exp_asked, 1)
                    dve.wait_ge(exp_ready, seen.upto(exp_ready))
                    dve.tensor_scalar(row_sum[:], gap[:], 1.0, None, ALU.add).then_inc(vector_wrote, 1)
                    dve.wait_ge(vector_wrote, seen.upto(vector_wrote))
                    dve.reciprocal(top_weight[:, :, 0], row_sum[:]).then_inc(vector_wrote, 1)
                    dve.wait_ge(vector_wrote, seen.upto(vector_wrote))
                    dve.tensor_tensor(top_weight[:, :, 1], gap[:], top_weight[:, :, 0], ALU.mult)\
                        .then_inc(vector_wrote, 1)
                    dve.wait_ge(vector_wrote, seen.upto(vector_wrote))
                else:
                    dve.tensor_tensor(row_sum[:], top[:, :, 0], top[:, :, 1], ALU.add).then_inc(vector_wrote, 1)
                    dve.wait_ge(vector_wrote, seen.upto(vector_wrote))
                    dve.tensor_scalar(row_sum[:], row_sum[:], 1e-20 if layer == 1 else 1e-8, None, ALU.add)\
                        .then_inc(vector_wrote, 1)
                    dve.wait_ge(vector_wrote, seen.upto(vector_wrote))
                    dve.reciprocal(row_sum[:], row_sum[:]).then_inc(vector_wrote, 1)
                    dve.wait_ge(vector_wrote, seen.upto(vector_wrote))
                    for n in range(2):
                        dve.tensor_tensor(top_weight[:, :, n], top[:, :, n], row_sum[:], ALU.mult)\
                            .then_inc(vector_wrote, 1)
                        dve.wait_ge(vector_wrote, seen.upto(vector_wrote))
                for t in range(T):
                    for n, target in ((0, combine), (1, second)):
                        dve.tensor_scalar(target[:, t, 0:count], iota[:, 0:count], top_place[:, t, n:n + 1],
                                          top_weight[:, t, n:n + 1], ALU.is_equal, ALU.mult).then_inc(vector_wrote, 1)
                        dve.wait_ge(vector_wrote, seen.upto(vector_wrote))
                dve.tensor_tensor(combine[:, :, 0:count], combine[:, :, 0:count], second[:, :, 0:count], ALU.add)\
                    .then_inc(vector_wrote, 1)
                dve.wait_ge(vector_wrote, seen.upto(vector_wrote))
                if layer == 0:
                    pairs = unit_weight[:, :, 0:16].rearrange("p t (e h) -> p t e h", h=2)
                    for h in range(2):
                        dve.tensor_copy(pairs[:, :, :, h], combine[:, :, 0:8]).then_inc(vector_wrote, 1)
                        dve.wait_ge(vector_wrote, seen.upto(vector_wrote))
                    dve.sem_inc(combine_ready, 1)
                else:
                    dve.tensor_copy(unit_weight[:, :, 0:count], combine[:, :, 0:count]).then_inc(vector_wrote, 1)
                    dve.wait_ge(vector_wrote, seen.upto(vector_wrote))
                    dve.memset(unit_weight[:, :, count:count + 2], 1.0 if layer == 1 else 0.5)\
                        .then_inc(vector_wrote, 1)
                    dve.wait_ge(vector_wrote, seen.upto(vector_wrote))

            def experts(layer):
                if layer != 1:
                    layernorm(rows, first=1 if layer == 2 else 0).then_inc(vector_wrote, 1)
                    dve.wait_ge(vector_wrote, seen.upto(vector_wrote))
                    dve.sem_inc(rows_ready, 1)
                units = UNITS[layer]
                catch_up(UNITS_AT[layer] + 3)
                split_cols(cols, (cols_high, cols_low))
                take_logits(layer)

                def clip_gate(u):
                    for f in range(3):
                        if f != 1:
                            dve.wait_ge(gate_done, seen.upto(gate_done))
                        ins = dve.tensor_scalar(gate_part[:, f, :], unit_tile(0, f),
                                                small[:, bass.ds(u * 6 + (SMALL["unit_bias"][0] + f), 1)], 7.0,
                                                ALU.add, ALU.min)
                        if f > 0:
                            ins.then_inc(gate_clipped, 1)

                def activate(u):
                    if layer == 0:
                        for f in range(3):
                            if f != 1:
                                dve.wait_ge(up_done, seen.upto(up_done))
                            ins = dve.tensor_scalar(up_part[:, f, :], unit_tile(1, f),
                                                    small[:, bass.ds(u * 6 + (SMALL["unit_bias"][0] + 3 + f), 1)],
                                                    7.0, ALU.add, ALU.min)
                        ins.then_inc(vector_wrote, 1)
                        dve.wait_ge(vector_wrote, seen.upto(vector_wrote))
                        dve.tensor_scalar(up_part[:], up_part[:], -7.0, 1.0, ALU.max, ALU.add)
                        dve.wait_ge(squashed, seen.upto(squashed, 2))
                        dve.tensor_tensor(gate_part[:], gate_part[:], squash[:], ALU.mult).then_inc(vector_wrote, 1)
                        dve.wait_ge(vector_wrote, seen.upto(vector_wrote))
                        dve.tensor_tensor(act_cols[:], gate_part[:], up_part[:], ALU.mult).then_inc(vector_wrote, 1)
                    else:
                        for last, tiles in ((0, slice(0, 2)), (1, slice(2, 3))):
                            dve.wait_ge(squashed, seen.upto(squashed))
                            dve.wait_ge(up_done, seen.upto(up_done))
                            ins = dve.tensor_tensor(act_cols[:, tiles, :].rearrange("p f n -> p (f n)"),
                                                    squash[:, tiles, :].rearrange("p f n -> p (f n)"),
                                                    unit_bank(1, last), ALU.mult)
                        ins.then_inc(vector_wrote, 1)
                    dve.wait_ge(vector_wrote, seen.upto(vector_wrote))
                    dve.tensor_copy(act_high[:], act_cols[:]).then_inc(vector_wrote, 1)
                    dve.wait_ge(vector_wrote, seen.upto(vector_wrote))
                    dve.tensor_tensor(act_low[:], act_cols[:], act_high[:].bitcast(F32), ALU.subtract)\
                        .then_inc(act_ready, 1)

                def add_unit(u):
                    for t in range(T):
                        for j, c, n in row_parts(D):
                            ins = dve.scalar_tensor_tensor(x[:, t, c:c + n], row_bank(t, j, n),
                                                           unit_weight[:, t, bass.ds(u, 1)], x[:, t, c:c + n],
                                                           ALU.mult, ALU.add)
                    ins.then_inc(down_taken, 1)

                def step(u, turn):
                    take_low(turn)
                    if layer == 0:
                        clip_gate(u + 1)
                    take_low(turn, 1)
                    dve.wait_ge(down_done, seen.upto(down_done))
                    take_low(turn, 2)
                    add_unit(u)
                    activate(u + 1)

                if layer == 0:
                    clip_gate(0)
                take_low()
                activate(0)
                take_low()
                if layer == 0:
                    clip_gate(1)
                take_low()
                route(layer)
                dve.wait_ge(down_done, seen.upto(down_done))
                take_low()
                add_unit(0)
                if layer == 0:
                    dve.wait_ge(combine_turned, seen.upto(combine_turned))
                    dve.tensor_copy(combine_cols[0:8, :], psum[0:8, 7, 0:N]).then_inc(combine_cols_ready, 1)
                activate(1)
                if layer == 0:
                    dve.wait_ge(down_done, seen.upto(down_done))
                    for t in range(T):
                        for j, c, n in row_parts(D):
                            ins = dve.tensor_tensor(x[:, t, c:c + n], x[:, t, c:c + n], row_bank(t, j, n), ALU.add)
                    ins.then_inc(down_taken, 1)
                grows = {squashed: 2, up_done: 2, down_done: 1}
                if layer == 0:
                    grows |= {gate_done: 2, vector_wrote: 4}
                else:
                    grows |= {vector_wrote: 2}
                with seen.loop(dve, units - 3, grows) as i:
                    step(i + 1, i)
                place[0] += 3 * (units - 3)
                take_low()
                if layer == 0:
                    clip_gate(units - 1)
                take_low()
                dve.wait_ge(down_done, seen.upto(down_done))
                add_unit(units - 2)
                activate(units - 1)
                take_low()
                take_low()
                assert place[0] == UNITS_AT[layer] + 3 * units + 2
                dve.wait_ge(down_done, seen.upto(down_done))
                add_unit(units - 1)
                dve.wait_ge(down_taken, seen.upto(down_taken, units + (1 if layer == 0 else 0)))
                if layer == 2:
                    dve.sem_inc(arena_free, 1)

            def edge_layer(n):
                layer = EDGE_LAYERS[n]
                rel, heads, width = layer["rel"], layer["heads"], layer["width"]
                out_width = heads * width
                messages = message_rows(layer)
                if n % 2 == 0:
                    layernorm(rows).then_inc(vector_wrote, 1)
                    dve.wait_ge(vector_wrote, seen.upto(vector_wrote))
                    dve.sem_inc(rows_ready, 1)
                catch_up(EDGES_AT[n] + 3)
                split_cols(wide_cols if n == 1 else cols, (wide_high, wide_low) if n == 1 else (cols_high, cols_low),
                           8 if n == 1 else K)
                if n == 0:
                    for t in range(T):
                        dve.tensor_tensor(all_counts[:, t, :], counts[:, t, 0, :], counts[:, t, 1, :], ALU.add)\
                            .then_inc(vector_wrote, 1)
                        dve.wait_ge(vector_wrote, seen.upto(vector_wrote))
                        dve.tensor_tensor(all_counts[:, t, :], all_counts[:, t, :], counts[:, t, 2, :], ALU.add)\
                            .then_inc(vector_wrote, 1)
                        dve.wait_ge(vector_wrote, seen.upto(vector_wrote))
                        dve.tensor_scalar(absent[:, t, 0:N], all_counts[:, t, :], 0.0, LOW, ALU.is_equal,
                                          ALU.mult).then_inc(vector_wrote, 1)
                        dve.wait_ge(vector_wrote, seen.upto(vector_wrote))
                        dve.tensor_reduce(dinv[:, t:t + 1], all_counts[:, t, :], AX_X, ALU.add)\
                            .then_inc(vector_wrote, 1)
                        dve.wait_ge(vector_wrote, seen.upto(vector_wrote))
                    dve.tensor_scalar(dinv[:], dinv[:], 1.0, None, ALU.add).then_inc(vector_wrote, 1)
                    dve.wait_ge(vector_wrote, seen.upto(vector_wrote))
                if n == 2:
                    for t in range(T):
                        dve.tensor_scalar(absent[:, t, :], counts[:, t].rearrange("p r n -> p (r n)"), 0.0, LOW,
                                          ALU.is_equal, ALU.mult).then_inc(vector_wrote, 1)
                        dve.wait_ge(vector_wrote, seen.upto(vector_wrote))
                catch_up(EDGES_AT[n] + (5 if rel == 1 else 4))
                for r in range(rel):
                    dve.wait_ge(rows_done, seen.upto(rows_done))
                    for t in range(T):
                        for j, c, size in row_parts(out_width):
                            ins = dve.tensor_copy(messages[:, r, t, c:c + size], row_bank(t, j, size))
                    ins.then_inc(vector_wrote, 1)
                    dve.wait_ge(vector_wrote, seen.upto(vector_wrote))
                    dve.sem_inc(rows_ready, 1)
                    catch_up(EDGES_AT[n] + ((6,) if rel == 1 else (6, 8, 9))[r])
                dve.wait_ge(query_keys_done, seen.upto(query_keys_done))
                dve.tensor_copy(queries_keys[:, :, 0:rel, 0:2 * heads],
                                psum[:, 7, 0:T * rel * 16].rearrange("p (t r c) -> p t r c", t=T, r=rel)
                                [:, :, :, 0:2 * heads]).then_inc(vector_wrote, 1)
                dve.wait_ge(vector_wrote, seen.upto(vector_wrote))
                for t in range(T):
                    dve.tensor_copy(keys[:, t, 0:rel * heads].rearrange("p (r h) -> p r h", r=rel),
                                    queries_keys[:, t, 0:rel, heads:2 * heads]).then_inc(vector_wrote, 1)
                    dve.wait_ge(vector_wrote, seen.upto(vector_wrote))
                dve.sem_inc(keys_ready, 1)
                dve.wait_ge(bias_landed, seen.upto(bias_landed, 16))
                target = wide_rows if n == 0 else rows
                items = [(t, h) for h in range(heads) for t in range(T)]

                def highest(i):
                    t, h = items[i]
                    scores = edge_scores[i % 2][:, 0:rel * N]
                    dve.wait_ge(lifted, seen.upto(lifted))
                    dve.scalar_tensor_tensor(scores, scores, 0.2, scores, ALU.mult, ALU.max).then_inc(vector_wrote, 1)
                    dve.wait_ge(vector_wrote, seen.upto(vector_wrote))
                    dve.tensor_tensor_reduce(scores, scores, absent[:, t, 0:rel * N], 1.0, -3e38, ALU.add,
                                             ALU.max, edge_max[:, i % 2:i % 2 + 1]).then_inc(vector_wrote, 1)
                    dve.wait_ge(vector_wrote, seen.upto(vector_wrote))
                    dve.tensor_scalar(edge_negmax[:, i % 2:i % 2 + 1], edge_max[:, i % 2:i % 2 + 1], -1.0, None,
                                      ALU.mult).then_inc(edge_max_ready, 1)

                def weigh(i):
                    t, h = items[i]
                    by = all_counts[:, t, :] if rel == 1 else counts[:, t].rearrange("p r n -> p (r n)")
                    q = i % 4
                    dve.wait_ge(edge_exp_ready, seen.upto(edge_exp_ready))
                    dve.tensor_tensor_reduce(edge_exp[i % 2][:, 0:rel * N], edge_exp[i % 2][:, 0:rel * N], by,
                                             1.0, 0.0, ALU.mult, ALU.add, edge_sum[:, q:q + 1])\
                        .then_inc(vector_wrote, 1)
                    dve.wait_ge(vector_wrote, seen.upto(vector_wrote))
                    dve.sem_inc(edge_weighted, 1)
                    dve.tensor_scalar(edge_sum[:, q:q + 1], edge_sum[:, q:q + 1], 1e-16, None, ALU.add)\
                        .then_inc(vector_wrote, 1)
                    dve.wait_ge(vector_wrote, seen.upto(vector_wrote))
                    dve.reciprocal(edge_inverse[:, q:q + 1], edge_sum[:, q:q + 1]).then_inc(vector_wrote, 1)
                    dve.wait_ge(vector_wrote, seen.upto(vector_wrote))

                def store(i):
                    t, h = items[i]
                    q = i % 4
                    dve.wait_ge(mixed, seen.upto(mixed))
                    for j, c, size in row_parts(width):
                        bank = 6 + j if width > 512 else 6 + i % 2
                        at = h * width + c
                        ins = dve.scalar_tensor_tensor(target[:, t, at:at + size], psum[:, bank, 0:size],
                                                       edge_inverse[:, q:q + 1], bias[:, at:at + size], ALU.mult,
                                                       ALU.add)
                    ins.then_inc(vector_wrote, 1)
                    dve.wait_ge(vector_wrote, seen.upto(vector_wrote))
                    dve.sem_inc(stored, 1)

                last = len(items)
                for s in range(last + 3):
                    if s < last:
                        highest(s)
                    if 0 <= s - 1 < last:
                        weigh(s - 1)
                    if 0 <= s - 3 < last:
                        store(s - 3)
                        if n % 2 == 1:
                            t = items[s - 3][0]
                            dve.tensor_tensor(x[:, t, :], x[:, t, :], rows[:, t, :], ALU.add)\
                                .then_inc(vector_wrote, 1)
                            dve.wait_ge(vector_wrote, seen.upto(vector_wrote))
                            if t == 0:
                                row_stats(t)
                dve.sem_inc(bias_used, 1)
                if n == 0:
                    dve.sem_inc(rows_ready, 1)
                elif n == 2:
                    dve.tensor_scalar(wide_rows[:, :, 0:D], rows[:], 0.0, None, ALU.min).then_inc(exp_asked, 1)
                    dve.tensor_scalar(rows[:], rows[:], 0.0, None, ALU.max).then_inc(vector_wrote, 1)
                    dve.wait_ge(vector_wrote, seen.upto(vector_wrote))
                    dve.wait_ge(exp_ready, seen.upto(exp_ready))
                    dve.scalar_tensor_tensor(rows[:], wide_rows[:, :, 0:D], -1.0, rows[:], ALU.add, ALU.add)\
                        .then_inc(vector_wrote, 1)
                    dve.wait_ge(vector_wrote, seen.upto(vector_wrote))
                    dve.sem_inc(rows_ready, 1)

            def rms_rows(target, source):
                for t in range(T):
                    dve.tensor_tensor_reduce(normed[:, t, :], source[:, t, :], source[:, t, :], 1.0, 0.0,
                                             ALU.mult, ALU.add, root[:, t:t + 1]).then_inc(vector_wrote, 1)
                    dve.wait_ge(vector_wrote, seen.upto(vector_wrote))
                dve.tensor_scalar(root[:, 0:T], root[:, 0:T], 1.0 / D, 1e-6, ALU.mult, ALU.add)\
                    .then_inc(root_asked, 1)
                dve.wait_ge(root_ready, seen.upto(root_ready))
                dve.reciprocal(inverse[:], root[:, 0:T]).then_inc(vector_wrote, 1)
                dve.wait_ge(vector_wrote, seen.upto(vector_wrote))
                for t in range(T):
                    dve.tensor_scalar(target[:, t, :], source[:, t, :], inverse[:, t:t + 1], None, ALU.mult)\
                        .then_inc(vector_wrote, 1)
                    dve.wait_ge(vector_wrote, seen.upto(vector_wrote))
                dve.sem_inc(rows_ready, 1)

            def self_attention():
                layernorm(rows, first=1).then_inc(vector_wrote, 1)
                dve.wait_ge(vector_wrote, seen.upto(vector_wrote))
                rms_rows(normed, rows)
                catch_up(HEADS_AT + 3)
                split_cols(cols, (cols_high, cols_low))
                catch_up(HEADS_AT + 8)
                dve.wait_ge(rows_done, seen.upto(rows_done))
                for t in range(T):
                    for j, c, n in row_parts(D):
                        ins = dve.tensor_copy(values[:, t, c:c + n], row_bank(t, j, n))
                ins.then_inc(vector_wrote, 1)
                dve.wait_ge(vector_wrote, seen.upto(vector_wrote))
                dve.sem_inc(rows_ready, 1)

                take_low()

                def highest(h):
                    q = h % 2
                    dve.wait_ge(scored, seen.upto(scored))
                    dve.tensor_reduce(head_max[:, q, :], psum[:, q, :].rearrange("p (t n) -> p t n", t=T), AX_X,
                                      ALU.max).then_inc(vector_wrote, 1)
                    dve.wait_ge(vector_wrote, seen.upto(vector_wrote))
                    dve.tensor_scalar(head_negmax[:, q, :], head_max[:, q, :], -HEAD ** -0.5, None, ALU.mult)\
                        .then_inc(head_max_ready, 1)

                def normalise(h):
                    q = h % 2
                    dve.wait_ge(probs_exp, seen.upto(probs_exp))
                    dve.reciprocal(head_inverse[:, q, :], head_sum[:, q, :]).then_inc(vector_wrote, 1)
                    dve.wait_ge(vector_wrote, seen.upto(vector_wrote))
                    for t in range(T):
                        ins = dve.tensor_scalar(probs[q][:, t, :], probs[q][:, t, :], head_inverse[:, q, t:t + 1],
                                                None, ALU.mult)
                    ins.then_inc(probs_ready, 1)

                def store(h):
                    at = h % 2 * HEAD
                    dve.wait_ge(context_done, seen.upto(context_done))
                    dve.tensor_copy(context[at:at + HEAD, h // 2, :], psum[at:at + HEAD, 4 + h % 2, 0:N])\
                        .then_inc(vector_wrote, 1)
                    dve.wait_ge(vector_wrote, seen.upto(vector_wrote))
                    dve.sem_inc(context_ready, 1)

                for s in range(HEADS + 2):
                    if 0 <= s - 1 < HEADS:
                        normalise(s - 1)
                    if s < HEADS:
                        highest(s)
                    if 0 <= s - 2 < HEADS:
                        store(s - 2)
                split_cols(context, (context_high, context_low))
                dve.wait_ge(rows_done, seen.upto(rows_done))
                for t in range(T):
                    for j, c, n in row_parts(D):
                        ins = dve.tensor_tensor(rows[:, t, c:c + n], rows[:, t, c:c + n], row_bank(t, j, n), ALU.add)
                ins.then_inc(vector_wrote, 1)
                dve.wait_ge(vector_wrote, seen.upto(vector_wrote))
                dve.tensor_tensor(x[:], x[:], rows[:], ALU.add).then_inc(vector_wrote, 1)
                dve.wait_ge(vector_wrote, seen.upto(vector_wrote))
                rms_rows(rows, rows)

            def l1_gnn():
                edge_layer(0)
                edge_layer(1)

            def l1_ffn():
                self_attention()
                experts(1)

            def l2_gnn():
                edge_layer(2)
                edge_layer(3)

            def l3_gnn():
                layernorm(rows).then_inc(vector_wrote, 1)
                dve.wait_ge(vector_wrote, seen.upto(vector_wrote))
                dve.sem_inc(rows_ready, 1)
                catch_up(SLOTS_AT + 1)
                split_cols(cols, (cols_high, cols_low))
                dve.tensor_copy(root[:, 0:T], dinv[:]).then_inc(vector_wrote, 1)
                dve.wait_ge(vector_wrote, seen.upto(vector_wrote))
                dve.sem_inc(root_asked, 1)
                dve.wait_ge(root_ready, seen.upto(root_ready))
                dve.reciprocal(dinv[:], root[:, 0:T]).then_inc(vector_wrote, 1)
                dve.wait_ge(vector_wrote, seen.upto(vector_wrote))
                dve.wait_ge(slots_landed, seen.upto(slots_landed, 48))
                dve.tensor_tensor(phi_squares[:], phi[:], phi[:], ALU.mult).then_inc(vector_wrote, 1)
                dve.wait_ge(vector_wrote, seen.upto(vector_wrote))
                dve.sem_inc(phi_squared, 1)
                dve.wait_ge(rows_done, seen.upto(rows_done))
                for t in range(T):
                    for j, c, n in row_parts(D):
                        ins = dve.tensor_scalar(rows[:, t, c:c + n], row_bank(t, j, n), dinv[:, t:t + 1], None,
                                                ALU.mult)
                ins.then_inc(vector_wrote, 1)
                dve.wait_ge(vector_wrote, seen.upto(vector_wrote))
                dve.sem_inc(rows_ready, 1)
                catch_up(SLOTS_AT + 3)
                dve.wait_ge(phi_summed, seen.upto(phi_summed))
                dve.tensor_copy(root[:], psum[:, 7, 0:SLOTS]).then_inc(root_asked, 1)
                dve.wait_ge(root_ready, seen.upto(root_ready))
                dve.tensor_scalar(phi_scale[:], root[:], 1e-12, None, ALU.max).then_inc(vector_wrote, 1)
                dve.wait_ge(vector_wrote, seen.upto(vector_wrote))
                dve.reciprocal(phi_scale[:], phi_scale[:]).then_inc(vector_wrote, 1)
                dve.wait_ge(vector_wrote, seen.upto(vector_wrote))
                dve.tensor_scalar(phi_scale[:], phi_scale[:], small_at("scale"), None, ALU.mult)\
                    .then_inc(vector_wrote, 1)
                dve.wait_ge(vector_wrote, seen.upto(vector_wrote))
                dve.tensor_tensor(phi[:], phi[:], phi_scale[:].unsqueeze(1).broadcast_to([P, K, SLOTS]),
                                  ALU.mult).then_inc(vector_wrote, 1)
                dve.wait_ge(vector_wrote, seen.upto(vector_wrote))
                dve.sem_inc(phi_ready, 1)
                dve.wait_ge(rows_done, seen.upto(rows_done))
                dve.wait_ge(bias_landed, seen.upto(bias_landed, 16))
                for t in range(T):
                    for j, c, n in row_parts(D):
                        ins = dve.scalar_tensor_tensor(rows[:, t, c:c + n], row_bank(t, j, n), dinv[:, t:t + 1],
                                                       bias[:, c:c + n], ALU.mult, ALU.add)
                ins.then_inc(vector_wrote, 1)
                dve.wait_ge(vector_wrote, seen.upto(vector_wrote))
                dve.sem_inc(bias_used, 1)
                dve.tensor_tensor(x[:], x[:], rows[:], ALU.add).then_inc(vector_wrote, 1)
                dve.wait_ge(vector_wrote, seen.upto(vector_wrote))

            def l3_ffn():
                layernorm(rows).then_inc(vector_wrote, 1)
                dve.wait_ge(vector_wrote, seen.upto(vector_wrote))
                for t in range(T):
                    dve.tensor_tensor_reduce(squares[:], rows[:, t, :], rows[:, t, :], 1.0, 0.0, ALU.mult,
                                             ALU.add, root[:, t:t + 1]).then_inc(vector_wrote, 1)
                    dve.wait_ge(vector_wrote, seen.upto(vector_wrote))
                dve.sem_inc(root_asked, 1)
                dve.wait_ge(root_ready, seen.upto(root_ready))
                dve.tensor_scalar(root[:, 0:T], root[:, 0:T], 1e-12, None, ALU.max).then_inc(vector_wrote, 1)
                dve.wait_ge(vector_wrote, seen.upto(vector_wrote))
                dve.reciprocal(inverse[:], root[:, 0:T]).then_inc(vector_wrote, 1)
                dve.wait_ge(vector_wrote, seen.upto(vector_wrote))
                for t in range(T):
                    dve.tensor_scalar(rows[:, t, :], rows[:, t, :], inverse[:, t:t + 1], None, ALU.mult)\
                        .then_inc(vector_wrote, 1)
                    dve.wait_ge(vector_wrote, seen.upto(vector_wrote))
                dve.sem_inc(rows_ready, 1)
                dve.wait_ge(slot_logits_done, seen.upto(slot_logits_done))
                dve.tensor_reduce(soft[:, 0:2], psum[:, 3, 0:T * SLOTS].rearrange("p (t n) -> p t n", t=T), AX_X,
                                  ALU.max).then_inc(vector_wrote, 1)
                dve.wait_ge(vector_wrote, seen.upto(vector_wrote))
                for t in range(T):
                    ins = dve.tensor_scalar(mixing[:, t, :], psum[:, 3, t * SLOTS:(t + 1) * SLOTS], soft[:, t:t + 1],
                                            None, ALU.subtract)
                ins.then_inc(vector_wrote, 1)
                dve.wait_ge(vector_wrote, seen.upto(vector_wrote))
                dve.sem_inc(exp_asked, 1)
                dve.tensor_reduce(soft[0:SLOTS, 2:3], psum[0:SLOTS, 4, 0:N], AX_X, ALU.max).then_inc(vector_wrote, 1)
                dve.wait_ge(vector_wrote, seen.upto(vector_wrote))
                dve.tensor_scalar(dispatch[:], psum[0:SLOTS, 4, 0:N], soft[0:SLOTS, 2:3], None, ALU.subtract)\
                    .then_inc(exp_asked, 1)
                dve.wait_ge(exp_ready, seen.upto(exp_ready))
                dve.tensor_reduce(soft[:, 4:6], mixing[:], AX_X, ALU.add).then_inc(vector_wrote, 1)
                dve.wait_ge(vector_wrote, seen.upto(vector_wrote))
                dve.reciprocal(soft[:, 4:6], soft[:, 4:6]).then_inc(vector_wrote, 1)
                dve.wait_ge(vector_wrote, seen.upto(vector_wrote))
                for t in range(T):
                    for h in range(2):
                        dve.tensor_scalar(mixing_pair[:, t, h, :], mixing[:, t, :], soft[:, 4 + t:5 + t], None,
                                          ALU.mult)
                dve.wait_ge(exp_ready, seen.upto(exp_ready))
                dve.tensor_reduce(soft[0:SLOTS, 6:7], dispatch[:], AX_X, ALU.add).then_inc(vector_wrote, 1)
                dve.wait_ge(vector_wrote, seen.upto(vector_wrote))
                dve.reciprocal(soft[0:SLOTS, 6:7], soft[0:SLOTS, 6:7]).then_inc(vector_wrote, 1)
                dve.wait_ge(vector_wrote, seen.upto(vector_wrote))
                dve.tensor_scalar(dispatch[:], dispatch[:], soft[0:SLOTS, 6:7], None, ALU.mult)\
                    .then_inc(soft_ready, 1)
                dve.wait_ge(soft_turned, seen.upto(soft_turned))
                dve.tensor_copy(mixing_cols[:], psum[0:SLOT_PAIR, 5, 0:N])
                dve.tensor_copy(dispatch_rows[:].rearrange("p t n -> p (t n)"), psum[:, 6, 0:T * SLOTS])\
                    .then_inc(soft_copied, 1)
                dve.wait_ge(slot_in_done, seen.upto(slot_in_done))
                dve.tensor_copy(slot_in[:].rearrange("p k n -> p (k n)"), psum[:, 7, 0:K * SLOTS])\
                    .then_inc(vector_wrote, 1)
                dve.wait_ge(vector_wrote, seen.upto(vector_wrote))

                dve.tensor_tensor(slot_fold[:], ident[:, 0:SLOTS], ident[:, SLOTS:SLOT_PAIR], ALU.add)

                def pair(source, tiles):
                    dve.tensor_copy(slot_pair[:, 0:tiles, 0:SLOTS], source[:]).then_inc(vector_wrote, 1)
                    dve.wait_ge(vector_wrote, seen.upto(vector_wrote))
                    dve.tensor_tensor(slot_pair[:, 0:tiles, SLOTS:SLOT_PAIR], source[:],
                                      slot_pair[:, 0:tiles, 0:SLOTS].bitcast(F32), ALU.subtract)\
                        .then_inc(vector_wrote, 1)
                    dve.wait_ge(vector_wrote, seen.upto(vector_wrote))

                def mask(slot, q, tiles):
                    both = "p k (h n) -> p (k h) n"
                    dve.scalar_tensor_tensor(slot_mask[q][:, 0:tiles, :].rearrange(both, h=2),
                                             iota[:].unsqueeze(1).broadcast_to([P, 2 * tiles, SLOTS]),
                                             iota[:, bass.ds(slot, 1)],
                                             slot_pair[:, 0:tiles, :].bitcast(F32).rearrange(both, h=2),
                                             ALU.is_equal, ALU.mult).then_inc(mask_ready, 1)

                rounds, rest = divmod(SLOTS - 3, RING)

                def slots(tiles):
                    first = place[0]
                    with dve.Fori(0, rounds) as i:
                        for a in range(RING):
                            take_low(i, a)
                            mask(i * RING + (3 + a), (first + a) % RING, tiles)
                    place[0] += rounds * RING
                    for n in range(SLOTS - rest, SLOTS):
                        q = place[0] % RING
                        take_low()
                        mask(n, q, tiles)

                pair(slot_in, K)
                for n in range(3):
                    mask(n, (SLOTS_AT + n) % RING, K)
                slots(K)
                catch_up(SLOTS_AT + SLOTS + 3)
                dve.wait_ge(slot_sums_done, seen.upto(slot_sums_done))
                dve.tensor_copy(slot_sum[:], psum[:, 3, 0:SLOT_HIDDEN]).then_inc(slot_sums_ready, 1)
                dve.wait_ge(slot_folded, seen.upto(slot_folded))
                dve.tensor_tensor(slot_hidden[:].rearrange("p k n -> p (k n)"), psum[:, 5, 0:3 * SLOTS],
                                  slot_b1[:].rearrange("p k n -> p (k n)"), ALU.add).then_inc(slot_pre, 1)
                dve.wait_ge(slot_act, seen.upto(slot_act))
                pair(slot_hidden, 3)
                for n in range(3):
                    mask(n, (SLOTS_AT + SLOTS + n) % RING, 3)
                slots(3)
                dve.wait_ge(slot_out_done, seen.upto(slot_out_done))
                for j, c, n in row_parts(D):
                    ins = dve.tensor_tensor(slot_out[:, c:c + n], psum[:, 3 + j, 0:n], slot_b2[:, c:c + n], ALU.add)
                ins.then_inc(slot_out_ready, 1)
                dve.wait_ge(rows_done, seen.upto(rows_done))
                for t in range(T):
                    for j, c, n in row_parts(D):
                        ins = dve.tensor_tensor(x[:, t, c:c + n], x[:, t, c:c + n], row_bank(t, j, n), ALU.add)
                ins.then_inc(vector_wrote, 1)
                dve.wait_ge(vector_wrote, seen.upto(vector_wrote))

            for stage in (l0_gnn, lambda: experts(0), l1_gnn, l1_ffn, l2_gnn, lambda: experts(2), l3_gnn,
                          l3_ffn):
                stage()
            dve.sem_inc(x_final, 1)



def _by_columns(w):
    w = w.reshape(K, P, D)
    return [w[:, :, h * HALF:(h + 1) * HALF].transpose(1, 0, 2).reshape(P, -1) for h in range(2)]


def _by_rows(w, pieces=((0, 3), (3, 6))):
    w = w.reshape(-1, P, w.shape[1])
    return [w[a:b].transpose(1, 0, 2).reshape(P, -1) for a, b in pieces]


def _unit(gate, up, down):
    return [gate.reshape(K, P, HALF).transpose(1, 0, 2).reshape(P, -1),
            up.reshape(K, P, HALF).transpose(1, 0, 2).reshape(P, -1)] + _by_rows(down, ((0, 3),))


def _in_order(units):
    pieces = [units[0][GATE], units[0][UP]]
    for unit, after in zip(units, units[1:]):
        pieces += [after[GATE], unit[DOWN], after[UP]]
    return pieces + [units[-1][DOWN]]


def _stream(a):
    pieces = _by_columns(a["L0_gnn_Wg"][:, D:].T)
    for n in (1, 2):
        pieces += _by_rows(a[f"L0_gnn_W_root{n}"])
        for r in range(REL):
            pieces += _by_rows(a[f"L0_gnn_W_rel{n}"][r])
        pieces += _by_columns(a["L0_gnn_Wg"][:, :D].T)
        hidden, query = _by_columns(a["L0_gnn_Wq"][:, :D].T), _by_columns(a["L0_gnn_Wq"][:, D:].T)
        pieces += [hidden[0], query[0], hidden[1], query[1]]
    units = []
    for e in range(8):
        for h in range(2):
            cut = slice(h * HALF, (h + 1) * HALF)
            units.append(_unit(a["L0_ffn_Wgu"][e][:, :D][:, cut], a["L0_ffn_Wgu"][e][:, D:][:, cut],
                               a["L0_ffn_Wd"][e][cut]))
    pieces += _in_order(units)
    pieces += _by_rows(a["L1_gnn_W1"].T, EDGE_LAYERS[0]["pieces"])
    pieces += _by_rows(a["L1_gnn_W2"].T, EDGE_LAYERS[1]["pieces"])
    pieces += _by_columns(a["L1_ffn_Wq"].T) + _by_columns(a["L1_ffn_Wk"].T)
    pieces += _by_rows(a["L1_ffn_Wv"].T) + _by_rows(a["L1_ffn_Wo"].T)
    units = []
    for e in range(8):
        units.append(_unit(a["L1_ffn_Weg"][e].T, a["L1_ffn_Weu"][e].T, a["L1_ffn_Wed"][e].T))
    for h in range(2):
        cut = slice(h * HALF, (h + 1) * HALF)
        units.append(_unit(a["L1_ffn_Wsg"][cut].T, a["L1_ffn_Wsu"][cut].T, a["L1_ffn_Wsd"].T[cut]))
    pieces += _in_order(units)
    for n in (1, 2):
        for r in range(REL):
            pieces += _by_rows(a[f"L2_gnn_W{n}"][r])
    units = [_unit(a["L2_ffn_wg"][e], a["L2_ffn_wu"][e], a["L2_ffn_wd"][e]) for e in range(16)]
    units += [_unit(a["L2_ffn_shared_wg"][e], a["L2_ffn_shared_wu"][e], a["L2_ffn_shared_wd"][e]) for e in range(2)]
    pieces += _in_order(units)
    pieces += _by_rows(a["L3_gnn_W"])
    for n in range(SLOTS):
        pieces += [a["L3_ffn_w1"][n].reshape(K, P, SLOT_HIDDEN).transpose(1, 0, 2).reshape(P, -1)]
    for n in range(SLOTS):
        pieces += _by_rows(a["L3_ffn_w2"][n], ((0, 3),))
    return pieces


def _small(a, np):
    def cols(v):
        return v.reshape(-1, P).T

    def tiled(m):
        return m.reshape(-1, P, m.shape[1]).transpose(1, 0, 2).reshape(P, -1)

    bgu = a["L0_ffn_bgu"].reshape(8, 2, 2, 3, P)
    att = np.zeros((8, P, 16), np.float32)
    for h in range(8):
        att[h, :, h] = a["L1_gnn_att_dst1"][h]
        att[h, :, 8 + h] = a["L1_gnn_att_src1"][h]
    parts = {
        "bg": cols(a["L0_gnn_bg"]), "bq": cols(a["L0_gnn_bq"]),
        "unit_bias": bgu.transpose(4, 0, 2, 1, 3).reshape(P, -1),
        "norm1": cols(a["L1_ffn_norm1_w"]), "norm2": cols(a["L1_ffn_norm2_w"]),
        "router0": tiled(a["L0_ffn_Wr"]), "router1": tiled(a["L1_ffn_gate_w"].T),
        "router2": tiled(a["L2_ffn_gate_w"].T),
        "br": np.broadcast_to(a["L0_ffn_br"], (P, 8)), "scale": np.broadcast_to(a["L3_ffn_scale"], (P, 1)),
        "att0": att.transpose(1, 0, 2).reshape(P, -1),
        "att1": tiled(np.stack([a["L1_gnn_att_dst2"][0], a["L1_gnn_att_src2"][0]], axis=1)),
        "att2": tiled(np.concatenate([a["L2_gnn_q1"], a["L2_gnn_k1"]], axis=1)),
        "att3": tiled(np.concatenate([a["L2_gnn_q2"], a["L2_gnn_k2"]], axis=1)),
    }
    assert all(parts[n].shape == (P, width) for n, (_, width) in SMALL.items())
    return np.concatenate([parts[n] for n in SMALL], axis=1)


def kernel(**inputs):
    import concourse.bacc as bacc
    import numpy as np
    from concourse.bass_utils import run_bass_kernel_spmd

    a = {name: np.asarray(value) for name, value in inputs.items()}
    pieces = _stream(a)
    assert len(pieces) == STREAM
    stream = np.zeros((STREAM, P, PIECE), np.float32)
    for n, piece in enumerate(pieces):
        stream[n, :, :piece.shape[1]] = piece
    edges = np.stack([a["src"], a["dst"], a["edge_type_3"]]).reshape(3, EDGE_TILES, P).transpose(2, 0, 1)
    query = a["L0_gnn_query_embs"].reshape(B * L, K, P).transpose(2, 1, 0)
    rows = [a[n] for n in ("L0_gnn_b1", "L0_gnn_b2", "L1_gnn_b1", "L1_gnn_b2", "L2_gnn_b1", "L2_gnn_b2", "L3_gnn_b")]
    arrays = {
        "x_in": a["x"], "edges": edges, "query": query, "small_in": _small(a, np),
        "bias_in": np.concatenate(rows)[None], "bd_in": a["L0_ffn_bd"],
        "phi_in": a["L3_ffn_phi"].reshape(K, P, SLOTS).transpose(1, 0, 2),
        "slot_b1_in": a["L3_ffn_b1"].reshape(SLOTS, 3, P).transpose(2, 1, 0),
        "slot_b2_in": np.concatenate([a["L3_ffn_b2"], np.zeros((SLOTS, D), np.float32)]), "stream": stream,
    }
    arrays = {name: np.ascontiguousarray(value) for name, value in arrays.items()}
    nc = bacc.Bacc("TRN2", target_bir_lowering=False, num_devices=1)
    tensors = [nc.dram_tensor(name, v.shape, mybir.dt.from_np(v.dtype), kind="ExternalInput").ap()
               for name, v in arrays.items()]
    out = nc.dram_tensor("out", (N, D), F32, kind="ExternalOutput").ap()
    build(nc, *tensors, out)
    result = run_bass_kernel_spmd(nc, [arrays], core_ids=[0])
    return result.results[0]["out"]
```
